# Optimizing a Trainium2 kernel written in Bass

```python
import numpy as np
import jax
import jax.numpy as jnp

def _softmax(x, axis=-1):
    return jax.nn.softmax(x, axis=axis)

def _gelu(x):
    return jax.nn.gelu(x, approximate=True)

def _silu(x):
    return jax.nn.silu(x)

def _sigmoid(x):
    return jax.nn.sigmoid(x)

def _layernorm(x, axis=-1, eps=1e-05):
    m = jnp.mean(x, axis=axis, keepdims=True)
    v = jnp.var(x, axis=axis, keepdims=True)
    return (x - m) / jnp.sqrt(v + eps)

def _scatter_add(tgt, idx, src, axis=0):
    return tgt.at[idx].add(src)

def _segment_sum(src, seg, n):
    return jax.ops.segment_sum(src, seg, n)
kernel_name = 'mk_gnn_resnorm_d4_gnn_r64_f66bf6'

def setup_inputs(seed: int=0):
    np.random.seed(seed)
    _w = jnp.asarray

    def _rec_inputs():
        import jax
        import jax.numpy as jnp
        _gk = jax.random.key(seed)
        x = 0.0007147 + 1 * jax.random.normal(jax.random.fold_in(_gk, 1), (100000, 64), jnp.float32)
        src = jax.random.randint(jax.random.fold_in(_gk, 2), (25000,), 0, 100000, jnp.int32)
        dst = jax.random.randint(jax.random.fold_in(_gk, 3), (25000,), 0, 100000, jnp.int32)
        _o = jnp.argsort(dst, stable=True)
        src = src[_o]
        dst = dst[_o]
        edge_attr_3 = 0.00117183 + 1.0004 * jax.random.normal(jax.random.fold_in(_gk, 12), (25000, 3), jnp.float32)
        return (x, src, dst, edge_attr_3)
    x, src, dst, edge_attr_3 = _rec_inputs()

    def _L0_gnn_setup():
        import jax, jax.numpy as jnp
        import numpy as np
        M = 50000
        E = 12500
        C_IN = 64
        C_OUT = 64
        DIM = 3
        RADIUS = 1.0
        EPS = 1e-05

        def layer_norm(x, g, b):
            mu = jnp.mean(x, axis=-1, keepdims=True)
            var = jnp.mean((x - mu) ** 2, axis=-1, keepdims=True)
            return (x - mu) * jax.lax.rsqrt(var + EPS) * g + b
        key = jax.random.key(seed)
        ks = jax.random.split(key, 12)
        inv = 1.0 / np.sqrt(C_OUT)
        return {'source': jax.random.randint(ks[0], (E,), 0, M), 'target': jax.random.randint(ks[1], (E,), 0, M), 'features': jax.random.normal(ks[2], (M, C_IN), dtype=jnp.float32), 'hood_coords': jax.random.normal(ks[3], (E, DIM), dtype=jnp.float32), 'Wd1': jax.random.normal(ks[4], (DIM, C_OUT), dtype=jnp.float32) / np.sqrt(DIM), 'bd1': jnp.zeros((C_OUT,), jnp.float32), 'g1': jnp.ones((C_OUT,), jnp.float32), 'b1': jnp.zeros((C_OUT,), jnp.float32), 'Wd2': jax.random.normal(ks[5], (C_OUT, C_OUT), dtype=jnp.float32) * inv, 'bd2': jnp.zeros((C_OUT,), jnp.float32), 'g2': jnp.ones((C_OUT,), jnp.float32), 'b2': jnp.zeros((C_OUT,), jnp.float32), 'W1': jax.random.normal(ks[6], (C_IN, C_OUT), dtype=jnp.float32) / np.sqrt(C_IN), 'W2': jax.random.normal(ks[7], (C_IN, C_OUT), dtype=jnp.float32) / np.sqrt(C_IN), 'W3': jax.random.normal(ks[8], (C_IN, C_OUT), dtype=jnp.float32) / np.sqrt(C_IN)}
    _L0_gnn_all = _L0_gnn_setup()
    _L0_gnn_in = {k: v for k, v in _L0_gnn_all.items() if k in ('Wd1', 'bd1', 'g1', 'b1', 'Wd2', 'bd2', 'g2', 'b2', 'W1', 'W2', 'W3')}
    del _L0_gnn_all

    def _L1_gnn_setup():
        import jax, jax.numpy as jnp
        import numpy as np
        N_NODES = 100000
        N_EDGES = 15625
        D = 64
        BN_EPS = 1e-05
        L2_EPS = 1e-12
        key = jax.random.key(seed)
        ks = jax.random.split(key, 7)
        scale = 1.0 / np.sqrt(D)
        x = jax.random.normal(ks[0], (N_NODES, D), dtype=jnp.float32)
        edge_index = jax.random.randint(ks[1], (2, N_EDGES), 0, N_NODES, dtype=jnp.int64)
        W_l = jax.random.normal(ks[2], (D, D), dtype=jnp.float32) * scale
        W_r = jax.random.normal(ks[3], (D, D), dtype=jnp.float32) * scale
        b = jnp.zeros((D,), dtype=jnp.float32)
        gamma = jnp.ones((D,), dtype=jnp.float32)
        beta = jnp.zeros((D,), dtype=jnp.float32)
        return {'x': x, 'W_l': W_l, 'W_r': W_r, 'b': b, 'gamma': gamma, 'beta': beta, 'edge_index': edge_index}
    _L1_gnn_all = _L1_gnn_setup()
    _L1_gnn_in = {k: v for k, v in _L1_gnn_all.items() if k in ('W_l', 'W_r', 'b', 'gamma', 'beta')}
    del _L1_gnn_all

    def _L2_gnn_setup():
        import jax, jax.numpy as jnp
        import numpy as np
        N_NODES = 100000
        N_EDGES = 25000
        INPUT_DIM = 64
        H_DIM = 1
        key = jax.random.key(seed)
        k_h, k_src, k_dst, k_w, k_b = jax.random.split(key, 5)
        h = jax.random.normal(k_h, (N_NODES, INPUT_DIM), dtype=jnp.float32)
        src = jax.random.randint(k_src, (N_EDGES,), 0, N_NODES, dtype=jnp.int32)
        dst = jax.random.randint(k_dst, (N_EDGES,), 0, N_NODES, dtype=jnp.int32)
        W = jax.random.normal(k_w, (H_DIM, 2 * INPUT_DIM), dtype=jnp.float32) * 0.1
        b = jax.random.normal(k_b, (H_DIM,), dtype=jnp.float32) * 0.1
        return {'h': h, 'src': src, 'dst': dst, 'W': W, 'b': b}
    _L2_gnn_all = _L2_gnn_setup()
    _L2_gnn_in = {k: v for k, v in _L2_gnn_all.items() if k in ('W', 'b')}
    del _L2_gnn_all

    def _L3_gnn_setup():
        import jax, jax.numpy as jnp
        import numpy as np
        N_NODES = 100000
        N_EDGES = 25000
        N_FEATS = 64
        HID1 = 128
        HID2 = 128

        def _gcn_conv(x, src, dst, norm, W, b, n_nodes):
            h = x @ W.T
            msg = h[src] * norm[:, None]
            out = jax.ops.segment_sum(msg, dst, num_segments=n_nodes)
            return out + b
        key = jax.random.key(seed)
        ks = jax.random.split(key, 8)
        x = jax.random.normal(ks[0], (N_NODES, N_FEATS), dtype=jnp.float32)
        edge_index = jax.random.randint(ks[1], (2, N_EDGES), 0, N_NODES, dtype=jnp.int64)
        W1 = jax.random.normal(ks[2], (HID1, N_FEATS), dtype=jnp.float32) * (1.0 / np.sqrt(N_FEATS))
        b1 = jnp.zeros((HID1,), dtype=jnp.float32)
        W2 = jax.random.normal(ks[3], (HID2, HID1), dtype=jnp.float32) * (1.0 / np.sqrt(HID1))
        b2 = jnp.zeros((HID2,), dtype=jnp.float32)
        W3 = jax.random.normal(ks[4], (N_FEATS, HID2), dtype=jnp.float32) * (1.0 / np.sqrt(HID2))
        b3 = jnp.zeros((N_FEATS,), dtype=jnp.float32)
        return {'x': x, 'edge_index': edge_index, 'W1': W1, 'b1': b1, 'W2': W2, 'b2': b2, 'W3': W3, 'b3': b3}
    _L3_gnn_all = _L3_gnn_setup()
    _L3_gnn_in = {k: v for k, v in _L3_gnn_all.items() if k in ('W1', 'b1', 'W2', 'b2', 'W3', 'b3')}
    del _L3_gnn_all
    return {'x': x, 'src': src, 'dst': dst, 'edge_attr_3': edge_attr_3, 'L0_gnn_Wd1': _L0_gnn_in['Wd1'], 'L0_gnn_bd1': _L0_gnn_in['bd1'], 'L0_gnn_g1': _L0_gnn_in['g1'], 'L0_gnn_b1': _L0_gnn_in['b1'], 'L0_gnn_Wd2': _L0_gnn_in['Wd2'], 'L0_gnn_bd2': _L0_gnn_in['bd2'], 'L0_gnn_g2': _L0_gnn_in['g2'], 'L0_gnn_b2': _L0_gnn_in['b2'], 'L0_gnn_W1': _L0_gnn_in['W1'], 'L0_gnn_W2': _L0_gnn_in['W2'], 'L0_gnn_W3': _L0_gnn_in['W3'], 'L1_gnn_W_l': _L1_gnn_in['W_l'], 'L1_gnn_W_r': _L1_gnn_in['W_r'], 'L1_gnn_b': _L1_gnn_in['b'], 'L1_gnn_gamma': _L1_gnn_in['gamma'], 'L1_gnn_beta': _L1_gnn_in['beta'], 'L2_gnn_W': _L2_gnn_in['W'], 'L2_gnn_b': _L2_gnn_in['b'], 'L3_gnn_W1': _L3_gnn_in['W1'], 'L3_gnn_b1': _L3_gnn_in['b1'], 'L3_gnn_W2': _L3_gnn_in['W2'], 'L3_gnn_b2': _L3_gnn_in['b2'], 'L3_gnn_W3': _L3_gnn_in['W3'], 'L3_gnn_b3': _L3_gnn_in['b3']}

def reference(x, src, dst, edge_attr_3, L0_gnn_Wd1, L0_gnn_bd1, L0_gnn_g1, L0_gnn_b1, L0_gnn_Wd2, L0_gnn_bd2, L0_gnn_g2, L0_gnn_b2, L0_gnn_W1, L0_gnn_W2, L0_gnn_W3, L1_gnn_W_l, L1_gnn_W_r, L1_gnn_b, L1_gnn_gamma, L1_gnn_beta, L2_gnn_W, L2_gnn_b, L3_gnn_W1, L3_gnn_b1, L3_gnn_W2, L3_gnn_b2, L3_gnn_W3, L3_gnn_b3):
    import jax
    import jax.numpy as jnp

    def _L0_gnn_ref(source, target, features, hood_coords, Wd1, bd1, g1, b1, Wd2, bd2, g2, b2, W1, W2, W3):
        import jax, jax.numpy as jnp
        import numpy as np
        M = 50000
        E = 12500
        C_IN = 64
        C_OUT = 64
        DIM = 3
        RADIUS = 1.0
        EPS = 1e-05

        def layer_norm(x, g, b):
            mu = jnp.mean(x, axis=-1, keepdims=True)
            var = jnp.mean((x - mu) ** 2, axis=-1, keepdims=True)
            return (x - mu) * jax.lax.rsqrt(var + EPS) * g + b
        m = features.shape[0]
        x = hood_coords / RADIUS
        d = jax.nn.gelu(layer_norm(x @ Wd1 + bd1, g1, b1), approximate=False)
        d = jax.nn.gelu(layer_norm(d @ Wd2 + bd2, g2, b2), approximate=False)
        w1 = features @ W1
        w2 = features @ W2
        w3 = features @ W3
        logits = w1[target] - w2[source] + d
        seg_max = jax.ops.segment_max(logits, target, num_segments=m)
        seg_max = jnp.where(jnp.isfinite(seg_max), seg_max, 0.0)
        e = jnp.exp(logits - seg_max[target])
        denom = jax.ops.segment_sum(e, target, num_segments=m)
        a = e / denom[target]
        out = jax.ops.segment_sum(a * (w3[source] + d), target, num_segments=m)
        return out

    def _L1_gnn_ref(x, W_l, W_r, b, gamma, beta, edge_index):
        import jax, jax.numpy as jnp
        import numpy as np
        N_NODES = 100000
        N_EDGES = 15625
        D = 64
        BN_EPS = 1e-05
        L2_EPS = 1e-12
        src, dst = (edge_index[0], edge_index[1])
        n = x.shape[0]
        msgs = x[src]
        summed = jax.ops.segment_sum(msgs, dst, num_segments=n)
        deg = jax.ops.segment_sum(jnp.ones_like(src, dtype=x.dtype), dst, num_segments=n)
        agg = summed / jnp.maximum(deg, 1.0)[:, None]
        h = agg @ W_l + x @ W_r + b
        mu = jnp.mean(h, axis=0)
        var = jnp.mean(jnp.square(h - mu), axis=0)
        h = (h - mu) * jax.lax.rsqrt(var + BN_EPS) * gamma + beta
        h = jax.nn.relu(h)
        norm = jnp.maximum(jnp.sqrt(jnp.sum(jnp.square(h), axis=-1, keepdims=True)), L2_EPS)
        return h / norm

    def _L2_gnn_ref(h, src, dst, W, b):
        import jax, jax.numpy as jnp
        import numpy as np
        N_NODES = 100000
        N_EDGES = 25000
        INPUT_DIM = 64
        H_DIM = 1
        n = h.shape[0]
        x = jnp.concatenate([h[src], h[dst]], axis=-1)
        e = jax.nn.leaky_relu(x @ W.T + b)
        e_max = jax.ops.segment_max(e, dst, num_segments=n)
        e_exp = jnp.exp(e - e_max[dst])
        e_sum = jax.ops.segment_sum(e_exp, dst, num_segments=n)
        alpha = e_exp / e_sum[dst]
        out = jax.ops.segment_sum(h[src] * alpha, dst, num_segments=n)
        return out

    def _L3_gnn_ref(x, edge_index, W1, b1, W2, b2, W3, b3):
        import jax, jax.numpy as jnp
        import numpy as np
        N_NODES = 100000
        N_EDGES = 25000
        N_FEATS = 64
        HID1 = 128
        HID2 = 128

        def _gcn_conv(x, src, dst, norm, W, b, n_nodes):
            h = x @ W.T
            msg = h[src] * norm[:, None]
            out = jax.ops.segment_sum(msg, dst, num_segments=n_nodes)
            return out + b
        n = x.shape[0]
        loop = jnp.arange(n, dtype=edge_index.dtype)
        src = jnp.concatenate([edge_index[0], loop])
        dst = jnp.concatenate([edge_index[1], loop])
        deg = jax.ops.segment_sum(jnp.ones(dst.shape, dtype=x.dtype), dst, num_segments=n)
        dinv = jnp.where(deg > 0, jax.lax.rsqrt(deg), 0.0)
        norm = dinv[src] * dinv[dst]
        h = jax.nn.relu(_gcn_conv(x, src, dst, norm, W1, b1, n))
        h = jax.nn.relu(_gcn_conv(h, src, dst, norm, W2, b2, n))
        h = _gcn_conv(h, src, dst, norm, W3, b3, n)
        return jax.nn.softmax(h, axis=1)
    edge_index = jnp.stack([src, dst])
    x = _layernorm(x + _L0_gnn_ref(src, dst, x, edge_attr_3, L0_gnn_Wd1, L0_gnn_bd1, L0_gnn_g1, L0_gnn_b1, L0_gnn_Wd2, L0_gnn_bd2, L0_gnn_g2, L0_gnn_b2, L0_gnn_W1, L0_gnn_W2, L0_gnn_W3), axis=-1)
    x = _layernorm(x + _L1_gnn_ref(x, L1_gnn_W_l, L1_gnn_W_r, L1_gnn_b, L1_gnn_gamma, L1_gnn_beta, edge_index), axis=-1)
    x = _layernorm(x + _L2_gnn_ref(x, src, dst, L2_gnn_W, L2_gnn_b), axis=-1)
    x = _layernorm(x + _L3_gnn_ref(x, edge_index, L3_gnn_W1, L3_gnn_b1, L3_gnn_W2, L3_gnn_b2, L3_gnn_W3, L3_gnn_b3), axis=-1)
    return x

_drawn_inputs = setup_inputs


def setup_inputs(seed=0):
    import zlib

    import numpy as np

    out = dict(_drawn_inputs(seed))
    spreads = {'L0_gnn_bd1': (0.0, 0.1),
     'L0_gnn_g1': (1.0, 0.2),
     'L0_gnn_b1': (0.0, 0.447),
     'L0_gnn_bd2': (0.0, 0.296),
     'L0_gnn_g2': (1.0, 0.2),
     'L0_gnn_b2': (0.0, 0.458),
     'L1_gnn_b': (0.0, 2.0),
     'L1_gnn_gamma': (1.0, 0.592),
     'L1_gnn_beta': (0.0, 0.54),
     'L3_gnn_b1': (0.0, 0.8),
     'L3_gnn_b2': (0.0, 2.0),
     'L3_gnn_b3': (0.0, 2.0)}
    factors = {'L0_gnn_W1': 64.0, 'L3_gnn_W1': 8.0, 'L3_gnn_W2': 8.0, 'L3_gnn_W3': 6.828}
    for name, (base, spread) in spreads.items():
        noise = np.random.default_rng([zlib.crc32(name.encode()), seed]).standard_normal(out[name].shape)
        drawn = base * np.exp(spread * noise) if base else spread * noise
        out[name] = jnp.asarray(drawn.astype(out[name].dtype))
    for name, factor in factors.items():
        out[name] = (out[name] * factor).astype(out[name].dtype)
    return out
```

```python
import math

import concourse.bass as bass
from concourse import mybir
from contextlib import ExitStack

F32 = mybir.dt.float32
I32 = mybir.dt.int32
BF16 = mybir.dt.bfloat16
ALU = mybir.AluOpType
ACT = mybir.ActivationFunctionType
AX = mybir.AxisListType.X

N = 100000
E = 25000
C = 64
H = 128
P = 128
CT = 4
CE = CT * P
ITERS = -(-E // (2 * CE))
EP = ITERS * 2 * CE
NT = EP // P
ST = 10
NODE_ROWS = 8
DN = P * NODE_ROWS
D_FULL = N // DN
D_REST = (N - D_FULL * DN) // NODE_ROWS
D_ITERS = D_FULL // 2
NONE = 1 << 20
EPS = 1e-5
BIG = 1e30
LN_EXP = "natural_log_exp_and_others"


class Plan:

    def __init__(self, nc, ctx):
        self.nc, self.ctx = nc, ctx

    def sb(self, name, shape, dt=F32):
        return self.ctx.enter_context(self.nc.sbuf_tensor(name, shape, dt))

    def dram(self, name, shape, dt=F32):
        return self.nc.dram_tensor(name, shape, dt, kind="Internal").ap()


class Stage:

    def __init__(self, nc, name):
        self.nc, self.name, self.sems = nc, name, []
        self.ctx = ExitStack()

    def __enter__(self):
        self.ctx.__enter__()
        return self

    def sb(self, name, shape, dt=F32):
        return self.ctx.enter_context(self.nc.sbuf_tensor(f"{self.name}_{name}", shape, dt))

    def ps(self, name, shape, dt=F32):
        return self.ctx.enter_context(self.nc.psum_tensor(f"{self.name}_{name}", shape, dt))

    def sem(self, name):
        s = self.nc.alloc_semaphore(f"{self.name}_{name}")
        self.sems.append(s)
        return s

    def pair(self, name):
        return [self.sem(f"{name}0"), self.sem(f"{name}1")]

    def __exit__(self, *a):
        self.ctx.__exit__(*a)
        if a[0] is None:
            self.nc.clear_and_free_semaphores(self.sems)
            self.nc.all_engine_barrier()
        return False


def groups(ap, n):
    return ap.rearrange("p (n f) -> p n f", n=n)


def over(ap, f):
    return ap.unsqueeze(2).to_broadcast([ap.shape[0], ap.shape[1], f])


def row(ap, n):
    return ap.rearrange("(a n) -> a n", a=1)


def build(nc, a, out):
    ctx = ExitStack()
    with ctx:
        k = Plan(nc, ctx)
        k.ident = k.sb("ident", [P, P])
        k.ones = k.sb("ones", [P, H])
        k.same = k.sb("same", [P, EP], BF16)
        k.last = k.sb("last", [P, NT])
        k.src = k.sb("src", [P, NT], I32)
        k.dst = k.sb("dst", [P, NT], I32)
        k.put = k.sb("put", [P, NT], I32)
        k.pos = k.sb("pos", [P, NT], I32)
        k.lastq = k.sb("lastq", [NT // 2, 2 * P])
        k.dinv = k.sb("dinv", [P, NT])
        k.eps = k.sb("eps", [P, 4])
        k.w_logit = k.sb("w_logit", [P, P])
        k.w_value = k.sb("w_value", [P, P])
        k.wd1 = k.sb("wd1", [4, C])
        k.wd2 = k.sb("wd2", [P, P])
        k.bd2 = k.sb("bd2", [1, CT, C])
        k.col = k.sb("col", [P, 8])
        k.wcat = k.sb("wcat", [P, C])
        k.wbn = k.sb("wbn", [P, C])
        k.wbn_r = k.sb("wbn_r", [P, P])
        k.bnrow = k.sb("bnrow", [1, 3, C])
        k.shift = k.sb("shift", [1, NODE_ROWS, C])
        k.w_att_s = k.sb("w_att_s", [P, P])
        k.w_att_d = k.sb("w_att_d", [P, C])
        k.b_att = k.sb("b_att", [P, 1])
        k.w1 = k.sb("w1", [P, H])
        k.w2 = k.sb("w2", [P, H])
        k.w3 = k.sb("w3", [P, C])
        k.b1row = k.sb("b1row", [P, H])
        k.b3row = k.sb("b3row", [1, NODE_ROWS, C])
        k.b3 = k.sb("b3", [P, C])
        k.gram = k.sb("gram", [P, P + 1])
        k.where = k.dram("where", (N, 1), I32)
        k.mlp = k.dram("mlp", (C, EP))
        k.x1 = k.dram("x1", (N, C))
        k.s1 = k.dram("s1", (EP, C)); k.d1 = k.dram("d1", (EP, C))
        k.agg = k.dram("agg", (EP, C))
        k.s2 = k.dram("s2", (EP, C)); k.d2 = k.dram("d2", (EP, C))
        k.att_d = k.dram("att_d", (EP,))
        k.dinv_row = k.dram("dinv_row", (EP,))
        k.s3 = k.dram("s3", (EP, C)); k.d3 = k.dram("d3", (EP, C)); k.x3 = k.dram("x3", (EP, C))
        k.s4 = k.dram("s4", (EP, H)); k.d4 = k.dram("d4", (EP, H))
        k.s5 = k.dram("s5", (EP, C)); k.d5 = k.dram("d5", (EP, C))

        index_stage(nc, k, a)
        mlp_and_gram_stage(nc, k, a)
        attention_stage(nc, k, a)
        mean_stage(nc, k)
        batch_norm_stage(nc, k)
        update_stage(nc, k)
        dense_stage(nc, k, out)
        attention2_stage(nc, k)
        gcn1_stage(nc, k)
        gcn2_stage(nc, k)
        output_stage(nc, k, out)


def by_chunk(ap):
    return ap.rearrange("(i t p) f -> i p t f", t=CT, p=P)


def one(ap, i):
    v = ap[bass.ds(i, 1)]
    return v.rearrange("a p t f -> (a p) t f")


def index_stage(nc, k, a):
    Q = NT // 2
    with Stage(nc, "ix") as g:
        ends = g.sb("ends", [Q, 3, 2 * P], I32)
        endf = g.sb("endf", [Q, 4, 2 * P])
        none = g.sb("none", [80, N // 80], I32)
        wcol = g.sb("wcol", [P, 1])
        win = [g.sb(f"win{b}", [P, CE + 1], I32) for b in range(2)]
        pT = [g.ps(f"pT{h}", [P, 2, 2, Q]) for h in range(2)]
        loaded = g.sem("loaded"); ends_in = g.sem("ends_in"); none_in = g.sem("none_in")
        consts = g.sem("consts"); wsteps = g.sem("wsteps"); esteps = g.sem("esteps"); turned = g.sem("turned")
        tables = g.sem("tables"); win_in = g.pair("win_in"); win_used = g.pair("win_used")
        filled = g.sem("filled"); zeros = g.sem("zeros")
        dstp = a["dstp"]
        with nc.Block() as block:
            n_loads = []

            @block.sync
            def _(sp):
                def load(dst, src):
                    sp.dma_start(dst, src).then_inc(loaded, 16)
                    n_loads.append(1)
                for n, v in enumerate((dstp[1:EP + 1], dstp[2:EP + 2], a["srcp"])):
                    sp.dma_start(ends[:, n, :], v.rearrange("(q e) -> q e", e=2 * P)).then_inc(ends_in, 16)
                sp.wait_ge(zeros, 1)
                for h in range(2):
                    rows = slice(C * h, C * h + C)
                    load(k.w_logit[0:C, rows], a["L0_gnn_W2"])
                    load(k.w_logit[C:P, rows], a["L0_gnn_W1"])
                    for n, name in enumerate(("g1", "b1", "g2", "b2")):
                        load(k.col[rows, n:n + 1], a["L0_gnn_" + name].rearrange("(n a) -> n a", a=1))
                    load(k.w1[rows, :], a["W1T"])
                    load(k.wd2[rows, rows], a["L0_gnn_Wd2"])
                load(k.w_value[0:C, C:P], a["L0_gnn_W3"])
                load(k.wd1[0:3, :], a["L0_gnn_Wd1"])
                load(k.wd1[3:4, :], row(a["L0_gnn_bd1"], C))
                for n in range(CT):
                    load(k.bd2[:, n, :], row(a["L0_gnn_bd2"], C))
                load(k.wcat[0:C, :], a["L1_gnn_W_r"])
                load(k.wcat[C:P, :], a["L1_gnn_W_l"])
                for n, name in enumerate(("b", "gamma", "beta")):
                    load(k.bnrow[:, n, :], row(a["L1_gnn_" + name], C))
                load(wcol[C:P, :], a["L2_gnn_W"][:, 0:C].rearrange("a n -> n a"))
                load(k.w_att_d[:, :], a["L2_gnn_W"][:, C:P].to_broadcast([P, C]))
                load(k.b_att[:, :], row(a["L2_gnn_b"], 1).to_broadcast([P, 1]))
                load(k.col[:, 4:5], a["L3_gnn_b1"].rearrange("(n a) -> n a", a=1))
                load(k.col[:, 5:6], a["L3_gnn_b2"].rearrange("(n a) -> n a", a=1))
                load(k.w2[:, :], a["W2T"])
                load(k.w3[:, :], a["W3T"])
                load(k.b1row[:, :], row(a["L3_gnn_b1"], H).to_broadcast([P, H]))
                for r in range(NODE_ROWS):
                    load(k.b3row[:, r, :], row(a["L3_gnn_b3"], C))
                load(k.b3[:, :], row(a["L3_gnn_b3"], C).to_broadcast([P, C]))
                sp.wait_ge(none_in, 1)
                sp.dma_start(k.where.rearrange("(q n) a -> q (n a)", q=80), none[:, :]).then_inc(filled, 16)
                with sp.Fori(0, ITERS) as j:
                    for b in range(2):
                        sp.wait_ge(win_used[b], j)
                        sp.dma_start(win[b][:, :], row(dstp[bass.ds((2 * j + b) * CE, CE + 1)], CE + 1)
                                     .to_broadcast([P, CE + 1])).then_inc(win_in[b], 16)
                sp.wait_ge(loaded, 16 * len(n_loads))
                sp.wait_ge(filled, 16)

            @block.gpsimd
            def _(pool):
                gp = nc.gpsimd
                gp.memset(none[:, :], NONE).then_inc(none_in, 1)
                gp.memset(k.wd2[:, :], 0.0).then_inc(zeros, 1)
                gp.memset(k.ident[:, :], 0.0)
                gp.memset(k.w_value[:, 0:C], 0.0)
                gp.memset(k.ones[:, :], 1.0)
                gp.memset(k.eps[:, 0:1], EPS)
                gp.memset(k.eps[:, 1:2], EPS * EPS)
                gp.memset(k.eps[:, 2:3], 10 * math.log(2.0))
                gp.memset(k.eps[:, 3:4], 1.0).then_inc(consts, 1)
                pool.wait_ge(consts, 1)
                gp.affine_select(out=k.ident[:, :], in_=k.ident[:, :], compare_op=ALU.not_equal, fill=1.0,
                                 base=0, pattern=[[-1, P]], channel_multiplier=1).then_inc(consts, 1)

            @block.tensor
            def _(pe):
                pe.wait_ge(consts, 2)
                pe.wait_ge(esteps, 5)
                for n in range(4):
                    for h in range(2):
                        i = nc.tensor.transpose(pT[n // 2][:, n % 2, h, :], endf[:, n, P * h:P * h + P],
                                                k.ident[0:Q, 0:Q])
                i.then_inc(turned, 1)

            @block.vector
            def _(dve):
                v = nc.vector
                dve.wait_ge(ends_in, 48)
                v.tensor_tensor(k.lastq[:, :], ends[:, 0, :], ends[:, 1, :], ALU.not_equal).then_inc(esteps, 1)
                v.tensor_copy(endf[:, 0, :], ends[:, 0, :]).then_inc(esteps, 1)
                v.tensor_copy(endf[:, 2, :], ends[:, 2, :]).then_inc(esteps, 1)
                dve.wait_ge(esteps, 1)
                v.tensor_copy(endf[:, 3, :], k.lastq[:, :])
                v.tensor_scalar(endf[:, 1, :], k.lastq[:, :], -float(NONE), float(NONE), ALU.mult,
                                ALU.add).then_inc(esteps, 1)
                dve.wait_ge(esteps, 4)
                v.tensor_tensor(endf[:, 1, :], endf[:, 1, :], endf[:, 0, :], ALU.add).then_inc(esteps, 1)
                dve.wait_ge(turned, 1)
                for n, dst in enumerate((k.dst, k.put, k.src, k.last)):
                    v.tensor_copy(dst[:, :].rearrange("p (q h) -> p h q", h=2), pT[n // 2][:, n % 2, :, :])\
                        .then_inc(tables, 1)
                with dve.Fori(0, ITERS) as j:
                    for b in range(2):
                        dve.wait_ge(win_in[b], 16 * j + 16)
                        v.tensor_tensor(k.same[:, bass.ds((2 * j + b) * CE, CE)], win[b][:, 1:CE + 1],
                                        win[b][:, 0:CE], ALU.is_equal).then_inc(win_used[b], 1)
                dve.wait_ge(loaded, 16 * len(n_loads))
                dve.wait_ge(consts, 2)
                v.tensor_scalar(k.w_logit[0:C, :], k.w_logit[0:C, :], -1.0, None, ALU.mult)
                v.memset(k.w_value[C:P, C:P], 0.0)
                v.memset(k.w_att_s[0:C, :], 0.0)
                v.tensor_scalar(k.w_att_s[C:P, :], k.ones[C:P, :], wcol[C:P, 0:1], None, ALU.mult)


def last_of(j, b):
    return 2 * j + (b + 1)


def mlp_and_gram_stage(nc, k, a):
    with Stage(nc, "mg") as g:
        edge = g.sb("edge", [P, NT], I32)
        stage_i = [g.sb(f"stage_i{b}", [P, ST], I32) for b in range(2)]
        stage_v = [g.sb(f"stage_v{b}", [P, ST], I32) for b in range(2)]
        attr = [g.sb(f"attr{b}", [4, CE]) for b in range(2)]
        z = g.sb("z", [P, NT * C], F32)
        zn = [g.sb(f"zn{b}", [P, CT * C]) for b in range(2)]
        zq = [g.sb(f"zq{b}", [P, CT * C]) for b in range(2)]
        zs = [g.sb(f"zs{b}", [P, CT]) for b in range(2)]
        q = g.sb("q", [P, NT])
        act = [g.sb(f"act{b}", [P, CE // 2]) for b in range(2)]
        pz = [g.ps(f"pz{b}", [P, CT * C]) for b in range(2)]
        pt = [g.ps(f"pt{b}", [P, CE // 2]) for b in range(2)]
        pos_sems = g.pair("put_done"), g.pair("got"), g.sem("staged"), g.sem("passed"), g.sem("copied")
        ones_in = g.sem("ones_in"); passed_dve = g.sem("passed_dve")
        attr_in = g.pair("attr_in"); mlp_out = g.pair("mlp_out")
        e = {}
        for layer in (1, 2):
            for n in ("prod", "sum", "cen", "sq", "sumsq", "scaled", "turned", "gelu"):
                e[n, layer] = g.sem(f"{n}{layer}")
        var_ln = g.sem("var_ln"); dev = g.sem("dev")
        X = [g.sb(f"x{b}", [P, NODE_ROWS * C]) for b in range(2)]
        Y = [g.sb(f"y{b}", [P, NODE_ROWS * C]) for b in range(2)]
        Q = [g.sb(f"sq{b}", [P, NODE_ROWS * C]) for b in range(2)]
        st = [g.sb(f"st{b}", [P, 3, NODE_ROWS]) for b in range(2)]
        pG = g.ps("pG", [C, C + 1])
        x_in = g.pair("x_in"); x1_out = g.pair("x1_out")
        d = {n: g.sem("d_" + n) for n in ("sum", "cen", "sq", "sumsq", "ln", "dev", "norm", "gram")}
        trips = D_FULL // 2
        assert D_FULL % 2 == 1
        with nc.Block() as block:

            @block.gpsimd
            def _(pool):
                put_done, got, staged, passed, copied = pos_sems
                gp = nc.gpsimd
                for b in range(2):
                    gp.memset(attr[b][:, :], 1.0).then_inc(ones_in, 1)
                pool.wait_ge(ones_in, 2)
                gp.iota(edge[:, :], pattern=[[P, NT]], base=0, channel_multiplier=1).then_inc(copied, 1)
                pool.wait_ge(copied, 1)
                bound = pool.to_reg(N - 1)
                with pool.Fori(0, NT // (2 * ST)) as j:
                    for b in range(2):
                        at = bass.ds((2 * j + b) * ST, ST)
                        pool.wait_ge(put_done[b], 16 * ST * j)
                        gp.tensor_copy(stage_i[b][:, :], k.put[:, at])
                        gp.tensor_copy(stage_v[b][:, :], edge[:, at]).then_inc(staged, 1)
                        pool.wait_ge(staged, last_of(j, b))
                        pool.sem_inc(passed, 1)
                        for t in range(ST):
                            gp.indirect_dma_start(
                                out=k.where, out_offset=bass.IndirectOffsetOnAxis(ap=stage_i[b][:, t:t + 1], axis=0),
                                in_=stage_v[b][:, t:t + 1], in_offset=None, bounds_check=bound,
                                oob_is_err=False).then_inc(put_done[b], 16)
                for b in range(2):
                    pool.wait_ge(put_done[b], 16 * NT // 2)
                with pool.Fori(0, NT // (2 * ST)) as j:
                    for b in range(2):
                        at = bass.ds((2 * j + b) * ST, ST)
                        gp.tensor_copy(stage_i[b][:, :], k.src[:, at]).then_inc(staged, 1)
                        pool.wait_ge(staged, 2 * j + (NT // ST + b + 1))
                        pool.wait_ge(copied, 2 * j + 1)
                        pool.sem_inc(passed, 1)
                        for t in range(ST):
                            gp.indirect_dma_start(
                                out=stage_v[b][:, t:t + 1], out_offset=None, in_=k.where,
                                in_offset=bass.IndirectOffsetOnAxis(ap=stage_i[b][:, t:t + 1], axis=0),
                                bounds_check=bound, oob_is_err=False).then_inc(got[b], 16)
                    for b in range(2):
                        pool.wait_ge(got[b], 16 * ST * j + 16 * ST)
                        gp.tensor_copy(k.pos[:, bass.ds((2 * j + b) * ST, ST)], stage_v[b][:, :])\
                            .then_inc(copied, 1)

            @block.sync
            def _(sp):
                sp.wait_ge(ones_in, 2)
                with sp.Fori(0, ITERS) as j:
                    for b in range(2):
                        sp.wait_ge(e["prod", 1], 2 * j)
                        sp.dma_start(attr[b][0:3, :], a["attrT"][:, bass.ds((2 * j + b) * CE, CE)])\
                            .then_inc(attr_in[b], 16)
                with sp.Fori(0, ITERS) as j:
                    for b in range(2):
                        sp.wait_ge(e["gelu", 2], last_of(j, b))
                        rows = k.mlp[:, bass.ds((2 * j + b) * CE, CE)].rearrange("c (n h e) -> c n h e", h=2, e=P)
                        for h in range(2):
                            sp.dma_start(rows[:, :, h, :], groups(act[b][C * h:C * h + C, :], CT // 2))\
                                .then_inc(mlp_out[b], 16)

                def load(j, b, parts, used=True):
                    if used:
                        sp.wait_ge(d["cen"], last_of(j - 1, b))
                    sp.dma_start(X[b][0:parts, :], node_rows(a["x"], 2 * j + b, parts)).then_inc(x_in[b], 16)

                def store(j, b, parts):
                    sp.wait_ge(d["norm"], last_of(j, b))
                    sp.dma_start(node_rows(k.x1, 2 * j + b, parts), Y[b][0:parts, :]).then_inc(x1_out[b], 16)

                load(0, 0, P, used=False)
                load(0, 1, P, used=False)
                with sp.Fori(0, trips - 1) as j:
                    for b in range(2):
                        load(j + 1, b, P)
                    for b in range(2):
                        store(j, b, P)
                for b in range(2):
                    load(trips, b, (P, D_REST)[b])
                for b in range(2):
                    store(trips - 1, b, P)
                for b in range(2):
                    store(trips, b, (P, D_REST)[b])
                for b in range(2):
                    sp.wait_ge(mlp_out[b], 32 * ITERS)
                    sp.wait_ge(x1_out[b], 16 * (trips + 1))

            @block.tensor
            def _(pe):
                t = nc.tensor

                def first_layer(j, b):
                    pe.wait_ge(e["cen", 1], 2 * j)
                    for n in range(CT):
                        i = t.matmul(pz[b][:, n * C:n * C + C], attr[b][:, n * P:n * P + P], k.wd1[:, :],
                                     start=True, stop=True)
                    i.then_inc(e["prod", 1], 1)

                def second_layer(j, b):
                    pe.wait_ge(e["cen", 2], 2 * j)
                    t.matmul(pz[b][:, :], k.ones[0:1, :], k.bd2[:, :, :].rearrange("a n c -> a (n c)"),
                             start=True, stop=False, skip_group_check=True)
                    for n in range(CT // 2):
                        i = t.matmul(pz[b][:, n * P:n * P + P], act[b][:, n * P:n * P + P], k.wd2[:, :],
                                     start=False, stop=n == CT // 2 - 1, skip_group_check=True)
                    i.then_inc(e["prod", 2], 1)

                def turn(j, b, layer):
                    pe.wait_ge(e["scaled", layer], last_of(j, b))
                    pe.wait_ge(e["gelu", layer], 2 * j)
                    for n in range(CT // 2):
                        i = t.transpose(pt[b][:, n * P:n * P + P], zn[b][:, n * P:n * P + P], k.ident[:, :])
                    i.then_inc(e["turned", layer], 1)

                with pe.Fori(0, ITERS) as j:
                    for b in range(2):
                        pe.wait_ge(attr_in[b], 16 * j + 16)
                        first_layer(j, b)
                with pe.Fori(0, ITERS) as j:
                    for b in range(2):
                        turn(j, b, 1)
                    for b in range(2):
                        pe.wait_ge(e["gelu", 1], last_of(j, b))
                        second_layer(j, b)
                with pe.Fori(0, ITERS) as j:
                    for b in range(2):
                        turn(j, b, 2)

                def gram(j, b, parts, first=False, last=False):
                    pe.wait_ge(d["norm"], last_of(j, b))
                    for n in range(NODE_ROWS):
                        rows = Y[b][0:parts, n * C:n * C + C]
                        end = last and n == NODE_ROWS - 1
                        t.matmul(pG[:, 0:C], rows, rows, start=False, stop=end, skip_group_check=True)
                        i = t.matmul(pG[:, C:C + 1], rows, k.ones[0:parts, 0:1], start=False, stop=end,
                                     skip_group_check=True)
                    i.then_inc(d["gram"], 1)

                zero = k.w_value[:, 0:C]
                t.matmul(pG[:, 0:C], zero, zero, start=True, stop=False, skip_group_check=True)
                t.matmul(pG[:, C:C + 1], zero, k.ones[:, 0:1], start=False, stop=False, skip_group_check=True)
                with pe.Fori(0, trips) as j:
                    for b in range(2):
                        gram(j, b, P)
                gram(trips, 0, P)
                gram(trips, 1, D_REST, last=True)

            @block.scalar
            def _(act_):
                s = nc.scalar

                def square_edges(j, b, layer):
                    act_.wait_ge(e["cen", layer], last_of(j, b))
                    act_.wait_ge(e["sumsq", layer], 2 * j)
                    s.activation(zq[b][:, :], z[:, bass.ds((2 * j + b) * CT * C, CT * C)], ACT.Square)\
                        .then_inc(e["sq", layer], 1)

                def deviations(layer):
                    act_.wait_ge(e["sumsq", layer], 2 * ITERS)
                    s.activation(q[:, :], q[:, :], ACT.Ln, scale=1.0 / C, bias=k.eps[:, 0:1]).then_inc(var_ln, 1)
                    act_.wait_ge(var_ln, layer)
                    s.activation(q[:, :], q[:, :], ACT.Exp, scale=-0.5).then_inc(dev, 1)

                def gelu(j, b, layer):
                    act_.wait_ge(e["turned", layer], last_of(j, b))
                    if layer == 1:
                        act_.wait_ge(e["prod", 2], 2 * j)
                    else:
                        act_.wait_ge(mlp_out[b], 32 * j)
                    s.activation(act[b][:, :], pt[b][:, :], ACT.Gelu, scale=k.col[:, 2 * layer - 2:2 * layer - 1],
                                 bias=k.col[:, 2 * layer - 1:2 * layer]).then_inc(e["gelu", layer], 1)

                s.preload_act_table_set(LN_EXP)
                with act_.Fori(0, ITERS) as j:
                    for b in range(2):
                        square_edges(j, b, 1)
                deviations(1)
                with act_.Fori(0, ITERS) as j:
                    for b in range(2):
                        gelu(j, b, 1)
                    for b in range(2):
                        square_edges(j, b, 2)
                deviations(2)
                with act_.Fori(0, ITERS) as j:
                    for b in range(2):
                        gelu(j, b, 2)
                s.preload_act_table_set(LN_EXP)

                def norm(j, sizes):
                    for b in range(2):
                        act_.wait_ge(d["cen"], last_of(j, b))
                        act_.wait_ge(d["sumsq"], 2 * j)
                        s.activation(Q[b][0:sizes[b], :], Y[b][0:sizes[b], :], ACT.Square).then_inc(d["sq"], 1)
                    for b in range(2):
                        act_.wait_ge(d["sumsq"], last_of(j, b))
                        s.activation(st[b][0:sizes[b], 1, :], st[b][0:sizes[b], 1, :], ACT.Ln, scale=1.0 / C,
                                     bias=k.eps[0:sizes[b], 0:1]).then_inc(d["ln"], 1)
                    for b in range(2):
                        act_.wait_ge(d["ln"], last_of(j, b))
                        s.activation(st[b][0:sizes[b], 2, :], st[b][0:sizes[b], 1, :], ACT.Exp,
                                     scale=-0.5).then_inc(d["dev"], 1)
                with act_.Fori(0, trips) as j:
                    norm(j, (P, P))
                norm(trips, (P, D_REST))

            @block.vector
            def _(dve):
                v = nc.vector

                def center_edges(j, layer):
                    for b in range(2):
                        dve.wait_ge(e["prod", layer], last_of(j, b))
                        v.tensor_reduce(out=zs[b][:, :], in_=groups(pz[b][:, :], CT), op=ALU.add, axis=AX)\
                            .then_inc(e["sum", layer], 1)
                    for b in range(2):
                        dve.wait_ge(e["sum", layer], last_of(j, b))
                        v.scalar_tensor_tensor(groups(z[:, bass.ds((2 * j + b) * CT * C, CT * C)], CT),
                                               over(zs[b][:, :], C), -1.0 / C, groups(pz[b][:, :], CT),
                                               ALU.mult, ALU.add).then_inc(e["cen", layer], 1)

                def sum_edges(j, layer):
                    for b in range(2):
                        dve.wait_ge(e["sq", layer], last_of(j, b))
                        dve.sem_inc(passed_dve, 1)
                        v.tensor_reduce(out=q[:, bass.ds((2 * j + b) * CT, CT)], in_=groups(zq[b][:, :], CT),
                                        op=ALU.add, axis=AX).then_inc(e["sumsq", layer], 1)

                def scale_edges(j, layer):
                    for b in range(2):
                        dve.wait_ge(e["turned", layer], 2 * j)
                        v.tensor_tensor(groups(zn[b][:, :], CT), groups(z[:, bass.ds((2 * j + b) * CT * C, CT * C)], CT),
                                        over(q[:, bass.ds((2 * j + b) * CT, CT)], C), ALU.mult)\
                            .then_inc(e["scaled", layer], 1)

                with dve.Fori(0, ITERS) as j:
                    center_edges(j, 1)
                    sum_edges(j, 1)
                dve.wait_ge(dev, 1)
                with dve.Fori(0, ITERS) as j:
                    scale_edges(j, 1)
                    center_edges(j, 2)
                    sum_edges(j, 2)
                dve.wait_ge(dev, 2)
                with dve.Fori(0, ITERS) as j:
                    scale_edges(j, 2)

                def norm(j, sizes):
                    for b in range(2):
                        dve.wait_ge(x_in[b], 16 * j + 16)
                        v.tensor_reduce(out=st[b][0:sizes[b], 0, :], in_=groups(X[b][0:sizes[b], :], NODE_ROWS),
                                        op=ALU.add, axis=AX).then_inc(d["sum"], 1)
                    for b in range(2):
                        dve.wait_ge(d["sum"], last_of(j, b))
                        dve.wait_ge(d["gram"], 2 * j)
                        dve.wait_ge(x1_out[b], 16 * j)
                        v.scalar_tensor_tensor(groups(Y[b][0:sizes[b], :], NODE_ROWS), over(st[b][0:sizes[b], 0, :], C),
                                               -1.0 / C, groups(X[b][0:sizes[b], :], NODE_ROWS), ALU.mult, ALU.add)\
                            .then_inc(d["cen"], 1)
                    for b in range(2):
                        dve.wait_ge(d["sq"], last_of(j, b))
                        dve.wait_ge(d["dev"], 2 * j)
                        v.tensor_reduce(out=st[b][0:sizes[b], 1, :], in_=groups(Q[b][0:sizes[b], :], NODE_ROWS),
                                        op=ALU.add, axis=AX).then_inc(d["sumsq"], 1)
                    for b in range(2):
                        dve.wait_ge(d["dev"], last_of(j, b))
                        v.tensor_tensor(groups(Y[b][0:sizes[b], :], NODE_ROWS), groups(Y[b][0:sizes[b], :], NODE_ROWS),
                                        over(st[b][0:sizes[b], 2, :], C), ALU.mult).then_inc(d["norm"], 1)
                with dve.Fori(0, trips) as j:
                    norm(j, (P, P))
                norm(trips, (P, D_REST))
                dve.wait_ge(d["gram"], 2 * (trips + 1))
                v.memset(k.gram[:, :], 0.0).then_inc(dev, 1)
                dve.wait_ge(dev, 3)
                v.tensor_copy(k.gram[0:C, 0:C], pG[:, 0:C])
                v.tensor_copy(k.gram[0:C, P:P + 1], pG[:, C:C + 1])


def node_rows(ap, chunk, parts):
    v = ap[bass.ds(chunk * DN, parts * NODE_ROWS)]
    return v.rearrange("(p n) f -> p (n f)", n=NODE_ROWS)


def attention_stage(nc, k, a):
    with Stage(nc, "at") as g:
        pairs = lambda name, shape, dt=F32: [g.sb(f"{name}{b}", shape, dt) for b in range(2)]
        idx = pairs("idx", [P, 2 * CT], I32)
        G = pairs("G", [P, 2 * CT * C])
        W = pairs("W", [P, 2 * CT * C])
        V = pairs("V", [P, CE])
        XF = pairs("XF", [P, CE])
        anew = pairs("anew", [P, CE])
        L = pairs("L", [P, CE])
        M = pairs("M", [P, CE + 1])
        A = pairs("A", [P, CE])
        S = pairs("S", [P, CE])
        Y = pairs("Y", [P, 2 * CT * C])
        Q = pairs("Q", [P, 2 * CT * C])
        Z = pairs("Z", [P, CT * C])
        R = pairs("R", [P, CT * C])
        em = pairs("em", [P, CT * C])
        st = pairs("st", [P, 3, 2 * CT])
        zt = pairs("zt", [P, 3, CT])
        pA = [g.ps(f"pA{b}", [P, CE]) for b in range(2)]
        pL = [g.ps(f"pL{b}", [P, CE]) for b in range(2)]
        pV = [g.ps(f"pV{b}", [P, CE]) for b in range(2)]
        pG = g.ps("pG", [C, C + 1])
        got = g.pair("got"); copied = g.pair("copied"); mlp_in = g.pair("mlp_in")
        s1_out = g.pair("s1_out"); d1_out = g.pair("d1_out")
        e = {n: g.sem(n) for n in ("staged", "passed", "zeros", "starts", "turned", "ends", "anew", "products", "logits", "values",
                                   "maxed", "diffs", "weights", "decay", "weighed", "summed", "back",
                                   "shifted", "recip", "ratio", "added", "sum", "cen", "sq", "sumsq", "ln", "dev", "norm", "masked",
                                   "gram", "zsum", "zcen", "zsq", "zsumsq", "zln", "zdev", "znorm")}
        low, high = slice(0, C), slice(C, P)
        with nc.Block() as block:

            @block.gpsimd
            def _(pool):
                gp = nc.gpsimd
                for b in range(2):
                    gp.memset(G[b][:, :], 0.0).then_inc(e["zeros"], 1)
                bound = pool.to_reg(N - 1)
                pool.wait_ge(e["zeros"], 2)
                with pool.Fori(0, ITERS) as j:
                    for b in range(2):
                        at = bass.ds((2 * j + b) * CT, CT)
                        pool.wait_ge(copied[b], 16 * j)
                        gp.tensor_copy(idx[b][:, 0:CT], k.src[:, at])
                        gp.tensor_copy(idx[b][:, CT:2 * CT], k.dst[:, at]).then_inc(e["staged"], 1)
                    for b in range(2):
                        pool.wait_ge(e["staged"], last_of(j, b))
                        pool.sem_inc(e["passed"], 1)
                        for t in range(CT):
                            for w in range(2):
                                gp.indirect_dma_start(
                                    out=G[b][:, (2 * t + w) * C:(2 * t + w + 1) * C], out_offset=None, in_=a["x"],
                                    in_offset=bass.IndirectOffsetOnAxis(
                                        ap=idx[b][:, w * CT + t:w * CT + t + 1], axis=0),
                                    bounds_check=bound, oob_is_err=False).then_inc(got[b], 16)

            @block.sync
            def _(sp):
                def load(j, used=True):
                    for b in range(2):
                        if used:
                            sp.wait_ge(e["weighed"], last_of(j - 1, b))
                        for h in (low, high):
                            sp.dma_start(V[b][h, :], k.mlp[:, bass.ds((2 * j + b) * CE, CE)]).then_inc(mlp_in[b], 16)
                    for b in range(2):
                        sp.wait_ge(got[b], 32 * CT * j + 32 * CT)
                        if used:
                            sp.wait_ge(e["added"], last_of(j - 1, b))
                        sp.dma_start(W[b][:, :], G[b][:, :]).then_inc(copied[b], 16)

                def store(j):
                    for b in range(2):
                        sp.wait_ge(e["norm"], last_of(j, b))
                        sp.dma_start(one(by_chunk(k.s1), 2 * j + b),
                                     Y[b][:, :].rearrange("p (t w c) -> p t w c", t=CT, w=2)[:, :, 0, :])\
                            .then_inc(s1_out[b], 16)
                    for b in range(2):
                        sp.wait_ge(e["znorm"], last_of(j, b))
                        sp.dma_start(one(by_chunk(k.d1), 2 * j + b), groups(Z[b][:, :], CT)).then_inc(d1_out[b], 16)

                load(0, used=False)
                with sp.Fori(0, ITERS - 1) as j:
                    load(j + 1)
                    store(j)
                store(ITERS - 1)
                for b in range(2):
                    sp.wait_ge(s1_out[b], 16 * ITERS)
                    sp.wait_ge(d1_out[b], 16 * ITERS)

            @block.tensor
            def _(pe):
                t = nc.tensor
                zero = k.w_value[:, low]
                t.matmul(pG[:, 0:C], zero, zero, start=True, stop=False, skip_group_check=True)
                t.matmul(pG[:, C:C + 1], zero, k.ones[:, 0:1], start=False, stop=False, skip_group_check=True)
                with pe.Fori(0, ITERS) as j:
                    for b in range(2):
                        pe.wait_ge(copied[b], 16 * j + 16)
                        pe.wait_ge(e["ratio"], 2 * j)
                        for n in range(CT):
                            i = t.transpose(pA[b][:, n * P:n * P + P], W[b][:, n * P:n * P + P], k.ident[:, :])
                        i.then_inc(e["turned"], 1)
                    for b in range(2):
                        pe.wait_ge(e["ends"], last_of(j, b))
                        t.matmul(pL[b][:, :], k.w_logit[:, :], XF[b][:, :], start=True, stop=True)
                        t.matmul(pV[b][:, :], k.w_value[:, :], XF[b][:, :], start=True, stop=True)\
                            .then_inc(e["products"], 1)
                    for b in range(2):
                        pe.wait_ge(e["masked"], last_of(j, b))
                        for n in range(CT):
                            m = em[b][:, n * C:n * C + C]
                            t.matmul(pG[:, 0:C], m, m, start=False, stop=False, skip_group_check=True)
                            i = t.matmul(pG[:, C:C + 1], m, k.ones[:, 0:1], start=False, stop=False,
                                         skip_group_check=True)
                        i.then_inc(e["gram"], 1)
                    for b in range(2):
                        pe.wait_ge(e["summed"], last_of(j, b))
                        for n in range(CT):
                            i = t.transpose(pA[b][:, n * P:n * P + P], S[b][:, n * P:n * P + P], k.ident[:, :])
                        i.then_inc(e["back"], 1)
                t.matmul(pG[:, C:C + 1], zero, k.ones[:, 0:1], start=False, stop=True,
                         skip_group_check=True).then_inc(e["gram"], 1)

            @block.scalar
            def _(act):
                s = nc.scalar
                s.preload_act_table_set(LN_EXP)

                with act.Fori(0, ITERS) as j:
                    for b in range(2):
                        act.wait_ge(e["turned"], last_of(j, b))
                        s.activation(XF[b][:, :], pA[b][:, :], ACT.Copy).then_inc(e["ends"], 1)
                    for b in range(2):
                        act.wait_ge(e["diffs"], 2 * j)
                        s.activation(anew[b][:, :], k.same[:, bass.ds((2 * j + b) * CE, CE)], ACT.Copy,
                                     scale=BIG, bias=-BIG).then_inc(e["anew"], 1)
                    for b in range(2):
                        act.wait_ge(e["cen"], last_of(j, b))
                        act.wait_ge(e["sumsq"], 2 * j)
                        s.activation(Q[b][:, :], Y[b][:, :], ACT.Square).then_inc(e["sq"], 1)
                    for b in range(2):
                        act.wait_ge(e["sumsq"], last_of(j, b))
                        s.activation(st[b][:, 1, :], st[b][:, 1, :], ACT.Ln, scale=1.0 / C, bias=k.eps[:, 0:1])\
                            .then_inc(e["ln"], 1)
                    for b in range(2):
                        act.wait_ge(e["ln"], last_of(j, b))
                        s.activation(st[b][:, 2, :], st[b][:, 1, :], ACT.Exp, scale=-0.5).then_inc(e["dev"], 1)
                    for b in range(2):
                        act.wait_ge(e["diffs"], last_of(j, b))
                        s.activation(A[b][:, :], A[b][:, :], ACT.Exp).then_inc(e["decay"], 1)
                        s.activation(L[b][:, :], L[b][:, :], ACT.Exp).then_inc(e["weights"], 1)
                    for b in range(2):
                        act.wait_ge(e["zcen"], last_of(j, b))
                        act.wait_ge(e["zsumsq"], 2 * j)
                        s.activation(R[b][:, :], Z[b][:, :], ACT.Square).then_inc(e["zsq"], 1)
                    for b in range(2):
                        act.wait_ge(e["zsumsq"], last_of(j, b))
                        s.activation(zt[b][:, 1, :], zt[b][:, 1, :], ACT.Ln, scale=1.0 / C, bias=k.eps[:, 0:1])\
                            .then_inc(e["zln"], 1)
                    for b in range(2):
                        act.wait_ge(e["zln"], last_of(j, b))
                        s.activation(zt[b][:, 2, :], zt[b][:, 1, :], ACT.Exp, scale=-0.5).then_inc(e["zdev"], 1)

            @block.vector
            def _(dve):
                v = nc.vector
                for b in range(2):
                    v.memset(M[b][:, :], -BIG).then_inc(e["starts"], 1)
                    v.memset(S[b][:, :], 0.0).then_inc(e["starts"], 1)
                dve.wait_ge(e["starts"], 4)
                with dve.Fori(0, ITERS) as j:
                    for b in range(2):
                        dve.wait_ge(copied[b], 16 * j + 16)
                        v.tensor_reduce(out=st[b][:, 0, :], in_=groups(W[b][:, :], 2 * CT), op=ALU.add, axis=AX)\
                            .then_inc(e["sum"], 1)
                    for b in range(2):
                        dve.wait_ge(e["sum"], last_of(j, b))
                        dve.wait_ge(s1_out[b], 16 * j)
                        dve.wait_ge(e["gram"], 2 * j)
                        v.scalar_tensor_tensor(groups(Y[b][:, :], 2 * CT), over(st[b][:, 0, :], C), -1.0 / C,
                                               groups(W[b][:, :], 2 * CT), ALU.mult, ALU.add).then_inc(e["cen"], 1)
                    for b in range(2):
                        dve.wait_ge(e["products"], last_of(j, b))
                        dve.wait_ge(mlp_in[b], 32 * j + 32)
                        v.tensor_tensor(L[b][:, :], pL[b][:, :], V[b][:, :], ALU.add).then_inc(e["logits"], 1)
                    for b in range(2):
                        dve.wait_ge(e["logits"], last_of(j, b))
                        v.tensor_tensor(V[b][high, :], V[b][high, :], pV[b][high, :], ALU.add)\
                            .then_inc(e["values"], 1)
                        v.tensor_copy(M[b][:, 0:1], M[1 - b][:, CE:CE + 1])
                        dve.wait_ge(e["anew"], last_of(j, b))
                        v.tensor_tensor_scan(M[b][:, 1:CE + 1], anew[b][:, :], L[b][:, :], M[1 - b][:, CE:CE + 1],
                                             ALU.add, ALU.max).then_inc(e["maxed"], 1)
                        dve.wait_ge(e["maxed"], last_of(j, b))
                    for b in range(2):
                        v.tensor_tensor(L[b][:, :], L[b][:, :], M[b][:, 1:CE + 1], ALU.subtract)
                        v.tensor_tensor(A[b][:, :], M[b][:, 0:CE], anew[b][:, :], ALU.add).then_inc(e["shifted"], 1)
                    for b in range(2):
                        dve.wait_ge(e["shifted"], last_of(j, b))
                        v.tensor_tensor(A[b][:, :], A[b][:, :], M[b][:, 1:CE + 1], ALU.subtract)\
                            .then_inc(e["diffs"], 1)
                    for b in range(2):
                        dve.wait_ge(e["sq"], last_of(j, b))
                        v.tensor_reduce(out=st[b][:, 1, :], in_=groups(Q[b][:, :], 2 * CT), op=ALU.add, axis=AX)\
                            .then_inc(e["sumsq"], 1)
                    for b in range(2):
                        dve.wait_ge(e["weights"], last_of(j, b))
                        v.tensor_tensor(L[b][high, :], L[b][high, :], V[b][high, :], ALU.mult)\
                            .then_inc(e["weighed"], 1)
                    for b in range(2):
                        dve.wait_ge(e["dev"], last_of(j, b))
                        v.tensor_tensor(groups(Y[b][:, :], 2 * CT), groups(Y[b][:, :], 2 * CT),
                                        over(st[b][:, 2, :], C), ALU.mult).then_inc(e["norm"], 1)
                    for b in range(2):
                        dve.wait_ge(e["weighed"], last_of(j, b))
                        v.tensor_tensor_scan(S[b][:, :], A[b][:, :], L[b][:, :], S[1 - b][:, CE - 1:CE],
                                             ALU.mult, ALU.add).then_inc(e["summed"], 1)
                        dve.wait_ge(e["summed"], last_of(j, b))
                    for b in range(2):
                        dve.wait_ge(e["norm"], last_of(j, b))
                        v.tensor_tensor(groups(em[b][:, :], CT),
                                        Y[b][:, :].rearrange("p (t w c) -> p t w c", t=CT, w=2)[:, :, 1, :],
                                        over(k.last[:, bass.ds((2 * j + b) * CT, CT)], C), ALU.mult)\
                            .then_inc(e["masked"], 1)
                    back = lambda b: pA[b][:, :].rearrange("p (t w c) -> p t w c", t=CT, w=2)
                    for b in range(2):
                        dve.wait_ge(e["back"], last_of(j, b))
                        dve.wait_ge(d1_out[b], 16 * j)
                        v.reciprocal(groups(Z[b][:, :], CT), back(b)[:, :, 0, :]).then_inc(e["recip"], 1)
                    for b in range(2):
                        dve.wait_ge(e["recip"], last_of(j, b))
                        v.tensor_tensor(groups(Z[b][:, :], CT), groups(Z[b][:, :], CT), back(b)[:, :, 1, :],
                                        ALU.mult).then_inc(e["ratio"], 1)
                    for b in range(2):
                        dve.wait_ge(e["ratio"], last_of(j, b))
                        v.tensor_tensor(groups(Z[b][:, :], CT), groups(Z[b][:, :], CT),
                                        W[b][:, :].rearrange("p (t w c) -> p t w c", t=CT, w=2)[:, :, 1, :],
                                        ALU.add).then_inc(e["added"], 1)
                    for b in range(2):
                        dve.wait_ge(e["added"], last_of(j, b))
                        v.tensor_reduce(out=zt[b][:, 0, :], in_=groups(Z[b][:, :], CT), op=ALU.add, axis=AX)\
                            .then_inc(e["zsum"], 1)
                    for b in range(2):
                        dve.wait_ge(e["zsum"], last_of(j, b))
                        v.scalar_tensor_tensor(groups(Z[b][:, :], CT), over(zt[b][:, 0, :], C), -1.0 / C,
                                               groups(Z[b][:, :], CT), ALU.mult, ALU.add).then_inc(e["zcen"], 1)
                    for b in range(2):
                        dve.wait_ge(e["zsq"], last_of(j, b))
                        v.tensor_reduce(out=zt[b][:, 1, :], in_=groups(R[b][:, :], CT), op=ALU.add, axis=AX)\
                            .then_inc(e["zsumsq"], 1)
                    for b in range(2):
                        dve.wait_ge(e["zdev"], last_of(j, b))
                        v.tensor_tensor(groups(Z[b][:, :], CT), groups(Z[b][:, :], CT), over(zt[b][:, 2, :], C),
                                        ALU.mult).then_inc(e["znorm"], 1)
                dve.wait_ge(e["gram"], 2 * ITERS + 1)
                v.tensor_tensor(k.gram[0:C, 0:C], k.gram[0:C, 0:C], pG[:, 0:C], ALU.subtract)
                v.tensor_tensor(k.gram[0:C, P:P + 1], k.gram[0:C, P:P + 1], pG[:, C:C + 1], ALU.subtract)


def override_rows(nc, pool, k, table, width, idx, landing, sems, trips, bound):
    gp = nc.gpsimd
    with pool.Fori(0, trips) as j:
        for b in range(2):
            pool.wait_ge(sems["copied"][b], 16 * j)
            gp.tensor_copy(idx[b][:, :], k.pos[:, bass.ds((2 * j + b) * CT, CT)]).then_inc(sems["staged"], 1)
        for b in range(2):
            pool.wait_ge(sems["staged"], last_of(j, b))
            pool.wait_ge(sems["landed"][b], 16 * j + 16)
            pool.sem_inc(sems["passed"], 1)
            for t in range(CT):
                gp.indirect_dma_start(out=landing[b][:, t * width:(t + 1) * width], out_offset=None, in_=table,
                                      in_offset=bass.IndirectOffsetOnAxis(ap=idx[b][:, t:t + 1], axis=0),
                                      bounds_check=bound, oob_is_err=False).then_inc(sems["got"][b], 16)


def ends(t):
    return t[:, :].rearrange("p (t w c) -> p t w c", t=CT, w=2)


def mean_stage(nc, k):
    with Stage(nc, "me") as g:
        pairs = lambda name, shape, dt=F32: [g.sb(f"{name}{b}", shape, dt) for b in range(2)]
        idx = pairs("idx", [P, CT], I32)
        landing = pairs("landing", [P, CT * C])
        W = pairs("W", [P, CE])
        S = pairs("S", [P, CE])
        X = pairs("X", [P, CE])
        XM = pairs("XM", [P, CE])
        st = pairs("st", [P, 3, CT])
        pA = [g.ps(f"pA{b}", [P, CE]) for b in range(2)]
        pB = [g.ps(f"pB{b}", [P, CE]) for b in range(2)]
        pG = g.ps("pG", [P, P + 1])
        landed = g.pair("landed"); got = g.pair("got"); copied = g.pair("copied"); d1_in = g.pair("d1_in")
        agg_out = g.pair("agg_out")
        e = {n: g.sem(n) for n in ("staged", "passed", "starts", "turned", "summed", "back", "degree", "rdeg", "mean", "ln",
                                   "dinv", "masked", "gram")}
        sems = dict(staged=e["staged"], passed=e["passed"], landed=landed, got=got, copied=copied)
        with nc.Block() as block:

            @block.gpsimd
            def _(pool):
                override_rows(nc, pool, k, k.d1, C, idx, landing, sems, ITERS, pool.to_reg(EP - 1))

            @block.sync
            def _(sp):
                def land(j):
                    for b in range(2):
                        if not isinstance(j, int):
                            sp.wait_ge(copied[b], 16 * j)
                        sp.dma_start(groups(landing[b][:, :], CT), one(by_chunk(k.s1), 2 * j + b))\
                            .then_inc(landed[b], 16)

                def load(j, used=True):
                    for b in range(2):
                        if used:
                            sp.wait_ge(e["masked"], last_of(j - 1, b))
                        sp.dma_start(ends(X[b])[:, :, 0, :], one(by_chunk(k.d1), 2 * j + b)).then_inc(d1_in[b], 16)

                def take(j, used=True):
                    for b in range(2):
                        sp.wait_ge(got[b], 16 * CT * j + 16 * CT)
                        if used:
                            sp.wait_ge(e["turned"], last_of(j - 1, b))
                        sp.dma_start(ends(W[b])[:, :, 0, :], groups(landing[b][:, :], CT)).then_inc(copied[b], 16)

                def store(j):
                    for b in range(2):
                        sp.wait_ge(e["mean"], last_of(j, b))
                        sp.dma_start(one(by_chunk(k.agg), 2 * j + b), ends(X[b])[:, :, 1, :]).then_inc(agg_out[b], 16)

                sp.wait_ge(e["starts"], 3)
                land(0)
                load(0, used=False)
                take(0, used=False)
                with sp.Fori(0, ITERS - 1) as j:
                    land(j + 1)
                    load(j + 1)
                    take(j + 1)
                    store(j)
                store(ITERS - 1)
                for b in range(2):
                    sp.wait_ge(agg_out[b], 16 * ITERS)

            @block.tensor
            def _(pe):
                t = nc.tensor
                pe.wait_ge(e["starts"], 3)
                t.matmul(pG[:, 0:P], S[1][:, 0:P], S[1][:, 0:P], start=True, stop=False, skip_group_check=True)
                t.matmul(pG[:, P:P + 1], S[1][:, 0:P], k.ones[:, 0:1], start=False, stop=False,
                         skip_group_check=True).then_inc(e["gram"], 1)
                with pe.Fori(0, ITERS) as j:
                    for b in range(2):
                        pe.wait_ge(copied[b], 16 * j + 16)
                        pe.wait_ge(e["summed"], 2 * j)
                        for n in range(CT):
                            i = t.transpose(pA[b][:, n * P:n * P + P], W[b][:, n * P:n * P + P], k.ident[:, :])
                        i.then_inc(e["turned"], 1)
                    for b in range(2):
                        pe.wait_ge(e["summed"], last_of(j, b))
                        pe.wait_ge(e["mean"], 2 * j)
                        for n in range(CT):
                            i = t.transpose(pB[b][:, n * P:n * P + P], S[b][:, n * P:n * P + P], k.ident[:, :])
                        i.then_inc(e["back"], 1)
                    for b in range(2):
                        pe.wait_ge(e["masked"], last_of(j, b))
                        for n in range(CT):
                            m = XM[b][:, n * P:n * P + P]
                            t.matmul(pG[:, 0:P], m, m, start=False, stop=False, skip_group_check=True)
                            i = t.matmul(pG[:, P:P + 1], m, k.ones[:, 0:1], start=False, stop=False,
                                         skip_group_check=True)
                        i.then_inc(e["gram"], 1)

            @block.scalar
            def _(act):
                s = nc.scalar
                s.preload_act_table_set(LN_EXP)
                with act.Fori(0, ITERS) as j:
                    for b in range(2):
                        act.wait_ge(e["dinv"], 2 * j)
                        act.wait_ge(e["degree"], last_of(j, b))
                        s.activation(st[b][:, 1, :], st[b][:, 2, :], ACT.Ln, bias=k.eps[:, 3:4])\
                            .then_inc(e["ln"], 1)
                    for b in range(2):
                        act.wait_ge(e["ln"], last_of(j, b))
                        s.activation(k.dinv[:, bass.ds((2 * j + b) * CT, CT)], st[b][:, 1, :], ACT.Exp, scale=-0.5)\
                            .then_inc(e["dinv"], 1)

            @block.vector
            def _(dve):
                v = nc.vector
                for b in range(2):
                    v.memset(W[b][:, :], 1.0).then_inc(e["starts"], 1)
                v.memset(S[1][:, :], 0.0).then_inc(e["starts"], 1)
                dve.wait_ge(e["gram"], 1)
                with dve.Fori(0, ITERS) as j:
                    for b in range(2):
                        at = bass.ds((2 * j + b) * CE, CE)
                        dve.wait_ge(e["turned"], last_of(j, b))
                        v.tensor_tensor_scan(S[b][:, :], k.same[:, at], pA[b][:, :], S[1 - b][:, CE - 1:CE],
                                             ALU.mult, ALU.add).then_inc(e["summed"], 1)
                        dve.wait_ge(e["summed"], last_of(j, b))
                    for b in range(2):
                        dve.wait_ge(e["back"], last_of(j, b))
                        dve.wait_ge(e["ln"], 2 * j)
                        v.tensor_copy(st[b][:, 2, :], ends(pB[b])[:, :, 1, 0]).then_inc(e["degree"], 1)
                    for b in range(2):
                        dve.wait_ge(e["degree"], last_of(j, b))
                        v.reciprocal(st[b][:, 0, :], st[b][:, 2, :]).then_inc(e["rdeg"], 1)
                    for b in range(2):
                        dve.wait_ge(e["rdeg"], last_of(j, b))
                        dve.wait_ge(agg_out[b], 16 * j)
                        v.tensor_tensor(ends(X[b])[:, :, 1, :], ends(pB[b])[:, :, 0, :], over(st[b][:, 0, :], C),
                                        ALU.mult).then_inc(e["mean"], 1)
                    for b in range(2):
                        dve.wait_ge(e["mean"], last_of(j, b))
                        dve.wait_ge(d1_in[b], 16 * j + 16)
                        dve.wait_ge(e["gram"], 2 * j + 1)
                        v.tensor_tensor(groups(XM[b][:, :], CT), groups(X[b][:, :], CT),
                                        over(k.last[:, bass.ds((2 * j + b) * CT, CT)], P), ALU.mult)\
                            .then_inc(e["masked"], 1)
                dve.wait_ge(e["gram"], 2 * ITERS + 1)
                v.tensor_tensor(k.gram[:, :], k.gram[:, :], pG[:, :], ALU.add)


def batch_norm_stage(nc, k):
    with Stage(nc, "bn") as g:
        gw = g.sb("gw", [P, C])
        r = g.sb("r", [1, 8, C])
        pW = g.ps("pW", [P, C]); pR = g.ps("pR", [1, 2, C]); pB = g.ps("pB", [P, C])
        prod = g.sem("prod"); steps = g.sem("steps"); ln = g.sem("ln"); fold = g.sem("fold")
        mean, ex2, var, scale, shift = (r[:, n, :] for n in range(5))
        with nc.Block() as block:

            @block.tensor
            def _(pe):
                t = nc.tensor
                t.matmul(pW[:, :], k.gram[:, 0:P], k.wcat[:, :], start=True, stop=True).then_inc(prod, 1)
                t.matmul(pR[:, 0, :], k.gram[:, P:P + 1], k.wcat[:, :], start=True, stop=True).then_inc(prod, 1)
                pe.wait_ge(steps, 1)
                pe.wait_ge(steps, 2)
                t.matmul(pR[:, 1, :], k.ones[:, 0:1], gw[:, :], start=True, stop=True).then_inc(prod, 1)
                pe.wait_ge(fold, 1)
                t.matmul(pB[:, :], k.ones[0:1, :], scale, start=True, stop=True).then_inc(prod, 1)

            @block.scalar
            def _(act):
                act.wait_ge(steps, 5)
                nc.scalar.activation(var, var, ACT.Ln, bias=k.eps[0:1, 0:1]).then_inc(ln, 1)
                act.wait_ge(ln, 1)
                nc.scalar.activation(scale, var, ACT.Exp, scale=-0.5).then_inc(ln, 1)

            @block.vector
            def _(dve):
                v = nc.vector
                b, gamma, beta = (k.bnrow[:, n, :] for n in range(3))
                dve.wait_ge(prod, 2)
                v.scalar_tensor_tensor(gw[:, :], pW[:, :], 1.0 / N, k.wcat[:, :], ALU.mult, ALU.mult)\
                    .then_inc(steps, 1)
                v.tensor_scalar(mean, pR[:, 0, :], 1.0 / N, None, ALU.mult).then_inc(steps, 1)
                dve.wait_ge(steps, 2)
                v.tensor_tensor(ex2, mean, mean, ALU.mult).then_inc(steps, 1)
                dve.wait_ge(steps, 3)
                dve.wait_ge(prod, 3)
                v.tensor_tensor(var, pR[:, 1, :], ex2, ALU.subtract).then_inc(steps, 1)
                dve.wait_ge(steps, 4)
                v.tensor_scalar(var, var, 0.0, None, ALU.max).then_inc(steps, 1)
                v.tensor_tensor(mean, mean, b, ALU.add).then_inc(steps, 1)
                dve.wait_ge(steps, 6)
                v.tensor_tensor(shift, b, mean, ALU.subtract).then_inc(steps, 1)
                dve.wait_ge(ln, 2)
                v.tensor_tensor(scale, scale, gamma, ALU.mult).then_inc(fold, 1)
                dve.wait_ge(fold, 1)
                dve.wait_ge(steps, 7)
                v.tensor_tensor(shift, shift, scale, ALU.mult).then_inc(steps, 1)
                dve.wait_ge(steps, 8)
                v.tensor_tensor(shift, shift, beta, ALU.add).then_inc(steps, 1)
                dve.wait_ge(steps, 9)
                for n in range(NODE_ROWS):
                    v.tensor_copy(k.shift[:, n, :], shift)
                v.memset(k.wbn_r[:, :], 0.0).then_inc(steps, 1)
                dve.wait_ge(prod, 4)
                v.tensor_tensor(k.wbn[:, :], k.wcat[:, :], pB[:, :], ALU.mult).then_inc(steps, 1)
                dve.wait_ge(steps, 11)
                v.tensor_copy(k.wbn_r[0:C, 0:C], k.wbn[0:C, :])
                v.tensor_copy(k.wbn_r[C:P, C:P], k.wbn[0:C, :])


def update_stage(nc, k):
    Q2 = NT // 2
    with Stage(nc, "up") as g:
        pairs = lambda name, shape, dt=F32: [g.sb(f"{name}{b}", shape, dt) for b in range(2)]
        X = pairs("X", [P, CE])
        R = pairs("R", [P, CT * C])
        XF = pairs("XF", [P, CE])
        RF = pairs("RF", [P, CE // 2])
        U = pairs("U", [P, 2 * CT * C])
        Q = pairs("Q", [P, 2 * CT * C])
        T = pairs("T", [P, CT * C])
        st = pairs("st", [P, 5, 2 * CT])
        dot = g.sb("dot", [P, NT])
        dq = g.sb("dq", [Q2, 2 * P]); more = g.sb("more", [Q2, 2 * P]); cum = g.sb("cum", [Q2, 2 * P])
        dvq = g.sb("dvq", [Q2, 2 * P]); zero = g.sb("zero", [Q2, 2 * P])
        crow = g.sb("crow", [1, 4, Q2 + 1])
        pX = [g.ps(f"pX{b}", [P, CE]) for b in range(2)]
        pR = [g.ps(f"pR{b}", [P, CE // 2]) for b in range(2)]
        pH = [g.ps(f"pH{b}", [P, 2 * CT * C]) for b in range(2)]
        x_in = g.pair("x_in"); out_sems = g.pair("out"); rows_out = g.sem("rows_out")
        names = ("turned", "flat", "product", "relu", "sq", "sumsq", "clamped", "ln", "inv", "scaled", "added", "sum",
                 "cen", "sq2", "sumsq2", "ln2", "dev", "norm", "weighed", "dot", "passed", "tail_pe", "tail", "ready")
        e = {n: g.sem(n) for n in names}
        with nc.Block() as block:

            @block.sync
            def _(sp):
                def load(j, used=True):
                    for b in range(2):
                        if used:
                            sp.wait_ge(e["added"], last_of(j - 1, b))
                        i = 2 * j + b
                        sp.dma_start(ends(X[b])[:, :, 0, :], one(by_chunk(k.d1), i)).then_inc(x_in[b], 16)
                        sp.dma_start(ends(X[b])[:, :, 1, :], one(by_chunk(k.agg), i)).then_inc(x_in[b], 16)
                        sp.dma_start(groups(R[b][:, :], CT), one(by_chunk(k.s1), i)).then_inc(x_in[b], 16)

                def store(j):
                    for b in range(2):
                        sp.wait_ge(e["norm"], last_of(j, b))
                        for n, table in enumerate((k.d2, k.s2)):
                            sp.dma_start(one(by_chunk(table), 2 * j + b),
                                         groups(U[b][:, n * CT * C:(n + 1) * CT * C], CT)).then_inc(out_sems[b], 16)

                load(0, used=False)
                with sp.Fori(0, ITERS - 1) as j:
                    load(j + 1)
                    store(j)
                store(ITERS - 1)
                sp.wait_ge(e["ready"], 1)
                sp.dma_start(k.att_d.rearrange("(q e) -> q e", e=2 * P), dq[:, :]).then_inc(rows_out, 16)
                sp.dma_start(k.dinv_row.rearrange("(q e) -> q e", e=2 * P), dvq[:, :]).then_inc(rows_out, 16)
                sp.wait_ge(rows_out, 32)
                for b in range(2):
                    sp.wait_ge(out_sems[b], 32 * ITERS)

            @block.tensor
            def _(pe):
                t = nc.tensor
                with pe.Fori(0, ITERS) as j:
                    for b in range(2):
                        pe.wait_ge(x_in[b], 48 * j + 48)
                        pe.wait_ge(e["flat"], 2 * j)
                        for n in range(CT):
                            t.transpose(pX[b][:, n * P:n * P + P], X[b][:, n * P:n * P + P], k.ident[:, :])
                        for n in range(CT // 2):
                            i = t.transpose(pR[b][:, n * P:n * P + P], R[b][:, n * P:n * P + P], k.ident[:, :])
                        i.then_inc(e["turned"], 1)
                    for b in range(2):
                        pe.wait_ge(e["flat"], last_of(j, b))
                        pe.wait_ge(e["relu"], 2 * j)
                        t.matmul(pH[b][:, :], k.ones[0:1, :], k.shift[:, :, :].rearrange("a n c -> a (n c)"),
                                 start=True, stop=False, skip_group_check=True)
                        for n in range(CT):
                            t.matmul(pH[b][:, n * C:n * C + C], XF[b][:, n * P:n * P + P], k.wbn[:, :],
                                     start=False, stop=False, skip_group_check=True)
                        for n in range(CT // 2):
                            i = t.matmul(pH[b][:, CT * C + n * P:CT * C + n * P + P], RF[b][:, n * P:n * P + P],
                                         k.wbn_r[:, :], start=False, stop=n == CT // 2 - 1, skip_group_check=True)
                        i.then_inc(e["product"], 1)
                pe.wait_ge(e["dot"], 2 * ITERS)
                for n, src in enumerate((dot, k.dinv)):
                    for h in range(2):
                        i = t.transpose(pX[n][0:Q2, h * P:h * P + P],
                                        src[:, :].rearrange("p (q h) -> p h q", h=2)[:, h, :], k.ident[:, :])
                i.then_inc(e["tail_pe"], 1)
                pe.wait_ge(e["tail"], 5)
                t.matmul(pR[0][0:1, 0:Q2], dq[:, 0:1], k.ident[0:Q2, 0:Q2], start=True, stop=True)
                t.matmul(pR[1][0:1, 0:Q2], cum[:, 0:1], k.ident[0:Q2, 0:Q2], start=True, stop=True)\
                    .then_inc(e["tail_pe"], 1)
                pe.wait_ge(e["tail"], 8)
                t.matmul(pH[0][0:Q2, 0:1], crow[:, 2, 1:Q2 + 1], k.ones[0:1, 0:1], start=True, stop=True)\
                    .then_inc(e["tail_pe"], 1)

            @block.scalar
            def _(act):
                s = nc.scalar
                s.preload_act_table_set(LN_EXP)
                with act.Fori(0, ITERS) as j:
                    for b in range(2):
                        act.wait_ge(e["turned"], last_of(j, b))
                        act.wait_ge(e["product"], 2 * j)
                        s.activation(XF[b][:, :], pX[b][:, :], ACT.Copy)
                        s.activation(RF[b][:, :], pR[b][:, :], ACT.Copy).then_inc(e["flat"], 1)
                    for b in range(2):
                        act.wait_ge(e["product"], last_of(j, b))
                        act.wait_ge(out_sems[b], 32 * j)
                        act.wait_ge(e["weighed"], 2 * j)
                        s.activation(U[b][:, :], pH[b][:, :], ACT.Relu).then_inc(e["relu"], 1)
                    for b in range(2):
                        act.wait_ge(e["relu"], last_of(j, b))
                        s.activation(Q[b][:, :], U[b][:, :], ACT.Square).then_inc(e["sq"], 1)
                    for b in range(2):
                        act.wait_ge(e["clamped"], last_of(j, b))
                        s.activation(st[b][:, 1, :], st[b][:, 0, :], ACT.Ln, scale=2.0 ** 20).then_inc(e["ln"], 1)
                    for b in range(2):
                        act.wait_ge(e["ln"], last_of(j, b))
                        s.activation(st[b][:, 1, :], st[b][:, 1, :], ACT.Exp, scale=-0.5, bias=k.eps[:, 2:3])\
                            .then_inc(e["inv"], 1)
                    for b in range(2):
                        act.wait_ge(e["cen"], last_of(j, b))
                        s.activation(Q[b][:, :], U[b][:, :], ACT.Square).then_inc(e["sq2"], 1)
                    for b in range(2):
                        act.wait_ge(e["sumsq2"], last_of(j, b))
                        s.activation(st[b][:, 3, :], st[b][:, 3, :], ACT.Ln, scale=1.0 / C, bias=k.eps[:, 0:1])\
                            .then_inc(e["ln2"], 1)
                    for b in range(2):
                        act.wait_ge(e["ln2"], last_of(j, b))
                        s.activation(st[b][:, 4, :], st[b][:, 3, :], ACT.Exp, scale=-0.5).then_inc(e["dev"], 1)

            @block.vector
            def _(dve):
                v = nc.vector
                U8 = lambda b: groups(U[b][:, :], 2 * CT)
                with dve.Fori(0, ITERS) as j:
                    for b in range(2):
                        dve.wait_ge(e["sq"], last_of(j, b))
                        v.tensor_reduce(out=st[b][:, 0, :], in_=groups(Q[b][:, :], 2 * CT), op=ALU.add, axis=AX)\
                            .then_inc(e["sumsq"], 1)
                    for b in range(2):
                        dve.wait_ge(e["sumsq"], last_of(j, b))
                        v.tensor_scalar(st[b][:, 0, :], st[b][:, 0, :], 1e-24, None, ALU.max).then_inc(e["clamped"], 1)
                    for b in range(2):
                        dve.wait_ge(e["inv"], last_of(j, b))
                        v.tensor_tensor(U8(b), U8(b), over(st[b][:, 1, :], C), ALU.mult).then_inc(e["scaled"], 1)
                    for b in range(2):
                        dve.wait_ge(e["scaled"], last_of(j, b))
                        v.tensor_tensor(U8(b)[:, 0:CT, :], U8(b)[:, 0:CT, :], ends(X[b])[:, :, 0, :], ALU.add)
                        v.tensor_tensor(U8(b)[:, CT:2 * CT, :], U8(b)[:, CT:2 * CT, :], groups(R[b][:, :], CT), ALU.add)\
                            .then_inc(e["added"], 1)
                    for b in range(2):
                        dve.wait_ge(e["added"], last_of(j, b))
                        v.tensor_reduce(out=st[b][:, 2, :], in_=U8(b), op=ALU.add, axis=AX).then_inc(e["sum"], 1)
                    for b in range(2):
                        dve.wait_ge(e["sum"], last_of(j, b))
                        v.scalar_tensor_tensor(U8(b), over(st[b][:, 2, :], C), -1.0 / C, U8(b), ALU.mult, ALU.add)\
                            .then_inc(e["cen"], 1)
                    for b in range(2):
                        dve.wait_ge(e["sq2"], last_of(j, b))
                        v.tensor_reduce(out=st[b][:, 3, :], in_=groups(Q[b][:, :], 2 * CT), op=ALU.add, axis=AX)\
                            .then_inc(e["sumsq2"], 1)
                    for b in range(2):
                        dve.wait_ge(e["dev"], last_of(j, b))
                        v.tensor_tensor(U8(b), U8(b), over(st[b][:, 4, :], C), ALU.mult).then_inc(e["norm"], 1)
                    for b in range(2):
                        dve.wait_ge(e["norm"], last_of(j, b))
                        v.tensor_tensor(groups(T[b][:, :], CT), U8(b)[:, 0:CT, :],
                                        k.w_att_d[:, :].unsqueeze(1).to_broadcast([P, CT, C]), ALU.mult)\
                            .then_inc(e["weighed"], 1)
                    for b in range(2):
                        dve.wait_ge(e["weighed"], last_of(j, b))
                        dve.sem_inc(e["passed"], 1)
                        v.tensor_reduce(out=dot[:, bass.ds((2 * j + b) * CT, CT)], in_=groups(T[b][:, :], CT),
                                        op=ALU.add, axis=AX).then_inc(e["dot"], 1)
                left = lambda ap: ap[:, ::-1]
                v.memset(zero[:, :], 0.0)
                v.memset(crow[:, 2, Q2:Q2 + 1], 0.0)
                v.tensor_scalar(more[:, :], k.lastq[:, :], -1.0, 1.0, ALU.mult, ALU.add).then_inc(e["tail"], 1)
                dve.wait_ge(e["tail_pe"], 1)
                v.tensor_copy(dvq[:, :], pX[1][0:Q2, 0:2 * P]).then_inc(e["tail"], 1)
                v.tensor_tensor(dq[:, :], pX[0][0:Q2, 0:2 * P], k.lastq[:, :], ALU.mult).then_inc(e["tail"], 1)
                dve.wait_ge(e["tail"], 3)
                v.tensor_tensor_scan(left(cum[:, :]), left(more[:, :]), left(zero[:, :]), 1.0, ALU.mult, ALU.add)\
                    .then_inc(e["tail"], 1)
                v.tensor_tensor_scan(left(dq[:, :]), left(more[:, :]), left(dq[:, :]), 0.0, ALU.mult, ALU.add)\
                    .then_inc(e["tail"], 1)
                dve.wait_ge(e["tail_pe"], 2)
                v.tensor_copy(crow[:, 0, 0:Q2], pR[0][0:1, 0:Q2])
                v.tensor_copy(crow[:, 1, 0:Q2], pR[1][0:1, 0:Q2]).then_inc(e["tail"], 1)
                dve.wait_ge(e["tail"], 6)
                v.tensor_tensor_scan(left(crow[:, 2, 0:Q2]), left(crow[:, 1, 0:Q2]), left(crow[:, 0, 0:Q2]), 0.0,
                                     ALU.mult, ALU.add).then_inc(e["tail"], 1)
                dve.wait_ge(e["tail"], 7)
                v.tensor_scalar(dq[:, :], dq[:, :], k.b_att[0:Q2, 0:1], None, ALU.add).then_inc(e["tail"], 1)
                dve.wait_ge(e["tail"], 8)
                dve.wait_ge(e["tail_pe"], 3)
                v.tensor_copy(more[:, 0:1], pH[0][0:Q2, 0:1]).then_inc(e["tail"], 1)
                dve.wait_ge(e["tail"], 9)
                v.scalar_tensor_tensor(dq[:, :], cum[:, :], more[:, 0:1], dq[:, :], ALU.mult, ALU.add)\
                    .then_inc(e["ready"], 1)


def attention2_stage(nc, k):
    with Stage(nc, "a2") as g:
        pairs = lambda name, shape, dt=F32: [g.sb(f"{name}{b}", shape, dt) for b in range(2)]
        idx = pairs("idx", [P, CT], I32)
        landing = pairs("landing", [P, CT * C])
        W = pairs("W", [P, CE])
        D = pairs("D", [P, CT * C])
        AD = pairs("AD", [P, CE])
        XF = pairs("XF", [P, CE])
        anew = pairs("anew", [P, CE])
        L = pairs("L", [P, CE])
        M = pairs("M", [P, CE + 1])
        A = pairs("A", [P, CE])
        S = pairs("S", [P, CE])
        Y = pairs("Y", [P, 2 * CT * C])
        Q = pairs("Q", [P, 2 * CT * C])
        T = pairs("T", [P, CT * C])
        st = pairs("st", [P, 3, 2 * CT])
        pA = [g.ps(f"pA{b}", [P, CE]) for b in range(2)]
        pL = [g.ps(f"pL{b}", [P, CE]) for b in range(2)]
        landed = g.pair("landed"); got = g.pair("got"); copied = g.pair("copied")
        own_in = g.pair("own_in"); rows_out = g.pair("rows_out")
        e = {n: g.sem(n) for n in ("staged", "passed", "starts", "turned", "ends", "own", "anew", "product", "sum1",
                                   "logits", "maxed", "shifted", "diffs", "weights", "weighed", "summed", "back",
                                   "recip", "ratio", "added", "sum", "cen", "sq", "sumsq", "ln", "dev", "norm", "over")}
        sems = dict(staged=e["staged"], passed=e["passed"], landed=landed, got=got, copied=copied)
        high = slice(C, P)
        with nc.Block() as block:

            @block.gpsimd
            def _(pool):
                override_rows(nc, pool, k, k.d2, C, idx, landing, sems, ITERS, pool.to_reg(EP - 1))

            @block.sync
            def _(sp):
                def load(j, used=True):
                    for b in range(2):
                        i = 2 * j + b
                        if used:
                            sp.wait_ge(copied[b], 16 * j)
                        sp.dma_start(groups(landing[b][:, :], CT), one(by_chunk(k.s2), i)).then_inc(landed[b], 16)
                    for b in range(2):
                        i = 2 * j + b
                        if used:
                            sp.wait_ge(e["added"], last_of(j - 1, b))
                        sp.dma_start(groups(D[b][:, :], CT), one(by_chunk(k.d2), i)).then_inc(own_in[b], 16)
                        sp.dma_start(AD[b][:, :], row(k.att_d[bass.ds(i * CE, CE)], CE).to_broadcast([P, CE]))\
                            .then_inc(own_in[b], 16)
                    for b in range(2):
                        sp.wait_ge(got[b], 16 * CT * j + 16 * CT)
                        if used:
                            sp.wait_ge(e["own"], last_of(j - 1, b))
                            sp.wait_ge(e["turned"], last_of(j - 1, b))
                        sp.dma_start(ends(W[b])[:, :, 1, :], groups(landing[b][:, :], CT)).then_inc(copied[b], 16)

                def store(j):
                    for b in range(2):
                        i = 2 * j + b
                        sp.wait_ge(e["norm"], last_of(j, b))
                        sp.dma_start(one(by_chunk(k.x3), i), groups(Y[b][:, 0:CT * C], CT)).then_inc(rows_out[b], 16)
                        sp.dma_start(one(by_chunk(k.s3), i), groups(Y[b][:, CT * C:], CT)).then_inc(rows_out[b], 16)
                    for b in range(2):
                        i = 2 * j + b
                        sp.wait_ge(e["over"], last_of(j, b))
                        sp.dma_start(one(by_chunk(k.d3), i), groups(T[b][:, :], CT)).then_inc(rows_out[b], 16)

                sp.wait_ge(e["starts"], 2)
                load(0, used=False)
                with sp.Fori(0, ITERS - 1) as j:
                    load(j + 1)
                    store(j)
                store(ITERS - 1)
                for b in range(2):
                    sp.wait_ge(rows_out[b], 48 * ITERS)

            @block.tensor
            def _(pe):
                t = nc.tensor
                with pe.Fori(0, ITERS) as j:
                    for b in range(2):
                        pe.wait_ge(copied[b], 16 * j + 16)
                        pe.wait_ge(e["ratio"], 2 * j)
                        for n in range(CT):
                            i = t.transpose(pA[b][:, n * P:n * P + P], W[b][:, n * P:n * P + P], k.ident[:, :])
                        i.then_inc(e["turned"], 1)
                    for b in range(2):
                        pe.wait_ge(e["ends"], last_of(j, b))
                        t.matmul(pL[b][:, :], k.w_att_s[:, :], XF[b][:, :], start=True, stop=True)\
                            .then_inc(e["product"], 1)
                    for b in range(2):
                        pe.wait_ge(e["summed"], last_of(j, b))
                        for n in range(CT):
                            i = t.transpose(pA[b][:, n * P:n * P + P], S[b][:, n * P:n * P + P], k.ident[:, :])
                        i.then_inc(e["back"], 1)

            @block.scalar
            def _(act):
                s = nc.scalar
                s.preload_act_table_set(LN_EXP)
                with act.Fori(0, ITERS) as j:
                    for b in range(2):
                        act.wait_ge(e["turned"], last_of(j, b))
                        act.wait_ge(e["weighed"], 2 * j)
                        s.activation(XF[b][:, :], pA[b][:, :], ACT.Copy).then_inc(e["ends"], 1)
                    for b in range(2):
                        act.wait_ge(copied[b], 16 * j + 16)
                        act.wait_ge(rows_out[b], 48 * j)
                        s.activation(groups(Y[b][:, CT * C:], CT), ends(W[b])[:, :, 1, :], ACT.Copy)\
                            .then_inc(e["own"], 1)
                    for b in range(2):
                        act.wait_ge(e["diffs"], 2 * j)
                        s.activation(anew[b][:, :], k.same[:, bass.ds((2 * j + b) * CE, CE)], ACT.Copy,
                                     scale=BIG, bias=-BIG).then_inc(e["anew"], 1)
                    for b in range(2):
                        act.wait_ge(e["diffs"], last_of(j, b))
                        s.activation(A[b][:, :], A[b][:, :], ACT.Exp)
                        s.activation(L[b][:, :], L[b][:, :], ACT.Exp).then_inc(e["weights"], 1)
                    for b in range(2):
                        act.wait_ge(e["cen"], last_of(j, b))
                        act.wait_ge(e["sumsq"], 2 * j)
                        s.activation(Q[b][:, :], Y[b][:, :], ACT.Square).then_inc(e["sq"], 1)
                    for b in range(2):
                        act.wait_ge(e["sumsq"], last_of(j, b))
                        s.activation(st[b][:, 1, :], st[b][:, 1, :], ACT.Ln, scale=1.0 / C, bias=k.eps[:, 0:1])\
                            .then_inc(e["ln"], 1)
                    for b in range(2):
                        act.wait_ge(e["ln"], last_of(j, b))
                        s.activation(st[b][:, 2, :], st[b][:, 1, :], ACT.Exp, scale=-0.5).then_inc(e["dev"], 1)

            @block.vector
            def _(dve):
                v = nc.vector
                Y8 = lambda b: groups(Y[b][:, :], 2 * CT)
                for b in range(2):
                    v.memset(W[b][:, :], 0.0).then_inc(e["starts"], 1)
                v.memset(M[1][:, :], -BIG).then_inc(e["starts"], 1)
                v.memset(S[1][:, :], 0.0).then_inc(e["starts"], 1)
                dve.wait_ge(e["starts"], 4)
                with dve.Fori(0, ITERS) as j:
                    for b in range(2):
                        dve.wait_ge(e["product"], last_of(j, b))
                        dve.wait_ge(own_in[b], 32 * j + 32)
                        v.tensor_tensor(L[b][:, :], pL[b][:, :], AD[b][:, :], ALU.add).then_inc(e["sum1"], 1)
                    for b in range(2):
                        dve.wait_ge(e["sum1"], last_of(j, b))
                        v.scalar_tensor_tensor(L[b][:, :], L[b][:, :], 0.01, L[b][:, :], ALU.mult, ALU.max)\
                            .then_inc(e["logits"], 1)
                    for b in range(2):
                        dve.wait_ge(e["logits"], last_of(j, b))
                        v.tensor_copy(M[b][:, 0:1], M[1 - b][:, CE:CE + 1])
                        dve.wait_ge(e["anew"], last_of(j, b))
                        v.tensor_tensor_scan(M[b][:, 1:CE + 1], anew[b][:, :], L[b][:, :], M[1 - b][:, CE:CE + 1],
                                             ALU.add, ALU.max).then_inc(e["maxed"], 1)
                        dve.wait_ge(e["maxed"], last_of(j, b))
                    for b in range(2):
                        v.tensor_tensor(L[b][:, :], L[b][:, :], M[b][:, 1:CE + 1], ALU.subtract)
                        v.tensor_tensor(A[b][:, :], M[b][:, 0:CE], anew[b][:, :], ALU.add).then_inc(e["shifted"], 1)
                    for b in range(2):
                        dve.wait_ge(e["shifted"], last_of(j, b))
                        v.tensor_tensor(A[b][:, :], A[b][:, :], M[b][:, 1:CE + 1], ALU.subtract)\
                            .then_inc(e["diffs"], 1)
                    for b in range(2):
                        dve.wait_ge(e["weights"], last_of(j, b))
                        v.tensor_tensor(L[b][high, :], L[b][high, :], XF[b][high, :], ALU.mult)\
                            .then_inc(e["weighed"], 1)
                    for b in range(2):
                        dve.wait_ge(e["weighed"], last_of(j, b))
                        v.tensor_tensor_scan(S[b][:, :], A[b][:, :], L[b][:, :], S[1 - b][:, CE - 1:CE],
                                             ALU.mult, ALU.add).then_inc(e["summed"], 1)
                        dve.wait_ge(e["summed"], last_of(j, b))
                    for b in range(2):
                        dve.wait_ge(e["back"], last_of(j, b))
                        v.reciprocal(st[b][:, 0, 0:CT], ends(pA[b])[:, :, 0, 0]).then_inc(e["recip"], 1)
                    for b in range(2):
                        dve.wait_ge(e["recip"], last_of(j, b))
                        dve.wait_ge(rows_out[b], 48 * j)
                        v.tensor_tensor(Y8(b)[:, 0:CT, :], ends(pA[b])[:, :, 1, :], over(st[b][:, 0, 0:CT], C),
                                        ALU.mult).then_inc(e["ratio"], 1)
                    for b in range(2):
                        dve.wait_ge(e["ratio"], last_of(j, b))
                        v.tensor_tensor(Y8(b)[:, 0:CT, :], Y8(b)[:, 0:CT, :], groups(D[b][:, :], CT), ALU.add)\
                            .then_inc(e["added"], 1)
                    for b in range(2):
                        dve.wait_ge(e["added"], last_of(j, b))
                        dve.wait_ge(e["own"], last_of(j, b))
                        v.tensor_reduce(out=st[b][:, 0, :], in_=Y8(b), op=ALU.add, axis=AX).then_inc(e["sum"], 1)
                    for b in range(2):
                        dve.wait_ge(e["sum"], last_of(j, b))
                        v.scalar_tensor_tensor(Y8(b), over(st[b][:, 0, :], C), -1.0 / C, Y8(b), ALU.mult, ALU.add)\
                            .then_inc(e["cen"], 1)
                    for b in range(2):
                        dve.wait_ge(e["sq"], last_of(j, b))
                        v.tensor_reduce(out=st[b][:, 1, :], in_=groups(Q[b][:, :], 2 * CT), op=ALU.add, axis=AX)\
                            .then_inc(e["sumsq"], 1)
                    for b in range(2):
                        dve.wait_ge(e["dev"], last_of(j, b))
                        v.tensor_tensor(Y8(b), Y8(b), over(st[b][:, 2, :], C), ALU.mult).then_inc(e["norm"], 1)
                    for b in range(2):
                        dve.wait_ge(e["norm"], last_of(j, b))
                        v.tensor_tensor(groups(T[b][:, :], CT), Y8(b)[:, 0:CT, :],
                                        over(k.dinv[:, bass.ds((2 * j + b) * CT, CT)], C), ALU.mult)\
                            .then_inc(e["over"], 1)


def gcn1_stage(nc, k):
    with Stage(nc, "g1") as g:
        pairs = lambda name, shape, dt=F32: [g.sb(f"{name}{b}", shape, dt) for b in range(2)]
        idx = pairs("idx", [P, CT], I32)
        landing = pairs("landing", [P, CT * C])
        W = pairs("W", [P, CE])
        SF = pairs("SF", [C, CE])
        T = pairs("T", [P, CE])
        HS = pairs("HS", [P, CT * H])
        HD = pairs("HD", [P, CT * H])
        b1 = g.sb("b1", [1, CT, H])
        pA = [g.ps(f"pA{b}", [P, CE]) for b in range(2)]
        pS = [g.ps(f"pS{b}", [P, CT * H]) for b in range(2)]
        pD = [g.ps(f"pD{b}", [P, CT * H]) for b in range(2)]
        landed = g.pair("landed"); got = g.pair("got"); copied = g.pair("copied")
        own_in = g.pair("own_in"); rows_out = g.pair("rows_out")
        e = {n: g.sem(n) for n in ("staged", "passed", "starts", "turned", "flat", "summed", "product_s", "product_d",
                                   "relu_s", "scaled", "biased", "done_d")}
        sems = dict(staged=e["staged"], passed=e["passed"], landed=landed, got=got, copied=copied)
        with nc.Block() as block:

            @block.gpsimd
            def _(pool):
                override_rows(nc, pool, k, k.d3, C, idx, landing, sems, ITERS, pool.to_reg(EP - 1))

            @block.sync
            def _(sp):
                def load(j, used=True):
                    for b in range(2):
                        i = 2 * j + b
                        if used:
                            sp.wait_ge(copied[b], 16 * j)
                        sp.dma_start(groups(landing[b][:, :], CT), one(by_chunk(k.s3), i)).then_inc(landed[b], 16)
                    for b in range(2):
                        if used:
                            sp.wait_ge(e["turned"], last_of(j - 1, b))
                        sp.dma_start(ends(W[b])[:, :, 1, :], one(by_chunk(k.d3), 2 * j + b)).then_inc(own_in[b], 16)
                    for b in range(2):
                        sp.wait_ge(got[b], 16 * CT * j + 16 * CT)
                        sp.dma_start(ends(W[b])[:, :, 0, :], groups(landing[b][:, :], CT)).then_inc(copied[b], 16)

                def store(j):
                    for b in range(2):
                        sp.wait_ge(e["relu_s"], last_of(j, b))
                        sp.dma_start(one(by_chunk(k.s4), 2 * j + b), groups(HS[b][:, :], CT)).then_inc(rows_out[b], 16)
                    for b in range(2):
                        sp.wait_ge(e["done_d"], last_of(j, b))
                        sp.dma_start(one(by_chunk(k.d4), 2 * j + b), groups(HD[b][:, :], CT)).then_inc(rows_out[b], 16)

                load(0, used=False)
                with sp.Fori(0, ITERS - 1) as j:
                    load(j + 1)
                    store(j)
                store(ITERS - 1)
                for b in range(2):
                    sp.wait_ge(rows_out[b], 32 * ITERS)

            @block.tensor
            def _(pe):
                t = nc.tensor
                with pe.Fori(0, ITERS) as j:
                    for b in range(2):
                        pe.wait_ge(copied[b], 16 * j + 16)
                        pe.wait_ge(own_in[b], 16 * j + 16)
                        pe.wait_ge(e["summed"], 2 * j)
                        for n in range(CT):
                            i = t.transpose(pA[b][:, n * P:n * P + P], W[b][:, n * P:n * P + P], k.ident[:, :])
                        i.then_inc(e["turned"], 1)
                    for b in range(2):
                        pe.wait_ge(e["flat"], last_of(j, b))
                        pe.wait_ge(e["relu_s"], 2 * j)
                        pe.wait_ge(e["starts"], CT + 1)
                        t.matmul(pS[b][:, :], k.ones[0:1, :], b1[:, :, :].rearrange("a n c -> a (n c)"),
                                 start=True, stop=False, skip_group_check=True)
                        for n in range(CT):
                            i = t.matmul(pS[b][:, n * H:n * H + H], SF[b][:, n * P:n * P + P], k.w1[0:C, :],
                                         start=False, stop=n == CT - 1, skip_group_check=True)
                        i.then_inc(e["product_s"], 1)
                    for b in range(2):
                        pe.wait_ge(e["summed"], last_of(j, b))
                        pe.wait_ge(e["scaled"], 2 * j)
                        for n in range(CT):
                            i = t.matmul(pD[b][:, n * H:n * H + H], T[b][:, n * P:n * P + P], k.w1[:, :],
                                         start=True, stop=True)
                        i.then_inc(e["product_d"], 1)

            @block.scalar
            def _(act):
                s = nc.scalar
                with act.Fori(0, ITERS) as j:
                    for b in range(2):
                        act.wait_ge(e["turned"], last_of(j, b))
                        act.wait_ge(e["product_d"], 2 * j)
                        s.activation(SF[b][:, :], pA[b][0:C, :], ACT.Copy)
                        s.activation(T[b][C:P, :], pA[b][C:P, :], ACT.Copy).then_inc(e["flat"], 1)
                    for b in range(2):
                        act.wait_ge(e["product_s"], last_of(j, b))
                        act.wait_ge(rows_out[b], 32 * j)
                        s.activation(HS[b][:, :], pS[b][:, :], ACT.Relu).then_inc(e["relu_s"], 1)

            @block.vector
            def _(dve):
                v = nc.vector
                v.memset(T[1][0:C, :], 0.0).then_inc(e["starts"], 1)
                for n in range(CT):
                    v.tensor_copy(b1[:, n, :], k.b1row[0:1, :]).then_inc(e["starts"], 1)
                dve.wait_ge(e["starts"], CT + 1)
                with dve.Fori(0, ITERS) as j:
                    for b in range(2):
                        at = bass.ds((2 * j + b) * CE, CE)
                        dve.wait_ge(e["flat"], last_of(j, b))
                        v.tensor_tensor_scan(T[b][0:C, :], k.same[0:C, at], pA[b][0:C, :],
                                             T[1 - b][0:C, CE - 1:CE], ALU.mult, ALU.add).then_inc(e["summed"], 1)
                        dve.wait_ge(e["summed"], last_of(j, b))
                    dinv = lambda b: over(k.dinv[:, bass.ds((2 * j + b) * CT, CT)], H)
                    H4 = lambda b: groups(HD[b][:, :], CT)
                    for b in range(2):
                        dve.wait_ge(e["product_d"], last_of(j, b))
                        dve.wait_ge(rows_out[b], 32 * j)
                        v.tensor_tensor(H4(b), groups(pD[b][:, :], CT), dinv(b), ALU.mult).then_inc(e["scaled"], 1)
                    for b in range(2):
                        dve.wait_ge(e["scaled"], last_of(j, b))
                        v.tensor_tensor(H4(b), H4(b), k.b1row[:, :].unsqueeze(1).to_broadcast([P, CT, H]), ALU.add)\
                            .then_inc(e["biased"], 1)
                    for b in range(2):
                        dve.wait_ge(e["biased"], last_of(j, b))
                        v.scalar_tensor_tensor(H4(b), H4(b), 0.0, dinv(b), ALU.max, ALU.mult).then_inc(e["done_d"], 1)


def gcn2_stage(nc, k):
    with Stage(nc, "g2") as g:
        pairs = lambda name, shape, dt=F32: [g.sb(f"{name}{b}", shape, dt) for b in range(2)]
        idx = pairs("idx", [P, CT], I32)
        landing = pairs("landing", [P, CT * H])
        W = pairs("W", [P, CT * H])
        D = pairs("D", [P, CT * H])
        DR = pairs("DR", [P, CE])
        WF = pairs("WF", [P, CE])
        DF = pairs("DF", [P, CE])
        S = pairs("S", [P, CE])
        HS = pairs("HS", [P, CE])
        HD = pairs("HD", [P, CE])
        Z = pairs("Z", [P, 2 * CT * C])
        pA = [g.ps(f"pA{b}", [P, CE]) for b in range(2)]
        pB = [g.ps(f"pB{b}", [P, CE]) for b in range(2)]
        pS = [g.ps(f"pS{b}", [P, CE]) for b in range(2)]
        pD = [g.ps(f"pD{b}", [P, CE]) for b in range(2)]
        landed = g.pair("landed"); got = g.pair("got"); copied = g.pair("copied")
        own_in = g.pair("own_in"); rows_out = g.pair("rows_out")
        e = {n: g.sem(n) for n in ("staged", "passed", "starts", "turned_s", "turned_d", "flat_s", "flat_d", "summed",
                                   "product_s", "product_d", "relu_s", "scaled", "relu_d", "third", "z_s", "z_d")}
        sems = dict(staged=e["staged"], passed=e["passed"], landed=landed, got=got, copied=copied)
        with nc.Block() as block:

            @block.gpsimd
            def _(pool):
                override_rows(nc, pool, k, k.d4, H, idx, landing, sems, ITERS, pool.to_reg(EP - 1))

            @block.sync
            def _(sp):
                def load(j, used=True):
                    for b in range(2):
                        i = 2 * j + b
                        if used:
                            sp.wait_ge(copied[b], 16 * j)
                        sp.dma_start(groups(landing[b][:, :], CT), one(by_chunk(k.s4), i)).then_inc(landed[b], 16)
                    for b in range(2):
                        i = 2 * j + b
                        if used:
                            sp.wait_ge(e["scaled"], last_of(j - 1, b))
                            sp.wait_ge(e["turned_d"], last_of(j - 1, b))
                        sp.dma_start(groups(D[b][:, :], CT), one(by_chunk(k.d4), i)).then_inc(own_in[b], 16)
                        sp.dma_start(DR[b][:, :], row(k.dinv_row[bass.ds(i * CE, CE)], CE).to_broadcast([P, CE]))\
                            .then_inc(own_in[b], 16)
                    for b in range(2):
                        sp.wait_ge(got[b], 16 * CT * j + 16 * CT)
                        if used:
                            sp.wait_ge(e["turned_s"], last_of(j - 1, b))
                        sp.dma_start(W[b][:, :], landing[b][:, :]).then_inc(copied[b], 16)

                def store(j):
                    for b in range(2):
                        i = 2 * j + b
                        sp.wait_ge(e["z_s"], last_of(j, b))
                        sp.wait_ge(e["z_d"], last_of(j, b))
                        sp.dma_start(one(by_chunk(k.d5), i), groups(Z[b][:, 0:CT * C], CT)).then_inc(rows_out[b], 16)
                        sp.dma_start(one(by_chunk(k.s5), i), groups(Z[b][:, CT * C:], CT)).then_inc(rows_out[b], 16)

                load(0, used=False)
                with sp.Fori(0, ITERS - 1) as j:
                    load(j + 1)
                    store(j)
                store(ITERS - 1)
                for b in range(2):
                    sp.wait_ge(rows_out[b], 32 * ITERS)

            @block.tensor
            def _(pe):
                t = nc.tensor
                with pe.Fori(0, ITERS) as j:
                    for b in range(2):
                        pe.wait_ge(own_in[b], 32 * j + 32)
                        pe.wait_ge(e["flat_d"], 2 * j)
                        for n in range(CT):
                            i = t.transpose(pB[b][:, n * P:n * P + P], D[b][:, n * P:n * P + P], k.ident[:, :])
                        i.then_inc(e["turned_d"], 1)
                    for b in range(2):
                        pe.wait_ge(copied[b], 16 * j + 16)
                        pe.wait_ge(e["z_s"], 2 * j)
                        pe.wait_ge(e["z_d"], 2 * j)
                        for n in range(CT):
                            i = t.transpose(pA[b][:, n * P:n * P + P], W[b][:, n * P:n * P + P], k.ident[:, :])
                        i.then_inc(e["turned_s"], 1)
                    for b in range(2):
                        pe.wait_ge(e["flat_s"], last_of(j, b))
                        pe.wait_ge(e["relu_s"], 2 * j)
                        t.matmul(pS[b][:, :], k.w2[:, :], WF[b][:, :], start=True, stop=True)\
                            .then_inc(e["product_s"], 1)
                    for b in range(2):
                        pe.wait_ge(e["summed"], last_of(j, b))
                        pe.wait_ge(e["flat_d"], last_of(j, b))
                        pe.wait_ge(e["scaled"], 2 * j)
                        t.matmul(pD[b][:, :], k.w2[:, :], S[b][:, :], start=True, stop=False)
                        t.matmul(pD[b][:, :], k.w2[:, :], DF[b][:, :], start=False, stop=True)\
                            .then_inc(e["product_d"], 1)
                    for b in range(2):
                        pe.wait_ge(e["relu_s"], last_of(j, b))
                        pe.wait_ge(e["relu_d"], last_of(j, b))
                        for n in range(2 * CT):
                            h = HD[b] if n < CT else HS[b]
                            i = t.matmul(pA[b][:, n * C:n * C + C], h[:, n % CT * P:n % CT * P + P], k.w3[:, :],
                                         start=True, stop=True)
                        i.then_inc(e["third"], 1)

            @block.scalar
            def _(act):
                s = nc.scalar
                with act.Fori(0, ITERS) as j:
                    for b in range(2):
                        act.wait_ge(e["turned_d"], last_of(j, b))
                        act.wait_ge(e["product_d"], 2 * j)
                        s.activation(DF[b][:, :], pB[b][:, :], ACT.Copy).then_inc(e["flat_d"], 1)
                    for b in range(2):
                        act.wait_ge(e["turned_s"], last_of(j, b))
                        act.wait_ge(e["product_s"], 2 * j)
                        s.activation(WF[b][:, :], pA[b][:, :], ACT.Copy).then_inc(e["flat_s"], 1)
                    for b in range(2):
                        act.wait_ge(e["product_s"], last_of(j, b))
                        act.wait_ge(e["third"], 2 * j)
                        s.activation(HS[b][:, :], pS[b][:, :], ACT.Relu, bias=k.col[:, 5:6]).then_inc(e["relu_s"], 1)
                    for b in range(2):
                        act.wait_ge(e["scaled"], last_of(j, b))
                        s.activation(HD[b][:, :], HD[b][:, :], ACT.Relu, bias=k.col[:, 5:6]).then_inc(e["relu_d"], 1)
                    for b in range(2):
                        act.wait_ge(e["third"], last_of(j, b))
                        act.wait_ge(rows_out[b], 32 * j)
                        s.activation(Z[b][:, CT * C:], pA[b][:, CT * C:], ACT.Copy).then_inc(e["z_s"], 1)

            @block.vector
            def _(dve):
                v = nc.vector
                v.memset(S[1][:, :], 0.0).then_inc(e["starts"], 1)
                dve.wait_ge(e["starts"], 1)
                with dve.Fori(0, ITERS) as j:
                    for b in range(2):
                        at = bass.ds((2 * j + b) * CE, CE)
                        dve.wait_ge(e["flat_s"], last_of(j, b))
                        v.tensor_tensor_scan(S[b][:, :], k.same[:, at], pA[b][:, :], S[1 - b][:, CE - 1:CE],
                                             ALU.mult, ALU.add).then_inc(e["summed"], 1)
                        dve.wait_ge(e["summed"], last_of(j, b))
                    for b in range(2):
                        dve.wait_ge(e["product_d"], last_of(j, b))
                        v.tensor_tensor(HD[b][:, :], pD[b][:, :], DR[b][:, :], ALU.mult).then_inc(e["scaled"], 1)
                    for b in range(2):
                        dve.wait_ge(e["z_s"], last_of(j, b))
                        v.tensor_tensor(groups(Z[b][:, 0:CT * C], CT), groups(pA[b][:, 0:CT * C], CT),
                                        over(k.dinv[:, bass.ds((2 * j + b) * CT, CT)], C), ALU.mult)\
                            .then_inc(e["z_d"], 1)


def output_stage(nc, k, out):
    with Stage(nc, "ou") as g:
        pairs = lambda name, shape, dt=F32: [g.sb(f"{name}{b}", shape, dt) for b in range(2)]
        idx = pairs("idx", [P, CT], I32)
        put = pairs("put", [P, CT], I32)
        landing = pairs("landing", [P, CT * C])
        W = pairs("W", [P, CE])
        T = pairs("T", [P, CE])
        X3 = pairs("X3", [P, CT * C])
        O = pairs("O", [P, CT * C])
        Q = pairs("Q", [P, CT * C])
        F = pairs("F", [P, CT * C])
        st = pairs("st", [P, 4, CT])
        twice = g.sb("twice", [P, C])
        pA = [g.ps(f"pA{b}", [P, CE]) for b in range(2)]
        pO = [g.ps(f"pO{b}", [P, CT * C]) for b in range(2)]
        landed = g.pair("landed"); got = g.pair("got"); copied = g.pair("copied")
        own_in = g.pair("own_in"); scattered = g.pair("scattered")
        e = {n: g.sem(n) for n in ("staged", "passed", "starts", "turned", "flat", "summed", "totals", "scaled", "biased",
                                   "max", "less", "exp", "esum", "erec", "soft", "added", "sum", "cen", "sq", "sumsq",
                                   "ln", "dev", "norm", "put")}
        gp = nc.gpsimd
        with nc.Block() as block:

            @block.gpsimd
            def _(pool):
                in_tables, in_out = pool.to_reg(EP - 1), pool.to_reg(N - 1)

                def gather(j):
                    for b in range(2):
                        if not isinstance(j, int):
                            pool.wait_ge(copied[b], 16 * j)
                        gp.tensor_copy(idx[b][:, :], k.pos[:, bass.ds((2 * j + b) * CT, CT)])\
                            .then_inc(e["staged"], 1)
                    for b in range(2):
                        pool.wait_ge(e["staged"], last_of(j, b))
                        pool.wait_ge(landed[b], 16 * j + 16)
                        pool.sem_inc(e["passed"], 1)
                        for t in range(CT):
                            gp.indirect_dma_start(out=landing[b][:, t * C:(t + 1) * C], out_offset=None, in_=k.d5,
                                                  in_offset=bass.IndirectOffsetOnAxis(ap=idx[b][:, t:t + 1], axis=0),
                                                  bounds_check=in_tables, oob_is_err=False).then_inc(got[b], 16)

                def scatter(j):
                    for b in range(2):
                        pool.wait_ge(scattered[b], 16 * CT * j)
                        gp.tensor_copy(put[b][:, :], k.put[:, bass.ds((2 * j + b) * CT, CT)]).then_inc(e["put"], 1)
                    for b in range(2):
                        pool.wait_ge(e["put"], last_of(j, b))
                        pool.wait_ge(e["norm"], last_of(j, b))
                        pool.sem_inc(e["passed"], 1)
                        for t in range(CT):
                            gp.indirect_dma_start(out=out, out_offset=bass.IndirectOffsetOnAxis(
                                ap=put[b][:, t:t + 1], axis=0), in_=F[b][:, t * C:(t + 1) * C], in_offset=None,
                                bounds_check=in_out, oob_is_err=False).then_inc(scattered[b], 16)

                gather(0)
                with pool.Fori(0, ITERS - 1) as j:
                    gather(j + 1)
                    scatter(j)
                scatter(ITERS - 1)
                for b in range(2):
                    pool.wait_ge(scattered[b], 16 * CT * ITERS)

            @block.sync
            def _(sp):
                def load(j, used=True):
                    for b in range(2):
                        if used:
                            sp.wait_ge(copied[b], 16 * j)
                        sp.dma_start(groups(landing[b][:, :], CT), one(by_chunk(k.s5), 2 * j + b))\
                            .then_inc(landed[b], 16)
                    for b in range(2):
                        i = 2 * j + b
                        if used:
                            sp.wait_ge(e["turned"], last_of(j - 1, b))
                        sp.dma_start(ends(W[b])[:, :, 1, :], one(by_chunk(k.d5), i)).then_inc(own_in[b], 16)
                        if used:
                            sp.wait_ge(e["added"], last_of(j - 1, b))
                        sp.dma_start(groups(X3[b][:, :], CT), one(by_chunk(k.x3), i)).then_inc(own_in[b], 16)
                    for b in range(2):
                        sp.wait_ge(got[b], 16 * CT * j + 16 * CT)
                        sp.dma_start(ends(W[b])[:, :, 0, :], groups(landing[b][:, :], CT)).then_inc(copied[b], 16)

                load(0, used=False)
                with sp.Fori(1, ITERS) as j:
                    load(j)

            @block.tensor
            def _(pe):
                t = nc.tensor
                with pe.Fori(0, ITERS) as j:
                    for b in range(2):
                        pe.wait_ge(copied[b], 16 * j + 16)
                        pe.wait_ge(own_in[b], 32 * j + 32)
                        pe.wait_ge(e["summed"], 2 * j)
                        for n in range(CT):
                            i = t.transpose(pA[b][:, n * P:n * P + P], W[b][:, n * P:n * P + P], k.ident[:, :])
                        i.then_inc(e["turned"], 1)
                    for b in range(2):
                        pe.wait_ge(e["summed"], last_of(j, b))
                        pe.wait_ge(e["starts"], 3)
                        pe.wait_ge(e["scaled"], 2 * j)
                        for n in range(CT):
                            i = t.matmul(pO[b][:, n * C:n * C + C], T[b][:, n * P:n * P + P], twice[:, :],
                                         start=True, stop=True)
                        i.then_inc(e["totals"], 1)

            @block.scalar
            def _(act):
                s = nc.scalar
                s.preload_act_table_set(LN_EXP)
                with act.Fori(0, ITERS) as j:
                    for b in range(2):
                        act.wait_ge(e["turned"], last_of(j, b))
                        act.wait_ge(e["totals"], 2 * j)
                        s.activation(T[b][C:P, :], pA[b][C:P, :], ACT.Copy).then_inc(e["flat"], 1)
                    for b in range(2):
                        act.wait_ge(e["less"], last_of(j, b))
                        s.activation(O[b][:, :], O[b][:, :], ACT.Exp).then_inc(e["exp"], 1)
                    for b in range(2):
                        act.wait_ge(e["cen"], last_of(j, b))
                        act.wait_ge(e["sumsq"], 2 * j)
                        s.activation(Q[b][:, :], O[b][:, :], ACT.Square).then_inc(e["sq"], 1)
                    for b in range(2):
                        act.wait_ge(e["sumsq"], last_of(j, b))
                        s.activation(st[b][:, 2, :], st[b][:, 2, :], ACT.Ln, scale=1.0 / C, bias=k.eps[:, 0:1])\
                            .then_inc(e["ln"], 1)
                    for b in range(2):
                        act.wait_ge(e["ln"], last_of(j, b))
                        s.activation(st[b][:, 3, :], st[b][:, 2, :], ACT.Exp, scale=-0.5).then_inc(e["dev"], 1)

            @block.vector
            def _(dve):
                v = nc.vector
                O4 = lambda b: groups(O[b][:, :], CT)
                v.memset(T[1][0:C, :], 0.0).then_inc(e["starts"], 1)
                v.tensor_copy(twice[0:C, :], k.ident[0:C, 0:C]).then_inc(e["starts"], 1)
                v.tensor_copy(twice[C:P, :], k.ident[C:P, C:P]).then_inc(e["starts"], 1)
                dve.wait_ge(e["starts"], 3)
                with dve.Fori(0, ITERS) as j:
                    for b in range(2):
                        at = bass.ds((2 * j + b) * CE, CE)
                        dve.wait_ge(e["flat"], last_of(j, b))
                        v.tensor_tensor_scan(T[b][0:C, :], k.same[0:C, at], pA[b][0:C, :],
                                             T[1 - b][0:C, CE - 1:CE], ALU.mult, ALU.add).then_inc(e["summed"], 1)
                        dve.wait_ge(e["summed"], last_of(j, b))
                    for b in range(2):
                        dve.wait_ge(e["totals"], last_of(j, b))
                        v.tensor_tensor(O4(b), groups(pO[b][:, :], CT),
                                        over(k.dinv[:, bass.ds((2 * j + b) * CT, CT)], C), ALU.mult)\
                            .then_inc(e["scaled"], 1)
                    for b in range(2):
                        dve.wait_ge(e["scaled"], last_of(j, b))
                        v.tensor_tensor(O4(b), O4(b), k.b3[:, :].unsqueeze(1).to_broadcast([P, CT, C]), ALU.add)\
                            .then_inc(e["biased"], 1)
                    for b in range(2):
                        dve.wait_ge(e["biased"], last_of(j, b))
                        v.tensor_reduce(out=st[b][:, 0, :], in_=O4(b), op=ALU.max, axis=AX).then_inc(e["max"], 1)
                    for b in range(2):
                        dve.wait_ge(e["max"], last_of(j, b))
                        v.tensor_tensor(O4(b), O4(b), over(st[b][:, 0, :], C), ALU.subtract).then_inc(e["less"], 1)
                    for b in range(2):
                        dve.wait_ge(e["exp"], last_of(j, b))
                        v.tensor_reduce(out=st[b][:, 1, :], in_=O4(b), op=ALU.add, axis=AX).then_inc(e["esum"], 1)
                    for b in range(2):
                        dve.wait_ge(e["esum"], last_of(j, b))
                        v.reciprocal(st[b][:, 0, :], st[b][:, 1, :]).then_inc(e["erec"], 1)
                    for b in range(2):
                        dve.wait_ge(e["erec"], last_of(j, b))
                        v.tensor_tensor(O4(b), O4(b), over(st[b][:, 0, :], C), ALU.mult).then_inc(e["soft"], 1)
                    for b in range(2):
                        dve.wait_ge(e["soft"], last_of(j, b))
                        v.tensor_tensor(O4(b), O4(b), groups(X3[b][:, :], CT), ALU.add).then_inc(e["added"], 1)
                    for b in range(2):
                        dve.wait_ge(e["added"], last_of(j, b))
                        v.tensor_reduce(out=st[b][:, 1, :], in_=O4(b), op=ALU.add, axis=AX).then_inc(e["sum"], 1)
                    for b in range(2):
                        dve.wait_ge(e["sum"], last_of(j, b))
                        v.scalar_tensor_tensor(O4(b), over(st[b][:, 1, :], C), -1.0 / C, O4(b), ALU.mult, ALU.add)\
                            .then_inc(e["cen"], 1)
                    for b in range(2):
                        dve.wait_ge(e["sq"], last_of(j, b))
                        v.tensor_reduce(out=st[b][:, 2, :], in_=groups(Q[b][:, :], CT), op=ALU.add, axis=AX)\
                            .then_inc(e["sumsq"], 1)
                    for b in range(2):
                        dve.wait_ge(e["dev"], last_of(j, b))
                        dve.wait_ge(scattered[b], 16 * CT * j)
                        v.tensor_tensor(groups(F[b][:, :], CT), O4(b), over(st[b][:, 3, :], C), ALU.mult)\
                            .then_inc(e["norm"], 1)


def dense_stage(nc, k, out):
    with Stage(nc, "de") as g:
        pairs = lambda name, shape, dt=F32: [g.sb(f"{name}{b}", shape, dt) for b in range(2)]
        G, F = NODE_ROWS, NODE_ROWS * C
        X = pairs("X", [P, F])
        XF = pairs("XF", [P, F])
        U = pairs("U", [P, F])
        Q = pairs("Q", [P, F])
        UF = pairs("UF", [P, F])
        H1 = pairs("H1", [P, 2, F])
        H2 = pairs("H2", [P, 2, F])
        O = pairs("O", [P, F])
        st = pairs("st", [P, 9, G])
        pX = [g.ps(f"pX{b}", [P, F]) for b in range(2)]
        pU = [g.ps(f"pU{b}", [P, F]) for b in range(2)]
        pH = [[g.ps(f"pH{b}{h}", [P, F]) for h in range(2)] for b in range(2)]
        x_in = g.pair("x_in"); o_out = g.pair("o_out")
        e = {n: g.sem(n) for n in (
            "turned", "flat", "product", "relu", "sq", "sumsq", "clamped", "ln", "inv", "scaled", "added", "sum", "cen",
            "sq2", "sumsq2", "ln2", "dev", "norm", "turned3", "flat3", "first0", "first1", "hid0", "hid1", "second0",
            "second1", "deep0", "deep1", "third", "max", "less", "exp", "esum", "erec", "soft", "mixed", "sum4", "cen4",
            "sq4", "sumsq4", "ln4", "dev4", "norm4")}
        trips = D_FULL // 2
        with nc.Block() as block:

            @block.sync
            def _(sp):
                def load(j, b, parts, used=True):
                    if used:
                        sp.wait_ge(e["added"], last_of(j - 1, b))
                    sp.dma_start(X[b][0:parts, :], node_rows(k.x1, 2 * j + b, parts)).then_inc(x_in[b], 16)

                def store(j, b, parts):
                    sp.wait_ge(e["norm4"], last_of(j, b))
                    sp.dma_start(node_rows(out, 2 * j + b, parts), O[b][0:parts, :]).then_inc(o_out[b], 16)

                load(0, 0, P, used=False)
                load(0, 1, P, used=False)
                with sp.Fori(0, trips - 1) as j:
                    for b in range(2):
                        load(j + 1, b, P)
                    for b in range(2):
                        store(j, b, P)
                for b in range(2):
                    load(trips, b, (P, D_REST)[b])
                for b in range(2):
                    store(trips - 1, b, P)
                for b in range(2):
                    store(trips, b, (P, D_REST)[b])
                for b in range(2):
                    sp.wait_ge(o_out[b], 16 * (trips + 1))

            @block.tensor
            def _(pe):
                t = nc.tensor

                def trip(j, sizes):
                    for b in range(2):
                        p = sizes[b]
                        pe.wait_ge(x_in[b], 16 * j + 16)
                        pe.wait_ge(e["flat"], 2 * j)
                        pe.wait_ge(e["less"], 2 * j)
                        for n in range(G // 2):
                            i = t.transpose(pX[b][:, n * P:n * P + p], X[b][0:p, n * P:n * P + P], k.ident[0:p, 0:p])
                        i.then_inc(e["turned"], 1)
                    for b in range(2):
                        p = sizes[b]
                        pe.wait_ge(e["flat"], last_of(j, b))
                        t.matmul(pU[b][0:p, :], k.ones[0:1, 0:p], k.shift[:, :, :].rearrange("a n c -> a (n c)"),
                                 start=True, stop=False, skip_group_check=True)
                        for n in range(G // 2):
                            i = t.matmul(pU[b][0:p, n * P:n * P + P], XF[b][:, n * P:n * P + p], k.wbn_r[:, :],
                                         start=False, stop=n == G // 2 - 1, skip_group_check=True)
                        i.then_inc(e["product"], 1)
                    for b in range(2):
                        p = sizes[b]
                        pe.wait_ge(e["norm"], last_of(j, b))
                        for n in range(G // 2):
                            i = t.transpose(pU[b][:, n * P:n * P + p], U[b][0:p, n * P:n * P + P], k.ident[0:p, 0:p])
                        i.then_inc(e["turned3"], 1)
                    for b in range(2):
                        pe.wait_ge(e["flat3"], last_of(j, b))
                        for h in range(2):
                            rows = slice(h * C, h * C + C)
                            t.matmul(pH[b][h][:, :], k.w1[rows, :], UF[b][rows, :], start=True, stop=True)\
                                .then_inc(e[f"first{h}"], 1)
                    for b in range(2):
                        for h in range(2):
                            pe.wait_ge(e[f"hid{h}"], last_of(j, b))
                            t.matmul(pH[b][h][:, :], k.w2[:, :], H1[b][:, h, :], start=True, stop=True)\
                                .then_inc(e[f"second{h}"], 1)
                    for b in range(2):
                        p = sizes[b]
                        t.matmul(pX[b][0:p, :], k.ones[0:1, 0:p], k.b3row[:, :, :].rearrange("a n c -> a (n c)"),
                                 start=True, stop=False, skip_group_check=True)
                        for h in range(2):
                            pe.wait_ge(e[f"deep{h}"], last_of(j, b))
                            for n in range(G // 2):
                                at = (2 * n + h) * C
                                i = t.matmul(pX[b][0:p, at:at + C], H2[b][:, h, n * P:n * P + p], k.w3[:, :],
                                             start=False, stop=h == 1 and n == G // 2 - 1, skip_group_check=True)
                        i.then_inc(e["third"], 1)

                with pe.Fori(0, trips) as j:
                    trip(j, (P, P))
                trip(trips, (P, D_REST))

            @block.scalar
            def _(act):
                s = nc.scalar
                s.preload_act_table_set(LN_EXP)

                def trip(j, sizes):
                    both = [(b, slice(0, sizes[b])) for b in range(2)]
                    for b, p in both:
                        act.wait_ge(e["turned"], last_of(j, b))
                        act.wait_ge(e["product"], 2 * j)
                        s.activation(XF[b][:, :], pX[b][:, :], ACT.Copy).then_inc(e["flat"], 1)
                    for b, p in both:
                        act.wait_ge(e["product"], last_of(j, b))
                        act.wait_ge(e["mixed"], 2 * j)
                        s.activation(U[b][p, :], pU[b][p, :], ACT.Relu).then_inc(e["relu"], 1)
                    for b, p in both:
                        act.wait_ge(e["relu"], last_of(j, b))
                        act.wait_ge(e["sumsq4"], 2 * j)
                        s.activation(Q[b][p, :], U[b][p, :], ACT.Square).then_inc(e["sq"], 1)
                    for b, p in both:
                        act.wait_ge(e["clamped"], last_of(j, b))
                        s.activation(st[b][p, 1, :], st[b][p, 0, :], ACT.Ln, scale=2.0 ** 20).then_inc(e["ln"], 1)
                    for b, p in both:
                        act.wait_ge(e["ln"], last_of(j, b))
                        s.activation(st[b][p, 1, :], st[b][p, 1, :], ACT.Exp, scale=-0.5, bias=k.eps[p, 2:3])\
                            .then_inc(e["inv"], 1)
                    for b, p in both:
                        act.wait_ge(e["cen"], last_of(j, b))
                        s.activation(Q[b][p, :], U[b][p, :], ACT.Square).then_inc(e["sq2"], 1)
                    for b, p in both:
                        act.wait_ge(e["sumsq2"], last_of(j, b))
                        s.activation(st[b][p, 3, :], st[b][p, 3, :], ACT.Ln, scale=(1.0 + EPS) / C,
                                     bias=k.eps[p, 1:2]).then_inc(e["ln2"], 1)
                    for b, p in both:
                        act.wait_ge(e["ln2"], last_of(j, b))
                        s.activation(st[b][p, 4, :], st[b][p, 3, :], ACT.Exp, scale=-0.5).then_inc(e["dev"], 1)
                    for b, p in both:
                        act.wait_ge(e["turned3"], last_of(j, b))
                        act.wait_ge(e["first1"], 2 * j)
                        s.activation(UF[b][:, :], pU[b][:, :], ACT.Copy).then_inc(e["flat3"], 1)
                    for b, p in both:
                        act.wait_ge(e["first0"], last_of(j, b))
                        act.wait_ge(e["second0"], 2 * j)
                        s.activation(H1[b][:, 0, :], pH[b][0][:, :], ACT.Relu, bias=k.col[:, 4:5])\
                            .then_inc(e["hid0"], 1)
                    for b, p in both:
                        act.wait_ge(e["second0"], last_of(j, b))
                        act.wait_ge(e["third"], 2 * j)
                        s.activation(H2[b][:, 0, :], pH[b][0][:, :], ACT.Relu, bias=k.col[:, 5:6])\
                            .then_inc(e["deep0"], 1)
                    for b, p in both:
                        act.wait_ge(e["less"], last_of(j, b))
                        s.activation(O[b][p, :], O[b][p, :], ACT.Exp).then_inc(e["exp"], 1)
                    for b, p in both:
                        act.wait_ge(e["cen4"], last_of(j, b))
                        s.activation(Q[b][p, :], O[b][p, :], ACT.Square).then_inc(e["sq4"], 1)
                    for b, p in both:
                        act.wait_ge(e["sumsq4"], last_of(j, b))
                        s.activation(st[b][p, 7, :], st[b][p, 7, :], ACT.Ln, scale=1.0 / C, bias=k.eps[p, 0:1])\
                            .then_inc(e["ln4"], 1)
                    for b, p in both:
                        act.wait_ge(e["ln4"], last_of(j, b))
                        s.activation(st[b][p, 8, :], st[b][p, 7, :], ACT.Exp, scale=-0.5).then_inc(e["dev4"], 1)

                with act.Fori(0, trips) as j:
                    trip(j, (P, P))
                trip(trips, (P, D_REST))

            @block.vector
            def _(dve):
                v = nc.vector

                def trip(j, sizes):
                    both = [(b, slice(0, sizes[b])) for b in range(2)]
                    g8 = lambda t, b: groups(t[b][0:sizes[b], :], G)
                    for b, p in both:
                        dve.wait_ge(e["sq"], last_of(j, b))
                        v.tensor_reduce(out=st[b][p, 0, :], in_=g8(Q, b), op=ALU.add, axis=AX).then_inc(e["sumsq"], 1)
                    for b, p in both:
                        dve.wait_ge(e["sumsq"], last_of(j, b))
                        v.tensor_scalar(st[b][p, 0, :], st[b][p, 0, :], 1e-24, None, ALU.max)\
                            .then_inc(e["clamped"], 1)
                    for b, p in both:
                        dve.wait_ge(e["inv"], last_of(j, b))
                        v.tensor_tensor(g8(U, b), g8(U, b), over(st[b][p, 1, :], C), ALU.mult).then_inc(e["scaled"], 1)
                    for b, p in both:
                        dve.wait_ge(e["scaled"], last_of(j, b))
                        v.tensor_tensor(U[b][p, :], U[b][p, :], X[b][p, :], ALU.add).then_inc(e["added"], 1)
                    for b, p in both:
                        dve.wait_ge(e["added"], last_of(j, b))
                        v.tensor_reduce(out=st[b][p, 2, :], in_=g8(U, b), op=ALU.add, axis=AX).then_inc(e["sum"], 1)
                    for b, p in both:
                        dve.wait_ge(e["sum"], last_of(j, b))
                        v.scalar_tensor_tensor(g8(U, b), over(st[b][p, 2, :], C), -1.0 / C, g8(U, b), ALU.mult, ALU.add)\
                            .then_inc(e["cen"], 1)
                    for b, p in both:
                        dve.wait_ge(e["sq2"], last_of(j, b))
                        v.tensor_reduce(out=st[b][p, 3, :], in_=g8(Q, b), op=ALU.add, axis=AX).then_inc(e["sumsq2"], 1)
                    for b, p in both:
                        dve.wait_ge(e["dev"], last_of(j, b))
                        v.tensor_tensor(g8(U, b), g8(U, b), over(st[b][p, 4, :], C), ALU.mult).then_inc(e["norm"], 1)
                    for b, p in both:
                        dve.wait_ge(e["first1"], last_of(j, b))
                        dve.wait_ge(e["second1"], 2 * j)
                        v.tensor_scalar(H1[b][:, 1, :], pH[b][1][:, :], k.col[:, 4:5], 0.0, ALU.add, ALU.max)\
                            .then_inc(e["hid1"], 1)
                    for b, p in both:
                        dve.wait_ge(e["second1"], last_of(j, b))
                        dve.wait_ge(e["third"], 2 * j)
                        v.tensor_scalar(H2[b][:, 1, :], pH[b][1][:, :], k.col[:, 5:6], 0.0, ALU.add, ALU.max)\
                            .then_inc(e["deep1"], 1)
                    for b, p in both:
                        dve.wait_ge(e["third"], last_of(j, b))
                        v.tensor_reduce(out=st[b][p, 5, :], in_=g8(pX, b), op=ALU.max, axis=AX).then_inc(e["max"], 1)
                    for b, p in both:
                        dve.wait_ge(e["max"], last_of(j, b))
                        dve.wait_ge(o_out[b], 16 * j)
                        v.tensor_tensor(g8(O, b), g8(pX, b), over(st[b][p, 5, :], C), ALU.subtract)\
                            .then_inc(e["less"], 1)
                    for b, p in both:
                        dve.wait_ge(e["exp"], last_of(j, b))
                        v.tensor_reduce(out=st[b][p, 6, :], in_=g8(O, b), op=ALU.add, axis=AX).then_inc(e["esum"], 1)
                    for b, p in both:
                        dve.wait_ge(e["esum"], last_of(j, b))
                        v.reciprocal(st[b][p, 5, :], st[b][p, 6, :]).then_inc(e["erec"], 1)
                    for b, p in both:
                        dve.wait_ge(e["erec"], last_of(j, b))
                        v.tensor_tensor(g8(O, b), g8(O, b), over(st[b][p, 5, :], C), ALU.mult).then_inc(e["soft"], 1)
                    for b, p in both:
                        dve.wait_ge(e["soft"], last_of(j, b))
                        v.tensor_tensor(O[b][p, :], O[b][p, :], U[b][p, :], ALU.add).then_inc(e["mixed"], 1)
                    for b, p in both:
                        dve.wait_ge(e["mixed"], last_of(j, b))
                        v.tensor_reduce(out=st[b][p, 6, :], in_=g8(O, b), op=ALU.add, axis=AX).then_inc(e["sum4"], 1)
                    for b, p in both:
                        dve.wait_ge(e["sum4"], last_of(j, b))
                        v.scalar_tensor_tensor(g8(O, b), over(st[b][p, 6, :], C), -1.0 / C, g8(O, b), ALU.mult, ALU.add)\
                            .then_inc(e["cen4"], 1)
                    for b, p in both:
                        dve.wait_ge(e["sq4"], last_of(j, b))
                        v.tensor_reduce(out=st[b][p, 7, :], in_=g8(Q, b), op=ALU.add, axis=AX).then_inc(e["sumsq4"], 1)
                    for b, p in both:
                        dve.wait_ge(e["dev4"], last_of(j, b))
                        v.tensor_tensor(g8(O, b), g8(O, b), over(st[b][p, 8, :], C), ALU.mult).then_inc(e["norm4"], 1)

                with dve.Fori(0, trips) as j:
                    trip(j, (P, P))
                trip(trips, (P, D_REST))


_RAW = ["x", "edge_attr_3"] + ["L0_gnn_" + n for n in "Wd1 bd1 g1 b1 Wd2 bd2 g2 b2 W1 W2 W3".split()] + \
    ["L1_gnn_" + n for n in "W_l W_r b gamma beta".split()] + ["L2_gnn_W", "L2_gnn_b"] + \
    ["L3_gnn_b1", "L3_gnn_b2", "L3_gnn_b3"]


def kernel(**inputs):
    import numpy as np
    import concourse.bacc as bacc
    from concourse.bass_utils import run_bass_kernel_spmd

    given = {n: np.asarray(v) for n, v in inputs.items()}
    arrays = {n: given[n] for n in _RAW if n != "edge_attr_3"}
    pad = EP - E
    arrays["srcp"] = np.concatenate([given["src"], np.zeros(pad, np.int32)])
    arrays["dstp"] = np.concatenate([np.full(1, -1, np.int32), given["dst"], np.full(pad, N, np.int32),
                                     np.full(1, N + 1, np.int32)])
    arrays["attrT"] = np.pad(given["edge_attr_3"].T, ((0, 0), (0, pad)))
    for n in (1, 2, 3):
        arrays[f"W{n}T"] = given[f"L3_gnn_W{n}"].T
    nc = bacc.Bacc("TRN2", target_bir_lowering=False, num_devices=1)
    aps = {}
    for n, v in arrays.items():
        arrays[n] = v = np.ascontiguousarray(v)
        aps[n] = nc.dram_tensor("in_" + n, v.shape, mybir.dt.from_np(v.dtype), kind="ExternalInput").ap()
    out = nc.dram_tensor("out", (N, C), F32, kind="ExternalOutput").ap()
    build(nc, aps, out)
    r = run_bass_kernel_spmd(nc, [{"in_" + n: v for n, v in arrays.items()}], core_ids=[0])
    return r.results[0]["out"]
```

```python
import math

import concourse.bass as bass
from concourse import mybir
from contextlib import ExitStack

F32 = mybir.dt.float32
I32 = mybir.dt.int32
BF16 = mybir.dt.bfloat16
ALU = mybir.AluOpType
ACT = mybir.ActivationFunctionType
AX = mybir.AxisListType.X

N = 100000
E = 25000
C = 64
H = 128
P = 128
CT = 4
CE = CT * P
ITERS = -(-E // (2 * CE))
EP = ITERS * 2 * CE
NT = EP // P
ST = 10
NODE_ROWS = 8
DN = P * NODE_ROWS
D_FULL = N // DN
D_REST = (N - D_FULL * DN) // NODE_ROWS
D_ITERS = D_FULL // 2
NONE = 1 << 20
EPS = 1e-5
BIG = 1e30
GELU = "gelu_and_others"
LN_EXP = "natural_log_exp_and_others"


class Plan:

    def __init__(self, nc, ctx):
        self.nc, self.ctx = nc, ctx

    def sb(self, name, shape, dt=F32):
        return self.ctx.enter_context(self.nc.sbuf_tensor(name, shape, dt))

    def dram(self, name, shape, dt=F32):
        return self.nc.dram_tensor(name, shape, dt, kind="Internal").ap()


class Stage:

    def __init__(self, nc, name):
        self.nc, self.name, self.sems = nc, name, []
        self.ctx = ExitStack()

    def __enter__(self):
        self.ctx.__enter__()
        return self

    def sb(self, name, shape, dt=F32):
        return self.ctx.enter_context(self.nc.sbuf_tensor(f"{self.name}_{name}", shape, dt))

    def ps(self, name, shape, dt=F32):
        return self.ctx.enter_context(self.nc.psum_tensor(f"{self.name}_{name}", shape, dt))

    def sem(self, name):
        s = self.nc.alloc_semaphore(f"{self.name}_{name}")
        self.sems.append(s)
        return s

    def pair(self, name):
        return [self.sem(f"{name}0"), self.sem(f"{name}1")]

    def __exit__(self, *a):
        self.ctx.__exit__(*a)
        if a[0] is None:
            self.nc.clear_and_free_semaphores(self.sems)
            self.nc.all_engine_barrier()
        return False


def groups(ap, n):
    return ap.rearrange("p (n f) -> p n f", n=n)


def over(ap, f):
    return ap.unsqueeze(2).to_broadcast([ap.shape[0], ap.shape[1], f])


def row(ap, n):
    return ap.rearrange("(a n) -> a n", a=1)


def build(nc, a, out):
    ctx = ExitStack()
    with ctx:
        k = Plan(nc, ctx)
        k.ident = k.sb("ident", [P, P])
        k.ones = k.sb("ones", [P, H])
        k.same = k.sb("same", [P, EP], BF16)
        k.last = k.sb("last", [P, NT])
        k.src = k.sb("src", [P, NT], I32)
        k.dst = k.sb("dst", [P, NT], I32)
        k.put = k.sb("put", [P, NT], I32)
        k.pos = k.sb("pos", [P, NT], I32)
        k.lastq = k.sb("lastq", [NT // 2, 2 * P])
        k.dinv = k.sb("dinv", [P, NT])
        k.eps = k.sb("eps", [P, 4])
        k.w_logit = k.sb("w_logit", [P, P])
        k.w_value = k.sb("w_value", [P, P])
        k.wd1 = k.sb("wd1", [4, C])
        k.wd2 = k.sb("wd2", [P, P])
        k.bd2 = k.sb("bd2", [1, CT, C])
        k.col = k.sb("col", [P, 8])
        k.wcat = k.sb("wcat", [P, C])
        k.wbn = k.sb("wbn", [P, C])
        k.wbn_r = k.sb("wbn_r", [P, P])
        k.bnrow = k.sb("bnrow", [1, 3, C])
        k.shift = k.sb("shift", [1, NODE_ROWS, C])
        k.w_att_s = k.sb("w_att_s", [P, P])
        k.w_att_d = k.sb("w_att_d", [P, C])
        k.b_att = k.sb("b_att", [P, 1])
        k.w1 = k.sb("w1", [P, H])
        k.w2 = k.sb("w2", [P, H])
        k.w3 = k.sb("w3", [P, C])
        k.b1row = k.sb("b1row", [P, H])
        k.b3 = k.sb("b3", [P, C])
        k.gram = k.sb("gram", [P, P + 1])
        k.where = k.dram("where", (N, 1), I32)
        k.mlp = k.dram("mlp", (C, EP))
        k.x1 = k.dram("x1", (N, C))
        k.s1 = k.dram("s1", (EP, C)); k.d1 = k.dram("d1", (EP, C))
        k.agg = k.dram("agg", (EP, C))
        k.s2 = k.dram("s2", (EP, C)); k.d2 = k.dram("d2", (EP, C))
        k.att_d = k.dram("att_d", (EP,))
        k.dinv_row = k.dram("dinv_row", (EP,))
        k.s3 = k.dram("s3", (EP, C)); k.d3 = k.dram("d3", (EP, C)); k.x3 = k.dram("x3", (EP, C))
        k.s4 = k.dram("s4", (EP, H)); k.d4 = k.dram("d4", (EP, H))
        k.s5 = k.dram("s5", (EP, C)); k.d5 = k.dram("d5", (EP, C))

        index_stage(nc, k, a)
        mlp_and_gram_stage(nc, k, a)
        attention_stage(nc, k, a)
        mean_stage(nc, k)
        batch_norm_stage(nc, k)
        update_stage(nc, k)
        dense_stage(nc, k, out)
        attention2_stage(nc, k)
        gcn1_stage(nc, k)
        gcn2_stage(nc, k)
        output_stage(nc, k, out)


def by_chunk(ap):
    return ap.rearrange("(i t p) f -> i p t f", t=CT, p=P)


def one(ap, i):
    v = ap[bass.ds(i, 1)]
    return v.rearrange("a p t f -> (a p) t f")


def index_stage(nc, k, a):
    Q = NT // 2
    with Stage(nc, "ix") as g:
        ends = g.sb("ends", [Q, 3, 2 * P], I32)
        endf = g.sb("endf", [Q, 4, 2 * P])
        none = g.sb("none", [80, N // 80], I32)
        wcol = g.sb("wcol", [P, 1])
        win = [g.sb(f"win{b}", [P, CE + 1], I32) for b in range(2)]
        pT = [g.ps(f"pT{h}", [P, 2, 2, Q]) for h in range(2)]
        loaded = g.sem("loaded"); ends_in = g.sem("ends_in"); none_in = g.sem("none_in")
        consts = g.sem("consts"); wsteps = g.sem("wsteps"); esteps = g.sem("esteps"); turned = g.sem("turned")
        tables = g.sem("tables"); win_in = g.pair("win_in"); win_used = g.pair("win_used")
        filled = g.sem("filled"); zeros = g.sem("zeros")
        dstp = a["dstp"]
        with nc.Block() as block:
            n_loads = []

            @block.sync
            def _(sp):
                def load(dst, src):
                    sp.dma_start(dst, src).then_inc(loaded, 16)
                    n_loads.append(1)
                for n, v in enumerate((dstp[1:EP + 1], dstp[2:EP + 2], a["srcp"])):
                    sp.dma_start(ends[:, n, :], v.rearrange("(q e) -> q e", e=2 * P)).then_inc(ends_in, 16)
                sp.wait_ge(zeros, 1)
                for h in range(2):
                    rows = slice(C * h, C * h + C)
                    load(k.w_logit[0:C, rows], a["L0_gnn_W2"])
                    load(k.w_logit[C:P, rows], a["L0_gnn_W1"])
                    for n, name in enumerate(("g1", "b1", "g2", "b2")):
                        load(k.col[rows, n:n + 1], a["L0_gnn_" + name].rearrange("(n a) -> n a", a=1))
                    load(k.w1[rows, :], a["W1T"])
                    load(k.col[rows, 6:7], a["L3_gnn_b3"].rearrange("(n a) -> n a", a=1))
                    load(k.wd2[rows, rows], a["L0_gnn_Wd2"])
                load(k.w_value[0:C, C:P], a["L0_gnn_W3"])
                load(k.wd1[0:3, :], a["L0_gnn_Wd1"])
                load(k.wd1[3:4, :], row(a["L0_gnn_bd1"], C))
                for n in range(CT):
                    load(k.bd2[:, n, :], row(a["L0_gnn_bd2"], C))
                load(k.wcat[0:C, :], a["L1_gnn_W_r"])
                load(k.wcat[C:P, :], a["L1_gnn_W_l"])
                for n, name in enumerate(("b", "gamma", "beta")):
                    load(k.bnrow[:, n, :], row(a["L1_gnn_" + name], C))
                load(wcol[C:P, :], a["L2_gnn_W"][:, 0:C].rearrange("a n -> n a"))
                load(k.w_att_d[:, :], a["L2_gnn_W"][:, C:P].to_broadcast([P, C]))
                load(k.b_att[:, :], row(a["L2_gnn_b"], 1).to_broadcast([P, 1]))
                load(k.col[:, 4:5], a["L3_gnn_b1"].rearrange("(n a) -> n a", a=1))
                load(k.col[:, 5:6], a["L3_gnn_b2"].rearrange("(n a) -> n a", a=1))
                load(k.w2[:, :], a["W2T"])
                load(k.w3[:, :], a["W3T"])
                load(k.b1row[:, :], row(a["L3_gnn_b1"], H).to_broadcast([P, H]))
                load(k.b3[:, :], row(a["L3_gnn_b3"], C).to_broadcast([P, C]))
                sp.wait_ge(none_in, 1)
                sp.dma_start(k.where.rearrange("(q n) a -> q (n a)", q=80), none[:, :]).then_inc(filled, 16)
                with sp.Fori(0, ITERS) as j:
                    for b in range(2):
                        sp.wait_ge(win_used[b], j)
                        sp.dma_start(win[b][:, :], row(dstp[bass.ds((2 * j + b) * CE, CE + 1)], CE + 1)
                                     .to_broadcast([P, CE + 1])).then_inc(win_in[b], 16)
                sp.wait_ge(loaded, 16 * len(n_loads))
                sp.wait_ge(filled, 16)

            @block.gpsimd
            def _(pool):
                gp = nc.gpsimd
                gp.memset(none[:, :], NONE).then_inc(none_in, 1)
                gp.memset(k.wd2[:, :], 0.0).then_inc(zeros, 1)
                gp.memset(k.ident[:, :], 0.0)
                gp.memset(k.w_value[:, 0:C], 0.0)
                gp.memset(k.ones[:, :], 1.0)
                gp.memset(k.eps[:, 0:1], EPS)
                gp.memset(k.eps[:, 1:2], EPS * EPS)
                gp.memset(k.eps[:, 2:3], 10 * math.log(2.0))
                gp.memset(k.eps[:, 3:4], 1.0).then_inc(consts, 1)
                pool.wait_ge(consts, 1)
                gp.affine_select(out=k.ident[:, :], in_=k.ident[:, :], compare_op=ALU.not_equal, fill=1.0,
                                 base=0, pattern=[[-1, P]], channel_multiplier=1).then_inc(consts, 1)

            @block.tensor
            def _(pe):
                pe.wait_ge(consts, 2)
                pe.wait_ge(esteps, 5)
                for n in range(4):
                    for h in range(2):
                        i = nc.tensor.transpose(pT[n // 2][:, n % 2, h, :], endf[:, n, P * h:P * h + P],
                                                k.ident[0:Q, 0:Q])
                i.then_inc(turned, 1)

            @block.vector
            def _(dve):
                v = nc.vector
                dve.wait_ge(ends_in, 48)
                v.tensor_tensor(k.lastq[:, :], ends[:, 0, :], ends[:, 1, :], ALU.not_equal).then_inc(esteps, 1)
                v.tensor_copy(endf[:, 0, :], ends[:, 0, :]).then_inc(esteps, 1)
                v.tensor_copy(endf[:, 2, :], ends[:, 2, :]).then_inc(esteps, 1)
                dve.wait_ge(esteps, 1)
                v.tensor_copy(endf[:, 3, :], k.lastq[:, :])
                v.tensor_scalar(endf[:, 1, :], k.lastq[:, :], -float(NONE), float(NONE), ALU.mult,
                                ALU.add).then_inc(esteps, 1)
                dve.wait_ge(esteps, 4)
                v.tensor_tensor(endf[:, 1, :], endf[:, 1, :], endf[:, 0, :], ALU.add).then_inc(esteps, 1)
                dve.wait_ge(turned, 1)
                for n, dst in enumerate((k.dst, k.put, k.src, k.last)):
                    v.tensor_copy(dst[:, :].rearrange("p (q h) -> p h q", h=2), pT[n // 2][:, n % 2, :, :])\
                        .then_inc(tables, 1)
                with dve.Fori(0, ITERS) as j:
                    for b in range(2):
                        dve.wait_ge(win_in[b], 16 * j + 16)
                        v.tensor_tensor(k.same[:, bass.ds((2 * j + b) * CE, CE)], win[b][:, 1:CE + 1],
                                        win[b][:, 0:CE], ALU.is_equal).then_inc(win_used[b], 1)
                dve.wait_ge(loaded, 16 * len(n_loads))
                dve.wait_ge(consts, 2)
                v.tensor_scalar(k.w_logit[0:C, :], k.w_logit[0:C, :], -1.0, None, ALU.mult)
                v.memset(k.w_value[C:P, C:P], 0.0)
                v.memset(k.w_att_s[0:C, :], 0.0)
                v.tensor_scalar(k.w_att_s[C:P, :], k.ones[C:P, :], wcol[C:P, 0:1], None, ALU.mult)


def reuse(eng, sem, value):
    if not (isinstance(value, int) and value == 0):
        eng.wait_ge(sem, value)


def last_of(j, b):
    return 2 * j + (b + 1)


def mlp_and_gram_stage(nc, k, a):
    with Stage(nc, "mg") as g:
        edge = g.sb("edge", [P, NT], I32)
        stage_i = [g.sb(f"stage_i{b}", [P, ST], I32) for b in range(2)]
        stage_v = [g.sb(f"stage_v{b}", [P, ST], I32) for b in range(2)]
        attr = [g.sb(f"attr{b}", [4, CE]) for b in range(2)]
        z = g.sb("z", [P, NT * C], F32)
        zn = [g.sb(f"zn{b}", [P, CT * C]) for b in range(2)]
        zq = [g.sb(f"zq{b}", [P, CT * C]) for b in range(2)]
        zs = [g.sb(f"zs{b}", [P, CT]) for b in range(2)]
        q = g.sb("q", [P, NT])
        act = [g.sb(f"act{b}", [P, CE // 2]) for b in range(2)]
        pz = [g.ps(f"pz{b}", [P, CT * C]) for b in range(2)]
        pt = [g.ps(f"pt{b}", [P, CE // 2]) for b in range(2)]
        pos_sems = g.pair("put_done"), g.pair("got"), g.sem("staged"), g.sem("passed"), g.sem("copied")
        ones_in = g.sem("ones_in"); passed_dve = g.sem("passed_dve")
        attr_in = g.pair("attr_in"); mlp_out = g.pair("mlp_out")
        e = {}
        for layer in (1, 2):
            for n in ("prod", "sum", "cen", "sq", "sumsq", "scaled", "turned", "gelu"):
                e[n, layer] = g.sem(f"{n}{layer}")
        var_ln = g.sem("var_ln"); dev = g.sem("dev")
        X = [[g.sb(f"x{w}{b}", [P, NODE_ROWS * C]) for b in range(2)] for w in range(2)]
        Y = [[g.sb(f"y{w}{b}", [P, NODE_ROWS * C]) for b in range(2)] for w in range(2)]
        Z = [[g.sb(f"z{w}{b}", [P, NODE_ROWS * C]) for b in range(2)] for w in range(2)]
        Q = [g.sb(f"sq{b}", [P, NODE_ROWS * C]) for b in range(2)]
        st = [g.sb(f"st{b}", [P, 3, NODE_ROWS]) for b in range(2)]
        lower = g.sb("lower", [C, C + 1])
        pG = g.ps("pG", [P, P + 1])
        x_in = [g.pair(f"x_in{w}_") for w in range(2)]; x1_out = [g.pair(f"x1_out{w}_") for w in range(2)]
        d = {n: g.sem("d_" + n) for n in ("sum", "cen", "sq", "sumsq", "ln", "dev", "norm", "gram")}
        pairs = D_FULL // 2 + 1
        assert D_FULL % 2 == 1 and pairs % 2 == 1

        def sizes(q):
            return (P, D_REST) if isinstance(q, int) and q == pairs - 1 else (P, P)

        def seen(q, w):
            return 8 * q + (8 if w else 16)

        with nc.Block() as block:

            @block.gpsimd
            def _(pool):
                put_done, got, staged, passed, copied = pos_sems
                gp = nc.gpsimd
                for b in range(2):
                    gp.memset(attr[b][:, :], 1.0).then_inc(ones_in, 1)
                pool.wait_ge(ones_in, 2)
                gp.iota(edge[:, :], pattern=[[P, NT]], base=0, channel_multiplier=1).then_inc(copied, 1)
                pool.wait_ge(copied, 1)
                bound = pool.to_reg(N - 1)
                with pool.Fori(0, NT // (2 * ST)) as j:
                    for b in range(2):
                        at = bass.ds((2 * j + b) * ST, ST)
                        pool.wait_ge(put_done[b], 16 * ST * j)
                        gp.tensor_copy(stage_i[b][:, :], k.put[:, at])
                        gp.tensor_copy(stage_v[b][:, :], edge[:, at]).then_inc(staged, 1)
                        pool.wait_ge(staged, last_of(j, b))
                        pool.sem_inc(passed, 1)
                        for t in range(ST):
                            gp.indirect_dma_start(
                                out=k.where, out_offset=bass.IndirectOffsetOnAxis(ap=stage_i[b][:, t:t + 1], axis=0),
                                in_=stage_v[b][:, t:t + 1], in_offset=None, bounds_check=bound,
                                oob_is_err=False).then_inc(put_done[b], 16)
                for b in range(2):
                    pool.wait_ge(put_done[b], 16 * NT // 2)
                with pool.Fori(0, NT // (2 * ST)) as j:
                    for b in range(2):
                        at = bass.ds((2 * j + b) * ST, ST)
                        gp.tensor_copy(stage_i[b][:, :], k.src[:, at]).then_inc(staged, 1)
                        pool.wait_ge(staged, 2 * j + (NT // ST + b + 1))
                        pool.wait_ge(copied, 2 * j + 1)
                        pool.sem_inc(passed, 1)
                        for t in range(ST):
                            gp.indirect_dma_start(
                                out=stage_v[b][:, t:t + 1], out_offset=None, in_=k.where,
                                in_offset=bass.IndirectOffsetOnAxis(ap=stage_i[b][:, t:t + 1], axis=0),
                                bounds_check=bound, oob_is_err=False).then_inc(got[b], 16)
                    for b in range(2):
                        pool.wait_ge(got[b], 16 * ST * j + 16 * ST)
                        gp.tensor_copy(k.pos[:, bass.ds((2 * j + b) * ST, ST)], stage_v[b][:, :])\
                            .then_inc(copied, 1)

            @block.sync
            def _(sp):
                sp.wait_ge(ones_in, 2)
                with sp.Fori(0, ITERS) as j:
                    for b in range(2):
                        sp.wait_ge(e["prod", 1], 2 * j)
                        sp.dma_start(attr[b][0:3, :], a["attrT"][:, bass.ds((2 * j + b) * CE, CE)])\
                            .then_inc(attr_in[b], 16)
                with sp.Fori(0, ITERS) as j:
                    for b in range(2):
                        sp.wait_ge(e["gelu", 2], last_of(j, b))
                        rows = k.mlp[:, bass.ds((2 * j + b) * CE, CE)].rearrange("c (n h e) -> c n h e", h=2, e=P)
                        for h in range(2):
                            sp.dma_start(rows[:, :, h, :], groups(act[b][C * h:C * h + C, :], CT // 2))\
                                .then_inc(mlp_out[b], 16)

                def load(q, w):
                    for b, p in enumerate(sizes(q)):
                        if not isinstance(q, int) or q >= 2:
                            sp.wait_ge(d["cen"], 2 * q - 2)
                        sp.dma_start(X[w][b][0:p, :], node_rows(a["x"], 2 * q + b, p)).then_inc(x_in[w][b], 16)

                def store(q, w):
                    for b, p in enumerate(sizes(q)):
                        sp.wait_ge(d["norm"], last_of(q, b))
                        sp.dma_start(node_rows(k.x1, 2 * q + b, p), Z[w][b][0:p, :]).then_inc(x1_out[w][b], 16)

                load(0, 0)
                load(1, 1)
                with sp.Fori(0, pairs // 2 - 1) as j:
                    load(2 * j + 2, 0)
                    store(2 * j, 0)
                    load(2 * j + 3, 1)
                    store(2 * j + 1, 1)
                load(pairs - 1, 0)
                for q in range(pairs - 3, pairs):
                    store(q, q % 2)
                for b in range(2):
                    sp.wait_ge(mlp_out[b], 32 * ITERS)
                    sp.wait_ge(x1_out[0][b], seen(pairs - 1, 0))
                    sp.wait_ge(x1_out[1][b], seen(pairs - 2, 1))

            @block.tensor
            def _(pe):
                t = nc.tensor

                def first_layer(j, b):
                    pe.wait_ge(e["cen", 1], 2 * j)
                    for n in range(CT):
                        i = t.matmul(pz[b][:, n * C:n * C + C], attr[b][:, n * P:n * P + P], k.wd1[:, :],
                                     start=True, stop=True)
                    i.then_inc(e["prod", 1], 1)

                def second_layer(j, b):
                    pe.wait_ge(e["cen", 2], 2 * j)
                    t.matmul(pz[b][:, :], k.ones[0:1, :], k.bd2[:, :, :].rearrange("a n c -> a (n c)"),
                             start=True, stop=False, skip_group_check=True)
                    for n in range(CT // 2):
                        i = t.matmul(pz[b][:, n * P:n * P + P], act[b][:, n * P:n * P + P], k.wd2[:, :],
                                     start=False, stop=n == CT // 2 - 1, skip_group_check=True)
                    i.then_inc(e["prod", 2], 1)

                def turn(j, b, layer):
                    pe.wait_ge(e["scaled", layer], last_of(j, b))
                    pe.wait_ge(e["gelu", layer], 2 * j)
                    for n in range(CT // 2):
                        i = t.transpose(pt[b][:, n * P:n * P + P], zn[b][:, n * P:n * P + P], k.ident[:, :])
                    i.then_inc(e["turned", layer], 1)

                with pe.Fori(0, ITERS) as j:
                    for b in range(2):
                        pe.wait_ge(attr_in[b], 16 * j + 16)
                        first_layer(j, b)
                with pe.Fori(0, ITERS) as j:
                    for b in range(2):
                        turn(j, b, 1)
                    for b in range(2):
                        pe.wait_ge(e["gelu", 1], last_of(j, b))
                        second_layer(j, b)
                with pe.Fori(0, ITERS) as j:
                    for b in range(2):
                        turn(j, b, 2)

                def gram(q, w):
                    for b, p in enumerate(sizes(q)):
                        pe.wait_ge(d["norm"], last_of(q, b))
                        for n in range(NODE_ROWS // 2):
                            first = isinstance(q, int) and q == 0 and b == 0 and n == 0
                            end = isinstance(q, int) and q == pairs - 1 and b == 1 and n == NODE_ROWS // 2 - 1
                            rows = Z[w][b][0:p, n * P:n * P + P]
                            t.matmul(pG[:, 0:P], rows, rows, start=first, stop=end, skip_group_check=True)
                            i = t.matmul(pG[:, P:P + 1], rows, k.ones[0:p, 0:1], start=False, stop=end,
                                         skip_group_check=True)
                        i.then_inc(d["gram"], 1)

                gram(0, 0)
                with pe.Fori(0, pairs // 2 - 1) as j:
                    gram(2 * j + 1, 1)
                    gram(2 * j + 2, 0)
                gram(pairs - 2, 1)
                gram(pairs - 1, 0)

            @block.scalar
            def _(act_):
                s = nc.scalar

                def square_edges(j, b, layer):
                    act_.wait_ge(e["cen", layer], last_of(j, b))
                    act_.wait_ge(e["sumsq", layer], 2 * j)
                    s.activation(zq[b][:, :], z[:, bass.ds((2 * j + b) * CT * C, CT * C)], ACT.Square)\
                        .then_inc(e["sq", layer], 1)

                def deviations(layer):
                    act_.wait_ge(e["sumsq", layer], 2 * ITERS)
                    s.activation(q[:, :], q[:, :], ACT.Ln, scale=1.0 / C, bias=k.eps[:, 0:1]).then_inc(var_ln, 1)
                    act_.wait_ge(var_ln, layer)
                    s.activation(q[:, :], q[:, :], ACT.Exp, scale=-0.5).then_inc(dev, 1)

                def gelu(j, b, layer):
                    act_.wait_ge(e["turned", layer], last_of(j, b))
                    if layer == 1:
                        act_.wait_ge(e["prod", 2], 2 * j)
                    else:
                        act_.wait_ge(mlp_out[b], 32 * j)
                    s.activation(act[b][:, :], pt[b][:, :], ACT.Gelu, scale=k.col[:, 2 * layer - 2:2 * layer - 1],
                                 bias=k.col[:, 2 * layer - 1:2 * layer]).then_inc(e["gelu", layer], 1)

                s.preload_act_table_set(LN_EXP)
                with act_.Fori(0, ITERS) as j:
                    for b in range(2):
                        square_edges(j, b, 1)
                deviations(1)
                s.preload_act_table_set(GELU)
                with act_.Fori(0, ITERS) as j:
                    for b in range(2):
                        gelu(j, b, 1)
                    for b in range(2):
                        square_edges(j, b, 2)
                deviations(2)
                s.preload_act_table_set(GELU)
                with act_.Fori(0, ITERS) as j:
                    for b in range(2):
                        gelu(j, b, 2)
                s.preload_act_table_set(LN_EXP)

                def deviate(q, w):
                    for b, p in enumerate(sizes(q)):
                        act_.wait_ge(d["cen"], last_of(q, b))
                        reuse(act_, d["sumsq"], 2 * q)
                        s.activation(Q[b][0:p, :], Y[w][b][0:p, :], ACT.Square).then_inc(d["sq"], 1)
                    for b, p in enumerate(sizes(q)):
                        act_.wait_ge(d["sumsq"], last_of(q, b))
                        s.activation(st[b][0:p, 1, :], st[b][0:p, 1, :], ACT.Ln, scale=1.0 / C,
                                     bias=k.eps[0:p, 0:1]).then_inc(d["ln"], 1)
                    for b, p in enumerate(sizes(q)):
                        act_.wait_ge(d["ln"], last_of(q, b))
                        s.activation(st[b][0:p, 2, :], st[b][0:p, 1, :], ACT.Exp, scale=-0.5).then_inc(d["dev"], 1)

                deviate(0, 0)
                with act_.Fori(0, pairs // 2 - 1) as j:
                    deviate(2 * j + 1, 1)
                    deviate(2 * j + 2, 0)
                deviate(pairs - 2, 1)
                deviate(pairs - 1, 0)

            @block.vector
            def _(dve):
                v = nc.vector

                def center_edges(j, layer):
                    for b in range(2):
                        dve.wait_ge(e["prod", layer], last_of(j, b))
                        v.tensor_reduce(out=zs[b][:, :], in_=groups(pz[b][:, :], CT), op=ALU.add, axis=AX)\
                            .then_inc(e["sum", layer], 1)
                    for b in range(2):
                        dve.wait_ge(e["sum", layer], last_of(j, b))
                        v.scalar_tensor_tensor(groups(z[:, bass.ds((2 * j + b) * CT * C, CT * C)], CT),
                                               over(zs[b][:, :], C), -1.0 / C, groups(pz[b][:, :], CT),
                                               ALU.mult, ALU.add).then_inc(e["cen", layer], 1)

                def sum_edges(j, layer):
                    for b in range(2):
                        dve.wait_ge(e["sq", layer], last_of(j, b))
                        dve.sem_inc(passed_dve, 1)
                        v.tensor_reduce(out=q[:, bass.ds((2 * j + b) * CT, CT)], in_=groups(zq[b][:, :], CT),
                                        op=ALU.add, axis=AX).then_inc(e["sumsq", layer], 1)

                def scale_edges(j, layer):
                    for b in range(2):
                        dve.wait_ge(e["turned", layer], 2 * j)
                        v.tensor_tensor(groups(zn[b][:, :], CT), groups(z[:, bass.ds((2 * j + b) * CT * C, CT * C)], CT),
                                        over(q[:, bass.ds((2 * j + b) * CT, CT)], C), ALU.mult)\
                            .then_inc(e["scaled", layer], 1)

                with dve.Fori(0, ITERS) as j:
                    center_edges(j, 1)
                    sum_edges(j, 1)
                dve.wait_ge(dev, 1)
                with dve.Fori(0, ITERS) as j:
                    scale_edges(j, 1)
                    center_edges(j, 2)
                    sum_edges(j, 2)
                dve.wait_ge(dev, 2)
                with dve.Fori(0, ITERS) as j:
                    scale_edges(j, 2)

                def step(q, r, w):
                    first, second = ([] if n is None else list(enumerate(sizes(n))) for n in (q, r))
                    for b, p in first:
                        dve.wait_ge(x_in[w][b], seen(q, w))
                        v.tensor_reduce(out=st[b][0:p, 0, :], in_=groups(X[w][b][0:p, :], NODE_ROWS),
                                        op=ALU.add, axis=AX).then_inc(d["sum"], 1)
                    for b, p in first:
                        dve.wait_ge(d["sum"], last_of(q, b))
                        v.scalar_tensor_tensor(groups(Y[w][b][0:p, :], NODE_ROWS), over(st[b][0:p, 0, :], C),
                                               -1.0 / C, groups(X[w][b][0:p, :], NODE_ROWS), ALU.mult, ALU.add)\
                            .then_inc(d["cen"], 1)
                    for b, p in second:
                        dve.wait_ge(d["dev"], last_of(r, b))
                        if not isinstance(r, int) or r >= 2:
                            dve.wait_ge(d["gram"], 2 * r - 2)
                            dve.wait_ge(x1_out[1 - w][b], seen(r, 1 - w) - 16)
                        v.tensor_tensor(groups(Z[1 - w][b][0:p, :], NODE_ROWS), groups(Y[1 - w][b][0:p, :], NODE_ROWS),
                                        over(st[b][0:p, 2, :], C), ALU.mult).then_inc(d["norm"], 1)
                    for b, p in first:
                        dve.wait_ge(d["sq"], last_of(q, b))
                        v.tensor_reduce(out=st[b][0:p, 1, :], in_=groups(Q[b][0:p, :], NODE_ROWS),
                                        op=ALU.add, axis=AX).then_inc(d["sumsq"], 1)

                step(0, None, 0)
                step(1, 0, 1)
                with dve.Fori(0, pairs // 2 - 1) as j:
                    step(2 * j + 2, 2 * j + 1, 0)
                    step(2 * j + 3, 2 * j + 2, 1)
                step(pairs - 1, pairs - 2, 0)
                step(None, pairs - 1, 1)
                dve.wait_ge(d["gram"], 2 * pairs)
                v.memset(k.gram[:, :], 0.0).then_inc(dev, 1)
                v.tensor_copy(lower[:, :], pG[C:P, C:P + 1]).then_inc(dev, 1)
                dve.wait_ge(dev, 4)
                v.tensor_tensor(k.gram[0:C, 0:C], pG[0:C, 0:C], lower[:, 0:C], ALU.add)
                v.tensor_tensor(k.gram[0:C, P:P + 1], pG[0:C, P:P + 1], lower[:, C:C + 1], ALU.add)


def node_rows(ap, chunk, parts):
    v = ap[bass.ds(chunk * DN, parts * NODE_ROWS)]
    return v.rearrange("(p n) f -> p (n f)", n=NODE_ROWS)


def attention_stage(nc, k, a):
    with Stage(nc, "at") as g:
        pairs = lambda name, shape, dt=F32: [g.sb(f"{name}{b}", shape, dt) for b in range(2)]
        both = lambda name, shape, dt=F32: [pairs(f"{name}{w}", shape, dt) for w in range(2)]
        idx = both("idx", [P, 2 * CT], I32)
        W = both("W", [P, 2 * CT * C])
        V = both("V", [P, CE])
        XF = pairs("XF", [P, CE])
        anew = pairs("anew", [P, CE])
        L = pairs("L", [P, CE])
        M = pairs("M", [P, CE + 1])
        A = pairs("A", [P, CE])
        S = pairs("S", [P, CE])
        Y = both("Y", [P, 2 * CT * C])
        N1 = pairs("N1", [P, 2 * CT * C])
        Q = pairs("Q", [P, 2 * CT * C])
        Z = pairs("Z", [P, CT * C])
        R = pairs("R", [P, CT * C])
        D = pairs("D", [P, CT * C])
        em = pairs("em", [P, CT * C])
        st = pairs("st", [P, 3, 2 * CT])
        zt = pairs("zt", [P, 3, CT])
        lower = g.sb("lower", [C, C + 1])
        pA = [g.ps(f"pA{b}", [P, CE]) for b in range(2)]
        pL = [g.ps(f"pL{b}", [P, CE]) for b in range(2)]
        pV = [g.ps(f"pV{b}", [P, CE]) for b in range(2)]
        pG = g.ps("pG", [P, P + 1])
        got = [g.pair(f"got{w}_") for w in range(2)]; mlp_in = [g.pair(f"mlp_in{w}_") for w in range(2)]
        s1_out = g.pair("s1_out"); d1_out = g.pair("d1_out")
        e = {n: g.sem(n) for n in ("staged", "passed", "zeros", "starts", "turned", "ends", "anew", "products", "logits", "values",
                                   "maxed", "diffs", "weights", "decay", "weighed", "summed", "back",
                                   "shifted", "ratio", "added", "sum", "cen", "sq", "sumsq", "ln", "dev", "norm", "masked",
                                   "gram", "lnsum", "sums", "zsum", "zcen", "zsq", "zsumsq", "zln", "zdev", "znorm")}
        low, high = slice(0, C), slice(C, P)

        def seen(q, w, per):
            return per // 2 * q + (per // 2 if w else per)

        def schedule(eng, step):
            assert ITERS % 2 == 1
            step(0, None, 0)
            with eng.Fori(0, ITERS // 2) as j:
                step(2 * j + 1, 2 * j, 1)
                step(2 * j + 2, 2 * j + 1, 0)
            step(None, ITERS - 1, 1)

        with nc.Block() as block:

            @block.gpsimd
            def _(pool):
                gp = nc.gpsimd
                for w in range(2):
                    for b in range(2):
                        gp.memset(W[w][b][:, :], 0.0).then_inc(e["zeros"], 1)
                bound = pool.to_reg(N - 1)
                pool.wait_ge(e["zeros"], 4)

                def gather(q, w):
                    for b in range(2):
                        at = bass.ds((2 * q + b) * CT, CT)
                        if not isinstance(q, int) or q >= 2:
                            pool.wait_ge(e["turned"], 2 * q - 2)
                            pool.wait_ge(e["cen"], 2 * q - 2)
                        gp.tensor_copy(idx[w][b][:, 0:CT], k.src[:, at])
                        gp.tensor_copy(idx[w][b][:, CT:2 * CT], k.dst[:, at]).then_inc(e["staged"], 1)
                    for b in range(2):
                        pool.wait_ge(e["staged"], last_of(q, b))
                        pool.sem_inc(e["passed"], 1)
                        for t in range(CT):
                            for h in range(2):
                                gp.indirect_dma_start(
                                    out=W[w][b][:, (2 * t + h) * C:(2 * t + h + 1) * C], out_offset=None, in_=a["x"],
                                    in_offset=bass.IndirectOffsetOnAxis(
                                        ap=idx[w][b][:, h * CT + t:h * CT + t + 1], axis=0),
                                    bounds_check=bound, oob_is_err=False).then_inc(got[w][b], 16)

                gather(0, 0)
                gather(1, 1)
                with pool.Fori(0, ITERS // 2 - 1) as j:
                    gather(2 * j + 2, 0)
                    gather(2 * j + 3, 1)
                gather(ITERS - 1, 0)

            @block.sync
            def _(sp):
                def load(q, w):
                    for b in range(2):
                        if not isinstance(q, int) or q >= 2:
                            sp.wait_ge(e["weighed"], 2 * q - 2)
                        for h in (low, high):
                            sp.dma_start(V[w][b][h, :], k.mlp[:, bass.ds((2 * q + b) * CE, CE)])\
                                .then_inc(mlp_in[w][b], 16)

                def step(q, r, w):
                    if q is not None:
                        if not isinstance(q, int):
                            load(q + 1, 1 - w)
                        for b in range(2):
                            sp.wait_ge(e["norm"], last_of(q, b))
                            sp.dma_start(one(by_chunk(k.s1), 2 * q + b), ends(N1[b])[:, :, 0, :]).then_inc(s1_out[b], 16)
                    if r is not None:
                        for b in range(2):
                            sp.wait_ge(e["znorm"], last_of(r, b))
                            sp.dma_start(one(by_chunk(k.d1), 2 * r + b), groups(Z[b][:, :], CT)).then_inc(d1_out[b], 16)

                load(0, 0)
                load(1, 1)
                step(0, None, 0)
                with sp.Fori(0, ITERS // 2 - 1) as j:
                    step(2 * j + 1, 2 * j, 1)
                    step(2 * j + 2, 2 * j + 1, 0)
                load(ITERS - 1, 0)
                step(ITERS - 2, ITERS - 3, 1)
                step(ITERS - 1, ITERS - 2, 0)
                step(None, ITERS - 1, 1)
                for b in range(2):
                    sp.wait_ge(s1_out[b], 16 * ITERS)
                    sp.wait_ge(d1_out[b], 16 * ITERS)

            @block.tensor
            def _(pe):
                t = nc.tensor

                def step(q, r, w):
                    if q is not None:
                        for b in range(2):
                            pe.wait_ge(got[w][b], seen(q, w, 32 * CT))
                            if not isinstance(q, int) or q >= 2:
                                pe.wait_ge(e["ratio"], 2 * q - 2)
                            for n in range(CT):
                                i = t.transpose(pA[b][:, n * P:n * P + P], W[w][b][:, n * P:n * P + P], k.ident[:, :])
                            i.then_inc(e["turned"], 1)
                        for b in range(2):
                            pe.wait_ge(e["ends"], last_of(q, b))
                            t.matmul(pL[b][:, :], k.w_logit[:, :], XF[b][:, :], start=True, stop=True)
                            t.matmul(pV[b][:, :], k.w_value[:, :], XF[b][:, :], start=True, stop=True)\
                                .then_inc(e["products"], 1)
                    if r is not None:
                        for b in range(2):
                            pe.wait_ge(e["summed"], last_of(r, b))
                            for n in range(CT):
                                i = t.transpose(pA[b][:, n * P:n * P + P], S[b][:, n * P:n * P + P], k.ident[:, :])
                            i.then_inc(e["back"], 1)
                        for b in range(2):
                            pe.wait_ge(e["masked"], last_of(r, b))
                            for n in range(CT // 2):
                                m = em[b][:, n * P:n * P + P]
                                first = isinstance(r, int) and r == 0 and b == 0 and n == 0
                                end = isinstance(r, int) and r == ITERS - 1 and b == 1 and n == CT // 2 - 1
                                t.matmul(pG[:, 0:P], m, m, start=first, stop=end, skip_group_check=True)
                                i = t.matmul(pG[:, P:P + 1], m, k.ones[:, 0:1], start=False, stop=end,
                                             skip_group_check=True)
                            i.then_inc(e["gram"], 1)

                step(0, None, 0)
                step(1, 0, 1)
                step(2, 1, 0)
                with pe.Fori(0, ITERS // 2 - 1) as j:
                    step(2 * j + 3, 2 * j + 2, 1)
                    step(2 * j + 4, 2 * j + 3, 0)
                step(None, ITERS - 1, 1)

            @block.scalar
            def _(act):
                s = nc.scalar
                s.preload_act_table_set(LN_EXP)

                def step(q, r, w):
                    first = [] if q is None else range(2)
                    second = [] if r is None else range(2)
                    for b in first:
                        act.wait_ge(e["turned"], last_of(q, b))
                        s.activation(XF[b][:, :], pA[b][:, :], ACT.Copy).then_inc(e["ends"], 1)
                    for b in first:
                        reuse(act, e["diffs"], 2 * q)
                        s.activation(anew[b][:, :], k.same[:, bass.ds((2 * q + b) * CE, CE)], ACT.Copy,
                                     scale=BIG, bias=-BIG).then_inc(e["anew"], 1)
                    for b in first:
                        act.wait_ge(e["cen"], last_of(q, b))
                        reuse(act, e["sumsq"], 2 * q)
                        s.activation(Q[b][:, :], Y[w][b][:, :], ACT.Square).then_inc(e["sq"], 1)
                    for b in first:
                        act.wait_ge(e["sumsq"], last_of(q, b))
                        s.activation(st[b][:, 1, :], st[b][:, 1, :], ACT.Ln, scale=1.0 / C, bias=k.eps[:, 0:1])\
                            .then_inc(e["ln"], 1)
                    for b in first:
                        act.wait_ge(e["ln"], last_of(q, b))
                        s.activation(st[b][:, 2, :], st[b][:, 1, :], ACT.Exp, scale=-0.5).then_inc(e["dev"], 1)
                    for b in second:
                        act.wait_ge(e["back"], last_of(r, b))
                        reuse(act, e["ratio"], 2 * r)
                        s.activation(groups(D[b][:, :], CT), ends(pA[b])[:, :, 0, :], ACT.Ln).then_inc(e["lnsum"], 1)
                    for b in second:
                        act.wait_ge(e["lnsum"], last_of(r, b))
                        s.activation(D[b][:, :], D[b][:, :], ACT.Exp, scale=-1.0).then_inc(e["sums"], 1)
                    for b in second:
                        act.wait_ge(e["zcen"], last_of(r, b))
                        reuse(act, e["zsumsq"], 2 * r)
                        s.activation(R[b][:, :], Z[b][:, :], ACT.Square).then_inc(e["zsq"], 1)
                    for b in first:
                        act.wait_ge(e["diffs"], last_of(q, b))
                        s.activation(A[b][:, :], A[b][:, :], ACT.Exp).then_inc(e["decay"], 1)
                    for b in second:
                        act.wait_ge(e["zsumsq"], last_of(r, b))
                        s.activation(zt[b][:, 1, :], zt[b][:, 1, :], ACT.Ln, scale=1.0 / C, bias=k.eps[:, 0:1])\
                            .then_inc(e["zln"], 1)
                    for b in second:
                        act.wait_ge(e["zln"], last_of(r, b))
                        s.activation(zt[b][:, 2, :], zt[b][:, 1, :], ACT.Exp, scale=-0.5).then_inc(e["zdev"], 1)
                    for b in first:
                        s.activation(L[b][:, :], L[b][:, :], ACT.Exp).then_inc(e["weights"], 1)

                schedule(act, step)

            @block.vector
            def _(dve):
                v = nc.vector
                for b in range(2):
                    v.memset(M[b][:, :], -BIG).then_inc(e["starts"], 1)
                    v.memset(S[b][:, :], 0.0).then_inc(e["starts"], 1)
                dve.wait_ge(e["starts"], 4)

                def step(q, r, w):
                    first = [] if q is None else range(2)
                    second = [] if r is None else range(2)
                    for b in second:
                        dve.wait_ge(e["weights"], last_of(r, b))
                        v.tensor_tensor(L[b][high, :], L[b][high, :], V[1 - w][b][high, :], ALU.mult)\
                            .then_inc(e["weighed"], 1)
                    for b in second:
                        dve.wait_ge(e["weighed"], last_of(r, b))
                        v.tensor_tensor_scan(S[b][:, :], A[b][:, :], L[b][:, :], S[1 - b][:, CE - 1:CE],
                                             ALU.mult, ALU.add).then_inc(e["summed"], 1)
                        dve.wait_ge(e["summed"], last_of(r, b))
                    for b in first:
                        dve.wait_ge(got[w][b], seen(q, w, 32 * CT))
                        v.tensor_reduce(out=st[b][:, 0, :], in_=groups(W[w][b][:, :], 2 * CT), op=ALU.add, axis=AX)\
                            .then_inc(e["sum"], 1)
                    for b in first:
                        dve.wait_ge(e["sum"], last_of(q, b))
                        v.scalar_tensor_tensor(groups(Y[w][b][:, :], 2 * CT), over(st[b][:, 0, :], C), -1.0 / C,
                                               groups(W[w][b][:, :], 2 * CT), ALU.mult, ALU.add).then_inc(e["cen"], 1)
                    for b in second:
                        reuse(dve, e["gram"], 2 * r)
                        v.tensor_tensor(groups(em[b][:, :], CT), ends(N1[b])[:, :, 1, :],
                                        over(k.last[:, bass.ds((2 * r + b) * CT, CT)], C), ALU.mult)\
                            .then_inc(e["masked"], 1)
                    for b in first:
                        dve.wait_ge(e["sq"], last_of(q, b))
                        v.tensor_reduce(out=st[b][:, 1, :], in_=groups(Q[b][:, :], 2 * CT), op=ALU.add, axis=AX)\
                            .then_inc(e["sumsq"], 1)
                    for b in first:
                        dve.wait_ge(e["products"], last_of(q, b))
                        dve.wait_ge(mlp_in[w][b], seen(q, w, 32))
                        v.tensor_tensor(L[b][:, :], pL[b][:, :], V[w][b][:, :], ALU.add).then_inc(e["logits"], 1)
                    for b in first:
                        dve.wait_ge(e["logits"], last_of(q, b))
                        v.tensor_tensor(V[w][b][high, :], V[w][b][high, :], pV[b][high, :], ALU.add)\
                            .then_inc(e["values"], 1)
                        v.tensor_copy(M[b][:, 0:1], M[1 - b][:, CE:CE + 1])
                        dve.wait_ge(e["anew"], last_of(q, b))
                        v.tensor_tensor_scan(M[b][:, 1:CE + 1], anew[b][:, :], L[b][:, :], M[1 - b][:, CE:CE + 1],
                                             ALU.add, ALU.max).then_inc(e["maxed"], 1)
                        dve.wait_ge(e["maxed"], last_of(q, b))
                    for b in second:
                        dve.wait_ge(e["sums"], last_of(r, b))
                        reuse(dve, d1_out[b], 16 * r)
                        v.tensor_tensor(groups(Z[b][:, :], CT), ends(pA[b])[:, :, 1, :], groups(D[b][:, :], CT),
                                        ALU.mult).then_inc(e["ratio"], 1)
                    for b in second:
                        dve.wait_ge(e["ratio"], last_of(r, b))
                        v.tensor_tensor(groups(Z[b][:, :], CT), groups(Z[b][:, :], CT), ends(Y[1 - w][b])[:, :, 1, :],
                                        ALU.add).then_inc(e["added"], 1)
                    for b in second:
                        dve.wait_ge(e["added"], last_of(r, b))
                        v.tensor_reduce(out=zt[b][:, 0, :], in_=groups(Z[b][:, :], CT), op=ALU.add, axis=AX)\
                            .then_inc(e["zsum"], 1)
                    for b in second:
                        dve.wait_ge(e["zsum"], last_of(r, b))
                        v.scalar_tensor_tensor(groups(Z[b][:, :], CT), over(zt[b][:, 0, :], C), -1.0 / C,
                                               groups(Z[b][:, :], CT), ALU.mult, ALU.add).then_inc(e["zcen"], 1)
                    for b in first:
                        v.tensor_tensor(L[b][:, :], L[b][:, :], M[b][:, 1:CE + 1], ALU.subtract)
                        v.tensor_tensor(A[b][:, :], M[b][:, 0:CE], anew[b][:, :], ALU.add).then_inc(e["shifted"], 1)
                    for b in first:
                        dve.wait_ge(e["shifted"], last_of(q, b))
                        v.tensor_tensor(A[b][:, :], A[b][:, :], M[b][:, 1:CE + 1], ALU.subtract)\
                            .then_inc(e["diffs"], 1)
                    for b in second:
                        dve.wait_ge(e["zsq"], last_of(r, b))
                        v.tensor_reduce(out=zt[b][:, 1, :], in_=groups(R[b][:, :], CT), op=ALU.add, axis=AX)\
                            .then_inc(e["zsumsq"], 1)
                    for b in first:
                        dve.wait_ge(e["dev"], last_of(q, b))
                        reuse(dve, s1_out[b], 16 * q)
                        v.tensor_tensor(groups(N1[b][:, :], 2 * CT), groups(Y[w][b][:, :], 2 * CT),
                                        over(st[b][:, 2, :], C), ALU.mult).then_inc(e["norm"], 1)
                    for b in second:
                        dve.wait_ge(e["zdev"], last_of(r, b))
                        v.tensor_tensor(groups(Z[b][:, :], CT), groups(Z[b][:, :], CT), over(zt[b][:, 2, :], C),
                                        ALU.mult).then_inc(e["znorm"], 1)

                schedule(dve, step)
                dve.wait_ge(e["gram"], 2 * ITERS)
                v.tensor_copy(lower[:, 0:C], pG[C:P, C:P])
                v.tensor_copy(lower[:, C:C + 1], pG[C:P, P:P + 1])
                v.tensor_tensor(k.gram[0:C, 0:C], k.gram[0:C, 0:C], pG[0:C, 0:C], ALU.subtract)
                v.tensor_tensor(k.gram[0:C, P:P + 1], k.gram[0:C, P:P + 1], pG[0:C, P:P + 1], ALU.subtract)\
                    .then_inc(e["starts"], 1)
                dve.wait_ge(e["starts"], 5)
                v.tensor_tensor(k.gram[0:C, 0:C], k.gram[0:C, 0:C], lower[:, 0:C], ALU.subtract)
                v.tensor_tensor(k.gram[0:C, P:P + 1], k.gram[0:C, P:P + 1], lower[:, C:C + 1], ALU.subtract)


def override_rows(nc, pool, k, table, width, idx, landing, sems, trips, bound):
    gp = nc.gpsimd
    with pool.Fori(0, trips) as j:
        for b in range(2):
            pool.wait_ge(sems["copied"][b], 16 * j)
            gp.tensor_copy(idx[b][:, :], k.pos[:, bass.ds((2 * j + b) * CT, CT)]).then_inc(sems["staged"], 1)
        for b in range(2):
            pool.wait_ge(sems["staged"], last_of(j, b))
            pool.wait_ge(sems["landed"][b], 16 * j + 16)
            pool.sem_inc(sems["passed"], 1)
            for t in range(CT):
                gp.indirect_dma_start(out=landing[b][:, t * width:(t + 1) * width], out_offset=None, in_=table,
                                      in_offset=bass.IndirectOffsetOnAxis(ap=idx[b][:, t:t + 1], axis=0),
                                      bounds_check=bound, oob_is_err=False).then_inc(sems["got"][b], 16)


def ends(t):
    return t[:, :].rearrange("p (t w c) -> p t w c", t=CT, w=2)


def mean_stage(nc, k):
    with Stage(nc, "me") as g:
        pairs = lambda name, shape, dt=F32: [g.sb(f"{name}{b}", shape, dt) for b in range(2)]
        idx = pairs("idx", [P, CT], I32)
        landing = pairs("landing", [P, CT * C])
        W = pairs("W", [P, CE])
        S = pairs("S", [P, CE])
        X = pairs("X", [P, CE])
        XM = pairs("XM", [P, CE])
        st = pairs("st", [P, 3, CT])
        pA = [g.ps(f"pA{b}", [P, CE]) for b in range(2)]
        pB = [g.ps(f"pB{b}", [P, CE]) for b in range(2)]
        pG = g.ps("pG", [P, P + 1])
        landed = g.pair("landed"); got = g.pair("got"); copied = g.pair("copied"); d1_in = g.pair("d1_in")
        agg_out = g.pair("agg_out")
        e = {n: g.sem(n) for n in ("staged", "passed", "starts", "turned", "summed", "back", "degree", "rdeg", "mean", "ln",
                                   "dinv", "masked", "gram")}
        sems = dict(staged=e["staged"], passed=e["passed"], landed=landed, got=got, copied=copied)
        with nc.Block() as block:

            @block.gpsimd
            def _(pool):
                override_rows(nc, pool, k, k.d1, C, idx, landing, sems, ITERS, pool.to_reg(EP - 1))

            @block.sync
            def _(sp):
                def land(j):
                    for b in range(2):
                        if not isinstance(j, int):
                            sp.wait_ge(copied[b], 16 * j)
                        sp.dma_start(groups(landing[b][:, :], CT), one(by_chunk(k.s1), 2 * j + b))\
                            .then_inc(landed[b], 16)

                def load(j, used=True):
                    for b in range(2):
                        if used:
                            sp.wait_ge(e["masked"], last_of(j - 1, b))
                        sp.dma_start(ends(X[b])[:, :, 0, :], one(by_chunk(k.d1), 2 * j + b)).then_inc(d1_in[b], 16)

                def take(j, used=True):
                    for b in range(2):
                        sp.wait_ge(got[b], 16 * CT * j + 16 * CT)
                        if used:
                            sp.wait_ge(e["turned"], last_of(j - 1, b))
                        sp.dma_start(ends(W[b])[:, :, 0, :], groups(landing[b][:, :], CT)).then_inc(copied[b], 16)

                def store(j):
                    for b in range(2):
                        sp.wait_ge(e["mean"], last_of(j, b))
                        sp.dma_start(one(by_chunk(k.agg), 2 * j + b), ends(X[b])[:, :, 1, :]).then_inc(agg_out[b], 16)

                sp.wait_ge(e["starts"], 3)
                land(0)
                load(0, used=False)
                take(0, used=False)
                with sp.Fori(0, ITERS - 1) as j:
                    land(j + 1)
                    load(j + 1)
                    take(j + 1)
                    store(j)
                store(ITERS - 1)
                for b in range(2):
                    sp.wait_ge(agg_out[b], 16 * ITERS)

            @block.tensor
            def _(pe):
                t = nc.tensor
                pe.wait_ge(e["starts"], 3)
                t.matmul(pG[:, 0:P], S[1][:, 0:P], S[1][:, 0:P], start=True, stop=False, skip_group_check=True)
                t.matmul(pG[:, P:P + 1], S[1][:, 0:P], k.ones[:, 0:1], start=False, stop=False,
                         skip_group_check=True).then_inc(e["gram"], 1)
                with pe.Fori(0, ITERS) as j:
                    for b in range(2):
                        pe.wait_ge(copied[b], 16 * j + 16)
                        pe.wait_ge(e["summed"], 2 * j)
                        for n in range(CT):
                            i = t.transpose(pA[b][:, n * P:n * P + P], W[b][:, n * P:n * P + P], k.ident[:, :])
                        i.then_inc(e["turned"], 1)
                    for b in range(2):
                        pe.wait_ge(e["summed"], last_of(j, b))
                        pe.wait_ge(e["mean"], 2 * j)
                        for n in range(CT):
                            i = t.transpose(pB[b][:, n * P:n * P + P], S[b][:, n * P:n * P + P], k.ident[:, :])
                        i.then_inc(e["back"], 1)
                    for b in range(2):
                        pe.wait_ge(e["masked"], last_of(j, b))
                        for n in range(CT):
                            m = XM[b][:, n * P:n * P + P]
                            t.matmul(pG[:, 0:P], m, m, start=False, stop=False, skip_group_check=True)
                            i = t.matmul(pG[:, P:P + 1], m, k.ones[:, 0:1], start=False, stop=False,
                                         skip_group_check=True)
                        i.then_inc(e["gram"], 1)

            @block.scalar
            def _(act):
                s = nc.scalar
                s.preload_act_table_set(LN_EXP)
                with act.Fori(0, ITERS) as j:
                    for b in range(2):
                        act.wait_ge(e["dinv"], 2 * j)
                        act.wait_ge(e["degree"], last_of(j, b))
                        s.activation(st[b][:, 1, :], st[b][:, 2, :], ACT.Ln, bias=k.eps[:, 3:4])\
                            .then_inc(e["ln"], 1)
                    for b in range(2):
                        act.wait_ge(e["ln"], last_of(j, b))
                        s.activation(k.dinv[:, bass.ds((2 * j + b) * CT, CT)], st[b][:, 1, :], ACT.Exp, scale=-0.5)\
                            .then_inc(e["dinv"], 1)

            @block.vector
            def _(dve):
                v = nc.vector
                for b in range(2):
                    v.memset(W[b][:, :], 1.0).then_inc(e["starts"], 1)
                v.memset(S[1][:, :], 0.0).then_inc(e["starts"], 1)
                dve.wait_ge(e["gram"], 1)
                with dve.Fori(0, ITERS) as j:
                    for b in range(2):
                        at = bass.ds((2 * j + b) * CE, CE)
                        dve.wait_ge(e["turned"], last_of(j, b))
                        v.tensor_tensor_scan(S[b][:, :], k.same[:, at], pA[b][:, :], S[1 - b][:, CE - 1:CE],
                                             ALU.mult, ALU.add).then_inc(e["summed"], 1)
                        dve.wait_ge(e["summed"], last_of(j, b))
                    for b in range(2):
                        dve.wait_ge(e["back"], last_of(j, b))
                        dve.wait_ge(e["ln"], 2 * j)
                        v.tensor_copy(st[b][:, 2, :], ends(pB[b])[:, :, 1, 0]).then_inc(e["degree"], 1)
                    for b in range(2):
                        dve.wait_ge(e["degree"], last_of(j, b))
                        v.reciprocal(st[b][:, 0, :], st[b][:, 2, :]).then_inc(e["rdeg"], 1)
                    for b in range(2):
                        dve.wait_ge(e["rdeg"], last_of(j, b))
                        dve.wait_ge(agg_out[b], 16 * j)
                        v.tensor_tensor(ends(X[b])[:, :, 1, :], ends(pB[b])[:, :, 0, :], over(st[b][:, 0, :], C),
                                        ALU.mult).then_inc(e["mean"], 1)
                    for b in range(2):
                        dve.wait_ge(e["mean"], last_of(j, b))
                        dve.wait_ge(d1_in[b], 16 * j + 16)
                        dve.wait_ge(e["gram"], 2 * j + 1)
                        v.tensor_tensor(groups(XM[b][:, :], CT), groups(X[b][:, :], CT),
                                        over(k.last[:, bass.ds((2 * j + b) * CT, CT)], P), ALU.mult)\
                            .then_inc(e["masked"], 1)
                dve.wait_ge(e["gram"], 2 * ITERS + 1)
                v.tensor_tensor(k.gram[:, :], k.gram[:, :], pG[:, :], ALU.add)


def batch_norm_stage(nc, k):
    with Stage(nc, "bn") as g:
        gw = g.sb("gw", [P, C])
        r = g.sb("r", [1, 8, C])
        pW = g.ps("pW", [P, C]); pR = g.ps("pR", [1, 2, C]); pB = g.ps("pB", [P, C])
        prod = g.sem("prod"); steps = g.sem("steps"); ln = g.sem("ln"); fold = g.sem("fold")
        mean, ex2, var, scale, shift = (r[:, n, :] for n in range(5))
        with nc.Block() as block:

            @block.tensor
            def _(pe):
                t = nc.tensor
                t.matmul(pW[:, :], k.gram[:, 0:P], k.wcat[:, :], start=True, stop=True).then_inc(prod, 1)
                t.matmul(pR[:, 0, :], k.gram[:, P:P + 1], k.wcat[:, :], start=True, stop=True).then_inc(prod, 1)
                pe.wait_ge(steps, 1)
                pe.wait_ge(steps, 2)
                t.matmul(pR[:, 1, :], k.ones[:, 0:1], gw[:, :], start=True, stop=True).then_inc(prod, 1)
                pe.wait_ge(fold, 1)
                t.matmul(pB[:, :], k.ones[0:1, :], scale, start=True, stop=True).then_inc(prod, 1)

            @block.scalar
            def _(act):
                act.wait_ge(steps, 5)
                nc.scalar.activation(var, var, ACT.Ln, bias=k.eps[0:1, 0:1]).then_inc(ln, 1)
                act.wait_ge(ln, 1)
                nc.scalar.activation(scale, var, ACT.Exp, scale=-0.5).then_inc(ln, 1)

            @block.vector
            def _(dve):
                v = nc.vector
                b, gamma, beta = (k.bnrow[:, n, :] for n in range(3))
                dve.wait_ge(prod, 2)
                v.scalar_tensor_tensor(gw[:, :], pW[:, :], 1.0 / N, k.wcat[:, :], ALU.mult, ALU.mult)\
                    .then_inc(steps, 1)
                v.tensor_scalar(mean, pR[:, 0, :], 1.0 / N, None, ALU.mult).then_inc(steps, 1)
                dve.wait_ge(steps, 2)
                v.tensor_tensor(ex2, mean, mean, ALU.mult).then_inc(steps, 1)
                dve.wait_ge(steps, 3)
                dve.wait_ge(prod, 3)
                v.tensor_tensor(var, pR[:, 1, :], ex2, ALU.subtract).then_inc(steps, 1)
                dve.wait_ge(steps, 4)
                v.tensor_scalar(var, var, 0.0, None, ALU.max).then_inc(steps, 1)
                v.tensor_tensor(mean, mean, b, ALU.add).then_inc(steps, 1)
                dve.wait_ge(steps, 6)
                v.tensor_tensor(shift, b, mean, ALU.subtract).then_inc(steps, 1)
                dve.wait_ge(ln, 2)
                v.tensor_tensor(scale, scale, gamma, ALU.mult).then_inc(fold, 1)
                dve.wait_ge(fold, 1)
                dve.wait_ge(steps, 7)
                v.tensor_tensor(shift, shift, scale, ALU.mult).then_inc(steps, 1)
                dve.wait_ge(steps, 8)
                v.tensor_tensor(shift, shift, beta, ALU.add).then_inc(steps, 1)
                dve.wait_ge(steps, 9)
                for n in range(NODE_ROWS):
                    v.tensor_copy(k.shift[:, n, :], shift)
                v.memset(k.wbn_r[:, :], 0.0).then_inc(steps, 1)
                dve.wait_ge(prod, 4)
                v.tensor_tensor(k.wbn[:, :], k.wcat[:, :], pB[:, :], ALU.mult).then_inc(steps, 1)
                dve.wait_ge(steps, 11)
                v.tensor_copy(k.wbn_r[0:C, 0:C], k.wbn[0:C, :])
                v.tensor_copy(k.wbn_r[C:P, C:P], k.wbn[0:C, :])


def update_stage(nc, k):
    Q2 = NT // 2
    with Stage(nc, "up") as g:
        pairs = lambda name, shape, dt=F32: [g.sb(f"{name}{b}", shape, dt) for b in range(2)]
        X = pairs("X", [P, CE])
        R = pairs("R", [P, CT * C])
        XF = pairs("XF", [P, CE])
        RF = pairs("RF", [P, CE // 2])
        U = pairs("U", [P, 2 * CT * C])
        Q = pairs("Q", [P, 2 * CT * C])
        T = pairs("T", [P, CT * C])
        st = pairs("st", [P, 5, 2 * CT])
        dot = g.sb("dot", [P, NT])
        dq = g.sb("dq", [Q2, 2 * P]); more = g.sb("more", [Q2, 2 * P]); cum = g.sb("cum", [Q2, 2 * P])
        dvq = g.sb("dvq", [Q2, 2 * P]); zero = g.sb("zero", [Q2, 2 * P])
        crow = g.sb("crow", [1, 4, Q2 + 1])
        pX = [g.ps(f"pX{b}", [P, CE]) for b in range(2)]
        pR = [g.ps(f"pR{b}", [P, CE // 2]) for b in range(2)]
        pH = [g.ps(f"pH{b}", [P, 2 * CT * C]) for b in range(2)]
        x_in = g.pair("x_in"); out_sems = g.pair("out"); rows_out = g.sem("rows_out")
        names = ("turned", "flat", "product", "relu", "sq", "sumsq", "clamped", "ln", "inv", "scaled", "added", "sum",
                 "cen", "sq2", "sumsq2", "ln2", "dev", "norm", "weighed", "dot", "passed", "tail_pe", "tail", "ready")
        e = {n: g.sem(n) for n in names}
        with nc.Block() as block:

            @block.sync
            def _(sp):
                def load(j, used=True):
                    for b in range(2):
                        if used:
                            sp.wait_ge(e["added"], last_of(j - 1, b))
                        i = 2 * j + b
                        sp.dma_start(ends(X[b])[:, :, 0, :], one(by_chunk(k.d1), i)).then_inc(x_in[b], 16)
                        sp.dma_start(ends(X[b])[:, :, 1, :], one(by_chunk(k.agg), i)).then_inc(x_in[b], 16)
                        sp.dma_start(groups(R[b][:, :], CT), one(by_chunk(k.s1), i)).then_inc(x_in[b], 16)

                def store(j):
                    for b in range(2):
                        sp.wait_ge(e["norm"], last_of(j, b))
                        for n, table in enumerate((k.d2, k.s2)):
                            sp.dma_start(one(by_chunk(table), 2 * j + b),
                                         groups(U[b][:, n * CT * C:(n + 1) * CT * C], CT)).then_inc(out_sems[b], 16)

                load(0, used=False)
                with sp.Fori(0, ITERS - 1) as j:
                    load(j + 1)
                    store(j)
                store(ITERS - 1)
                sp.wait_ge(e["ready"], 1)
                sp.dma_start(k.att_d.rearrange("(q e) -> q e", e=2 * P), dq[:, :]).then_inc(rows_out, 16)
                sp.dma_start(k.dinv_row.rearrange("(q e) -> q e", e=2 * P), dvq[:, :]).then_inc(rows_out, 16)
                sp.wait_ge(rows_out, 32)
                for b in range(2):
                    sp.wait_ge(out_sems[b], 32 * ITERS)

            @block.tensor
            def _(pe):
                t = nc.tensor
                with pe.Fori(0, ITERS) as j:
                    for b in range(2):
                        pe.wait_ge(x_in[b], 48 * j + 48)
                        pe.wait_ge(e["flat"], 2 * j)
                        for n in range(CT):
                            t.transpose(pX[b][:, n * P:n * P + P], X[b][:, n * P:n * P + P], k.ident[:, :])
                        for n in range(CT // 2):
                            i = t.transpose(pR[b][:, n * P:n * P + P], R[b][:, n * P:n * P + P], k.ident[:, :])
                        i.then_inc(e["turned"], 1)
                    for b in range(2):
                        pe.wait_ge(e["flat"], last_of(j, b))
                        pe.wait_ge(e["relu"], 2 * j)
                        t.matmul(pH[b][:, :], k.ones[0:1, :], k.shift[:, :, :].rearrange("a n c -> a (n c)"),
                                 start=True, stop=False, skip_group_check=True)
                        for n in range(CT):
                            t.matmul(pH[b][:, n * C:n * C + C], XF[b][:, n * P:n * P + P], k.wbn[:, :],
                                     start=False, stop=False, skip_group_check=True)
                        for n in range(CT // 2):
                            i = t.matmul(pH[b][:, CT * C + n * P:CT * C + n * P + P], RF[b][:, n * P:n * P + P],
                                         k.wbn_r[:, :], start=False, stop=n == CT // 2 - 1, skip_group_check=True)
                        i.then_inc(e["product"], 1)
                pe.wait_ge(e["dot"], 2 * ITERS)
                for n, src in enumerate((dot, k.dinv)):
                    for h in range(2):
                        i = t.transpose(pX[n][0:Q2, h * P:h * P + P],
                                        src[:, :].rearrange("p (q h) -> p h q", h=2)[:, h, :], k.ident[:, :])
                i.then_inc(e["tail_pe"], 1)
                pe.wait_ge(e["tail"], 5)
                t.matmul(pR[0][0:1, 0:Q2], dq[:, 0:1], k.ident[0:Q2, 0:Q2], start=True, stop=True)
                t.matmul(pR[1][0:1, 0:Q2], cum[:, 0:1], k.ident[0:Q2, 0:Q2], start=True, stop=True)\
                    .then_inc(e["tail_pe"], 1)
                pe.wait_ge(e["tail"], 8)
                t.matmul(pH[0][0:Q2, 0:1], crow[:, 2, 1:Q2 + 1], k.ones[0:1, 0:1], start=True, stop=True)\
                    .then_inc(e["tail_pe"], 1)

            @block.scalar
            def _(act):
                s = nc.scalar
                s.preload_act_table_set(LN_EXP)
                with act.Fori(0, ITERS) as j:
                    for b in range(2):
                        act.wait_ge(e["turned"], last_of(j, b))
                        act.wait_ge(e["product"], 2 * j)
                        s.activation(XF[b][:, :], pX[b][:, :], ACT.Copy)
                        s.activation(RF[b][:, :], pR[b][:, :], ACT.Copy).then_inc(e["flat"], 1)
                    for b in range(2):
                        act.wait_ge(e["product"], last_of(j, b))
                        act.wait_ge(out_sems[b], 32 * j)
                        act.wait_ge(e["weighed"], 2 * j)
                        s.activation(U[b][:, :], pH[b][:, :], ACT.Relu).then_inc(e["relu"], 1)
                    for b in range(2):
                        act.wait_ge(e["relu"], last_of(j, b))
                        s.activation(Q[b][:, :], U[b][:, :], ACT.Square).then_inc(e["sq"], 1)
                    for b in range(2):
                        act.wait_ge(e["clamped"], last_of(j, b))
                        s.activation(st[b][:, 1, :], st[b][:, 0, :], ACT.Ln, scale=2.0 ** 20).then_inc(e["ln"], 1)
                    for b in range(2):
                        act.wait_ge(e["ln"], last_of(j, b))
                        s.activation(st[b][:, 1, :], st[b][:, 1, :], ACT.Exp, scale=-0.5, bias=k.eps[:, 2:3])\
                            .then_inc(e["inv"], 1)
                    for b in range(2):
                        act.wait_ge(e["cen"], last_of(j, b))
                        s.activation(Q[b][:, :], U[b][:, :], ACT.Square).then_inc(e["sq2"], 1)
                    for b in range(2):
                        act.wait_ge(e["sumsq2"], last_of(j, b))
                        s.activation(st[b][:, 3, :], st[b][:, 3, :], ACT.Ln, scale=1.0 / C, bias=k.eps[:, 0:1])\
                            .then_inc(e["ln2"], 1)
                    for b in range(2):
                        act.wait_ge(e["ln2"], last_of(j, b))
                        s.activation(st[b][:, 4, :], st[b][:, 3, :], ACT.Exp, scale=-0.5).then_inc(e["dev"], 1)

            @block.vector
            def _(dve):
                v = nc.vector
                U8 = lambda b: groups(U[b][:, :], 2 * CT)
                with dve.Fori(0, ITERS) as j:
                    for b in range(2):
                        dve.wait_ge(e["sq"], last_of(j, b))
                        v.tensor_reduce(out=st[b][:, 0, :], in_=groups(Q[b][:, :], 2 * CT), op=ALU.add, axis=AX)\
                            .then_inc(e["sumsq"], 1)
                    for b in range(2):
                        dve.wait_ge(e["sumsq"], last_of(j, b))
                        v.tensor_scalar(st[b][:, 0, :], st[b][:, 0, :], 1e-24, None, ALU.max).then_inc(e["clamped"], 1)
                    for b in range(2):
                        dve.wait_ge(e["inv"], last_of(j, b))
                        v.tensor_tensor(U8(b), U8(b), over(st[b][:, 1, :], C), ALU.mult).then_inc(e["scaled"], 1)
                    for b in range(2):
                        dve.wait_ge(e["scaled"], last_of(j, b))
                        v.tensor_tensor(U8(b)[:, 0:CT, :], U8(b)[:, 0:CT, :], ends(X[b])[:, :, 0, :], ALU.add)
                        v.tensor_tensor(U8(b)[:, CT:2 * CT, :], U8(b)[:, CT:2 * CT, :], groups(R[b][:, :], CT), ALU.add)\
                            .then_inc(e["added"], 1)
                    for b in range(2):
                        dve.wait_ge(e["added"], last_of(j, b))
                        v.tensor_reduce(out=st[b][:, 2, :], in_=U8(b), op=ALU.add, axis=AX).then_inc(e["sum"], 1)
                    for b in range(2):
                        dve.wait_ge(e["sum"], last_of(j, b))
                        v.scalar_tensor_tensor(U8(b), over(st[b][:, 2, :], C), -1.0 / C, U8(b), ALU.mult, ALU.add)\
                            .then_inc(e["cen"], 1)
                    for b in range(2):
                        dve.wait_ge(e["sq2"], last_of(j, b))
                        v.tensor_reduce(out=st[b][:, 3, :], in_=groups(Q[b][:, :], 2 * CT), op=ALU.add, axis=AX)\
                            .then_inc(e["sumsq2"], 1)
                    for b in range(2):
                        dve.wait_ge(e["dev"], last_of(j, b))
                        v.tensor_tensor(U8(b), U8(b), over(st[b][:, 4, :], C), ALU.mult).then_inc(e["norm"], 1)
                    for b in range(2):
                        dve.wait_ge(e["norm"], last_of(j, b))
                        v.tensor_tensor(groups(T[b][:, :], CT), U8(b)[:, 0:CT, :],
                                        k.w_att_d[:, :].unsqueeze(1).to_broadcast([P, CT, C]), ALU.mult)\
                            .then_inc(e["weighed"], 1)
                    for b in range(2):
                        dve.wait_ge(e["weighed"], last_of(j, b))
                        dve.sem_inc(e["passed"], 1)
                        v.tensor_reduce(out=dot[:, bass.ds((2 * j + b) * CT, CT)], in_=groups(T[b][:, :], CT),
                                        op=ALU.add, axis=AX).then_inc(e["dot"], 1)
                left = lambda ap: ap[:, ::-1]
                v.memset(zero[:, :], 0.0)
                v.memset(crow[:, 2, Q2:Q2 + 1], 0.0)
                v.tensor_scalar(more[:, :], k.lastq[:, :], -1.0, 1.0, ALU.mult, ALU.add).then_inc(e["tail"], 1)
                dve.wait_ge(e["tail_pe"], 1)
                v.tensor_copy(dvq[:, :], pX[1][0:Q2, 0:2 * P]).then_inc(e["tail"], 1)
                v.tensor_tensor(dq[:, :], pX[0][0:Q2, 0:2 * P], k.lastq[:, :], ALU.mult).then_inc(e["tail"], 1)
                dve.wait_ge(e["tail"], 3)
                v.tensor_tensor_scan(left(cum[:, :]), left(more[:, :]), left(zero[:, :]), 1.0, ALU.mult, ALU.add)\
                    .then_inc(e["tail"], 1)
                v.tensor_tensor_scan(left(dq[:, :]), left(more[:, :]), left(dq[:, :]), 0.0, ALU.mult, ALU.add)\
                    .then_inc(e["tail"], 1)
                dve.wait_ge(e["tail_pe"], 2)
                v.tensor_copy(crow[:, 0, 0:Q2], pR[0][0:1, 0:Q2])
                v.tensor_copy(crow[:, 1, 0:Q2], pR[1][0:1, 0:Q2]).then_inc(e["tail"], 1)
                dve.wait_ge(e["tail"], 6)
                v.tensor_tensor_scan(left(crow[:, 2, 0:Q2]), left(crow[:, 1, 0:Q2]), left(crow[:, 0, 0:Q2]), 0.0,
                                     ALU.mult, ALU.add).then_inc(e["tail"], 1)
                dve.wait_ge(e["tail"], 7)
                v.tensor_scalar(dq[:, :], dq[:, :], k.b_att[0:Q2, 0:1], None, ALU.add).then_inc(e["tail"], 1)
                dve.wait_ge(e["tail"], 8)
                dve.wait_ge(e["tail_pe"], 3)
                v.tensor_copy(more[:, 0:1], pH[0][0:Q2, 0:1]).then_inc(e["tail"], 1)
                dve.wait_ge(e["tail"], 9)
                v.scalar_tensor_tensor(dq[:, :], cum[:, :], more[:, 0:1], dq[:, :], ALU.mult, ALU.add)\
                    .then_inc(e["ready"], 1)


def attention2_stage(nc, k):
    with Stage(nc, "a2") as g:
        pairs = lambda name, shape, dt=F32: [g.sb(f"{name}{b}", shape, dt) for b in range(2)]
        idx = pairs("idx", [P, CT], I32)
        landing = pairs("landing", [P, CT * C])
        W = pairs("W", [P, CE])
        D = pairs("D", [P, CT * C])
        AD = pairs("AD", [P, CE])
        XF = pairs("XF", [P, CE])
        anew = pairs("anew", [P, CE])
        L = pairs("L", [P, CE])
        M = pairs("M", [P, CE + 1])
        A = pairs("A", [P, CE])
        S = pairs("S", [P, CE])
        Y = pairs("Y", [P, 2 * CT * C])
        Q = pairs("Q", [P, 2 * CT * C])
        T = pairs("T", [P, CT * C])
        st = pairs("st", [P, 3, 2 * CT])
        pA = [g.ps(f"pA{b}", [P, CE]) for b in range(2)]
        pL = [g.ps(f"pL{b}", [P, CE]) for b in range(2)]
        landed = g.pair("landed"); got = g.pair("got"); copied = g.pair("copied")
        own_in = g.pair("own_in"); rows_out = g.pair("rows_out")
        e = {n: g.sem(n) for n in ("staged", "passed", "starts", "turned", "ends", "own", "anew", "product", "sum1",
                                   "logits", "maxed", "shifted", "diffs", "weights", "weighed", "summed", "back",
                                   "recip", "ratio", "added", "sum", "cen", "sq", "sumsq", "ln", "dev", "norm", "over")}
        sems = dict(staged=e["staged"], passed=e["passed"], landed=landed, got=got, copied=copied)
        high = slice(C, P)
        with nc.Block() as block:

            @block.gpsimd
            def _(pool):
                override_rows(nc, pool, k, k.d2, C, idx, landing, sems, ITERS, pool.to_reg(EP - 1))

            @block.sync
            def _(sp):
                def load(j, used=True):
                    for b in range(2):
                        i = 2 * j + b
                        if used:
                            sp.wait_ge(copied[b], 16 * j)
                        sp.dma_start(groups(landing[b][:, :], CT), one(by_chunk(k.s2), i)).then_inc(landed[b], 16)
                    for b in range(2):
                        i = 2 * j + b
                        if used:
                            sp.wait_ge(e["added"], last_of(j - 1, b))
                        sp.dma_start(groups(D[b][:, :], CT), one(by_chunk(k.d2), i)).then_inc(own_in[b], 16)
                        sp.dma_start(AD[b][:, :], row(k.att_d[bass.ds(i * CE, CE)], CE).to_broadcast([P, CE]))\
                            .then_inc(own_in[b], 16)
                    for b in range(2):
                        sp.wait_ge(got[b], 16 * CT * j + 16 * CT)
                        if used:
                            sp.wait_ge(e["own"], last_of(j - 1, b))
                            sp.wait_ge(e["turned"], last_of(j - 1, b))
                        sp.dma_start(ends(W[b])[:, :, 1, :], groups(landing[b][:, :], CT)).then_inc(copied[b], 16)

                def store(j):
                    for b in range(2):
                        i = 2 * j + b
                        sp.wait_ge(e["norm"], last_of(j, b))
                        sp.dma_start(one(by_chunk(k.x3), i), groups(Y[b][:, 0:CT * C], CT)).then_inc(rows_out[b], 16)
                        sp.dma_start(one(by_chunk(k.s3), i), groups(Y[b][:, CT * C:], CT)).then_inc(rows_out[b], 16)
                    for b in range(2):
                        i = 2 * j + b
                        sp.wait_ge(e["over"], last_of(j, b))
                        sp.dma_start(one(by_chunk(k.d3), i), groups(T[b][:, :], CT)).then_inc(rows_out[b], 16)

                sp.wait_ge(e["starts"], 2)
                load(0, used=False)
                with sp.Fori(0, ITERS - 1) as j:
                    load(j + 1)
                    store(j)
                store(ITERS - 1)
                for b in range(2):
                    sp.wait_ge(rows_out[b], 48 * ITERS)

            @block.tensor
            def _(pe):
                t = nc.tensor
                with pe.Fori(0, ITERS) as j:
                    for b in range(2):
                        pe.wait_ge(copied[b], 16 * j + 16)
                        pe.wait_ge(e["ratio"], 2 * j)
                        for n in range(CT):
                            i = t.transpose(pA[b][:, n * P:n * P + P], W[b][:, n * P:n * P + P], k.ident[:, :])
                        i.then_inc(e["turned"], 1)
                    for b in range(2):
                        pe.wait_ge(e["ends"], last_of(j, b))
                        t.matmul(pL[b][:, :], k.w_att_s[:, :], XF[b][:, :], start=True, stop=True)\
                            .then_inc(e["product"], 1)
                    for b in range(2):
                        pe.wait_ge(e["summed"], last_of(j, b))
                        for n in range(CT):
                            i = t.transpose(pA[b][:, n * P:n * P + P], S[b][:, n * P:n * P + P], k.ident[:, :])
                        i.then_inc(e["back"], 1)

            @block.scalar
            def _(act):
                s = nc.scalar
                s.preload_act_table_set(LN_EXP)
                with act.Fori(0, ITERS) as j:
                    for b in range(2):
                        act.wait_ge(e["turned"], last_of(j, b))
                        act.wait_ge(e["weighed"], 2 * j)
                        s.activation(XF[b][:, :], pA[b][:, :], ACT.Copy).then_inc(e["ends"], 1)
                    for b in range(2):
                        act.wait_ge(copied[b], 16 * j + 16)
                        act.wait_ge(rows_out[b], 48 * j)
                        s.activation(groups(Y[b][:, CT * C:], CT), ends(W[b])[:, :, 1, :], ACT.Copy)\
                            .then_inc(e["own"], 1)
                    for b in range(2):
                        act.wait_ge(e["diffs"], 2 * j)
                        s.activation(anew[b][:, :], k.same[:, bass.ds((2 * j + b) * CE, CE)], ACT.Copy,
                                     scale=BIG, bias=-BIG).then_inc(e["anew"], 1)
                    for b in range(2):
                        act.wait_ge(e["diffs"], last_of(j, b))
                        s.activation(A[b][:, :], A[b][:, :], ACT.Exp)
                        s.activation(L[b][:, :], L[b][:, :], ACT.Exp).then_inc(e["weights"], 1)
                    for b in range(2):
                        act.wait_ge(e["cen"], last_of(j, b))
                        act.wait_ge(e["sumsq"], 2 * j)
                        s.activation(Q[b][:, :], Y[b][:, :], ACT.Square).then_inc(e["sq"], 1)
                    for b in range(2):
                        act.wait_ge(e["sumsq"], last_of(j, b))
                        s.activation(st[b][:, 1, :], st[b][:, 1, :], ACT.Ln, scale=1.0 / C, bias=k.eps[:, 0:1])\
                            .then_inc(e["ln"], 1)
                    for b in range(2):
                        act.wait_ge(e["ln"], last_of(j, b))
                        s.activation(st[b][:, 2, :], st[b][:, 1, :], ACT.Exp, scale=-0.5).then_inc(e["dev"], 1)

            @block.vector
            def _(dve):
                v = nc.vector
                Y8 = lambda b: groups(Y[b][:, :], 2 * CT)
                for b in range(2):
                    v.memset(W[b][:, :], 0.0).then_inc(e["starts"], 1)
                v.memset(M[1][:, :], -BIG).then_inc(e["starts"], 1)
                v.memset(S[1][:, :], 0.0).then_inc(e["starts"], 1)
                dve.wait_ge(e["starts"], 4)
                with dve.Fori(0, ITERS) as j:
                    for b in range(2):
                        dve.wait_ge(e["product"], last_of(j, b))
                        dve.wait_ge(own_in[b], 32 * j + 32)
                        v.tensor_tensor(L[b][:, :], pL[b][:, :], AD[b][:, :], ALU.add).then_inc(e["sum1"], 1)
                    for b in range(2):
                        dve.wait_ge(e["sum1"], last_of(j, b))
                        v.scalar_tensor_tensor(L[b][:, :], L[b][:, :], 0.01, L[b][:, :], ALU.mult, ALU.max)\
                            .then_inc(e["logits"], 1)
                    for b in range(2):
                        dve.wait_ge(e["logits"], last_of(j, b))
                        v.tensor_copy(M[b][:, 0:1], M[1 - b][:, CE:CE + 1])
                        dve.wait_ge(e["anew"], last_of(j, b))
                        v.tensor_tensor_scan(M[b][:, 1:CE + 1], anew[b][:, :], L[b][:, :], M[1 - b][:, CE:CE + 1],
                                             ALU.add, ALU.max).then_inc(e["maxed"], 1)
                        dve.wait_ge(e["maxed"], last_of(j, b))
                    for b in range(2):
                        v.tensor_tensor(L[b][:, :], L[b][:, :], M[b][:, 1:CE + 1], ALU.subtract)
                        v.tensor_tensor(A[b][:, :], M[b][:, 0:CE], anew[b][:, :], ALU.add).then_inc(e["shifted"], 1)
                    for b in range(2):
                        dve.wait_ge(e["shifted"], last_of(j, b))
                        v.tensor_tensor(A[b][:, :], A[b][:, :], M[b][:, 1:CE + 1], ALU.subtract)\
                            .then_inc(e["diffs"], 1)
                    for b in range(2):
                        dve.wait_ge(e["weights"], last_of(j, b))
                        v.tensor_tensor(L[b][high, :], L[b][high, :], XF[b][high, :], ALU.mult)\
                            .then_inc(e["weighed"], 1)
                    for b in range(2):
                        dve.wait_ge(e["weighed"], last_of(j, b))
                        v.tensor_tensor_scan(S[b][:, :], A[b][:, :], L[b][:, :], S[1 - b][:, CE - 1:CE],
                                             ALU.mult, ALU.add).then_inc(e["summed"], 1)
                        dve.wait_ge(e["summed"], last_of(j, b))
                    for b in range(2):
                        dve.wait_ge(e["back"], last_of(j, b))
                        v.reciprocal(st[b][:, 0, 0:CT], ends(pA[b])[:, :, 0, 0]).then_inc(e["recip"], 1)
                    for b in range(2):
                        dve.wait_ge(e["recip"], last_of(j, b))
                        dve.wait_ge(rows_out[b], 48 * j)
                        v.tensor_tensor(Y8(b)[:, 0:CT, :], ends(pA[b])[:, :, 1, :], over(st[b][:, 0, 0:CT], C),
                                        ALU.mult).then_inc(e["ratio"], 1)
                    for b in range(2):
                        dve.wait_ge(e["ratio"], last_of(j, b))
                        v.tensor_tensor(Y8(b)[:, 0:CT, :], Y8(b)[:, 0:CT, :], groups(D[b][:, :], CT), ALU.add)\
                            .then_inc(e["added"], 1)
                    for b in range(2):
                        dve.wait_ge(e["added"], last_of(j, b))
                        dve.wait_ge(e["own"], last_of(j, b))
                        v.tensor_reduce(out=st[b][:, 0, :], in_=Y8(b), op=ALU.add, axis=AX).then_inc(e["sum"], 1)
                    for b in range(2):
                        dve.wait_ge(e["sum"], last_of(j, b))
                        v.scalar_tensor_tensor(Y8(b), over(st[b][:, 0, :], C), -1.0 / C, Y8(b), ALU.mult, ALU.add)\
                            .then_inc(e["cen"], 1)
                    for b in range(2):
                        dve.wait_ge(e["sq"], last_of(j, b))
                        v.tensor_reduce(out=st[b][:, 1, :], in_=groups(Q[b][:, :], 2 * CT), op=ALU.add, axis=AX)\
                            .then_inc(e["sumsq"], 1)
                    for b in range(2):
                        dve.wait_ge(e["dev"], last_of(j, b))
                        v.tensor_tensor(Y8(b), Y8(b), over(st[b][:, 2, :], C), ALU.mult).then_inc(e["norm"], 1)
                    for b in range(2):
                        dve.wait_ge(e["norm"], last_of(j, b))
                        v.tensor_tensor(groups(T[b][:, :], CT), Y8(b)[:, 0:CT, :],
                                        over(k.dinv[:, bass.ds((2 * j + b) * CT, CT)], C), ALU.mult)\
                            .then_inc(e["over"], 1)


def gcn1_stage(nc, k):
    with Stage(nc, "g1") as g:
        pairs = lambda name, shape, dt=F32: [g.sb(f"{name}{b}", shape, dt) for b in range(2)]
        idx = pairs("idx", [P, CT], I32)
        landing = pairs("landing", [P, CT * C])
        W = pairs("W", [P, CE])
        SF = pairs("SF", [C, CE])
        T = pairs("T", [P, CE])
        HS = pairs("HS", [P, CT * H])
        HD = pairs("HD", [P, CT * H])
        b1 = g.sb("b1", [1, CT, H])
        pA = [g.ps(f"pA{b}", [P, CE]) for b in range(2)]
        pS = [g.ps(f"pS{b}", [P, CT * H]) for b in range(2)]
        pD = [g.ps(f"pD{b}", [P, CT * H]) for b in range(2)]
        landed = g.pair("landed"); got = g.pair("got"); copied = g.pair("copied")
        own_in = g.pair("own_in"); rows_out = g.pair("rows_out")
        e = {n: g.sem(n) for n in ("staged", "passed", "starts", "turned", "flat", "summed", "product_s", "product_d",
                                   "relu_s", "scaled", "biased", "done_d")}
        sems = dict(staged=e["staged"], passed=e["passed"], landed=landed, got=got, copied=copied)
        with nc.Block() as block:

            @block.gpsimd
            def _(pool):
                override_rows(nc, pool, k, k.d3, C, idx, landing, sems, ITERS, pool.to_reg(EP - 1))

            @block.sync
            def _(sp):
                def load(j, used=True):
                    for b in range(2):
                        i = 2 * j + b
                        if used:
                            sp.wait_ge(copied[b], 16 * j)
                        sp.dma_start(groups(landing[b][:, :], CT), one(by_chunk(k.s3), i)).then_inc(landed[b], 16)
                    for b in range(2):
                        if used:
                            sp.wait_ge(e["turned"], last_of(j - 1, b))
                        sp.dma_start(ends(W[b])[:, :, 1, :], one(by_chunk(k.d3), 2 * j + b)).then_inc(own_in[b], 16)
                    for b in range(2):
                        sp.wait_ge(got[b], 16 * CT * j + 16 * CT)
                        sp.dma_start(ends(W[b])[:, :, 0, :], groups(landing[b][:, :], CT)).then_inc(copied[b], 16)

                def store(j):
                    for b in range(2):
                        sp.wait_ge(e["relu_s"], last_of(j, b))
                        sp.dma_start(one(by_chunk(k.s4), 2 * j + b), groups(HS[b][:, :], CT)).then_inc(rows_out[b], 16)
                    for b in range(2):
                        sp.wait_ge(e["done_d"], last_of(j, b))
                        sp.dma_start(one(by_chunk(k.d4), 2 * j + b), groups(HD[b][:, :], CT)).then_inc(rows_out[b], 16)

                load(0, used=False)
                with sp.Fori(0, ITERS - 1) as j:
                    load(j + 1)
                    store(j)
                store(ITERS - 1)
                for b in range(2):
                    sp.wait_ge(rows_out[b], 32 * ITERS)

            @block.tensor
            def _(pe):
                t = nc.tensor
                with pe.Fori(0, ITERS) as j:
                    for b in range(2):
                        pe.wait_ge(copied[b], 16 * j + 16)
                        pe.wait_ge(own_in[b], 16 * j + 16)
                        pe.wait_ge(e["summed"], 2 * j)
                        for n in range(CT):
                            i = t.transpose(pA[b][:, n * P:n * P + P], W[b][:, n * P:n * P + P], k.ident[:, :])
                        i.then_inc(e["turned"], 1)
                    for b in range(2):
                        pe.wait_ge(e["flat"], last_of(j, b))
                        pe.wait_ge(e["relu_s"], 2 * j)
                        pe.wait_ge(e["starts"], CT + 1)
                        t.matmul(pS[b][:, :], k.ones[0:1, :], b1[:, :, :].rearrange("a n c -> a (n c)"),
                                 start=True, stop=False, skip_group_check=True)
                        for n in range(CT):
                            i = t.matmul(pS[b][:, n * H:n * H + H], SF[b][:, n * P:n * P + P], k.w1[0:C, :],
                                         start=False, stop=n == CT - 1, skip_group_check=True)
                        i.then_inc(e["product_s"], 1)
                    for b in range(2):
                        pe.wait_ge(e["summed"], last_of(j, b))
                        pe.wait_ge(e["scaled"], 2 * j)
                        for n in range(CT):
                            i = t.matmul(pD[b][:, n * H:n * H + H], T[b][:, n * P:n * P + P], k.w1[:, :],
                                         start=True, stop=True)
                        i.then_inc(e["product_d"], 1)

            @block.scalar
            def _(act):
                s = nc.scalar
                with act.Fori(0, ITERS) as j:
                    for b in range(2):
                        act.wait_ge(e["turned"], last_of(j, b))
                        act.wait_ge(e["product_d"], 2 * j)
                        s.activation(SF[b][:, :], pA[b][0:C, :], ACT.Copy)
                        s.activation(T[b][C:P, :], pA[b][C:P, :], ACT.Copy).then_inc(e["flat"], 1)
                    for b in range(2):
                        act.wait_ge(e["product_s"], last_of(j, b))
                        act.wait_ge(rows_out[b], 32 * j)
                        s.activation(HS[b][:, :], pS[b][:, :], ACT.Relu).then_inc(e["relu_s"], 1)

            @block.vector
            def _(dve):
                v = nc.vector
                v.memset(T[1][0:C, :], 0.0).then_inc(e["starts"], 1)
                for n in range(CT):
                    v.tensor_copy(b1[:, n, :], k.b1row[0:1, :]).then_inc(e["starts"], 1)
                dve.wait_ge(e["starts"], CT + 1)
                with dve.Fori(0, ITERS) as j:
                    for b in range(2):
                        at = bass.ds((2 * j + b) * CE, CE)
                        dve.wait_ge(e["flat"], last_of(j, b))
                        v.tensor_tensor_scan(T[b][0:C, :], k.same[0:C, at], pA[b][0:C, :],
                                             T[1 - b][0:C, CE - 1:CE], ALU.mult, ALU.add).then_inc(e["summed"], 1)
                        dve.wait_ge(e["summed"], last_of(j, b))
                    dinv = lambda b: over(k.dinv[:, bass.ds((2 * j + b) * CT, CT)], H)
                    H4 = lambda b: groups(HD[b][:, :], CT)
                    for b in range(2):
                        dve.wait_ge(e["product_d"], last_of(j, b))
                        dve.wait_ge(rows_out[b], 32 * j)
                        v.tensor_tensor(H4(b), groups(pD[b][:, :], CT), dinv(b), ALU.mult).then_inc(e["scaled"], 1)
                    for b in range(2):
                        dve.wait_ge(e["scaled"], last_of(j, b))
                        v.tensor_tensor(H4(b), H4(b), k.b1row[:, :].unsqueeze(1).to_broadcast([P, CT, H]), ALU.add)\
                            .then_inc(e["biased"], 1)
                    for b in range(2):
                        dve.wait_ge(e["biased"], last_of(j, b))
                        v.scalar_tensor_tensor(H4(b), H4(b), 0.0, dinv(b), ALU.max, ALU.mult).then_inc(e["done_d"], 1)


def gcn2_stage(nc, k):
    with Stage(nc, "g2") as g:
        pairs = lambda name, shape, dt=F32: [g.sb(f"{name}{b}", shape, dt) for b in range(2)]
        idx = pairs("idx", [P, CT], I32)
        landing = pairs("landing", [P, CT * H])
        W = pairs("W", [P, CT * H])
        D = pairs("D", [P, CT * H])
        DR = pairs("DR", [P, CE])
        WF = pairs("WF", [P, CE])
        DF = pairs("DF", [P, CE])
        S = pairs("S", [P, CE])
        HS = pairs("HS", [P, CE])
        HD = pairs("HD", [P, CE])
        Z = pairs("Z", [P, 2 * CT * C])
        pA = [g.ps(f"pA{b}", [P, CE]) for b in range(2)]
        pB = [g.ps(f"pB{b}", [P, CE]) for b in range(2)]
        pS = [g.ps(f"pS{b}", [P, CE]) for b in range(2)]
        pD = [g.ps(f"pD{b}", [P, CE]) for b in range(2)]
        landed = g.pair("landed"); got = g.pair("got"); copied = g.pair("copied")
        own_in = g.pair("own_in"); rows_out = g.pair("rows_out")
        e = {n: g.sem(n) for n in ("staged", "passed", "starts", "turned_s", "turned_d", "flat_s", "flat_d", "summed",
                                   "product_s", "product_d", "relu_s", "scaled", "relu_d", "third", "z_s", "z_d")}
        sems = dict(staged=e["staged"], passed=e["passed"], landed=landed, got=got, copied=copied)
        with nc.Block() as block:

            @block.gpsimd
            def _(pool):
                override_rows(nc, pool, k, k.d4, H, idx, landing, sems, ITERS, pool.to_reg(EP - 1))

            @block.sync
            def _(sp):
                def load(j, used=True):
                    for b in range(2):
                        i = 2 * j + b
                        if used:
                            sp.wait_ge(copied[b], 16 * j)
                        sp.dma_start(groups(landing[b][:, :], CT), one(by_chunk(k.s4), i)).then_inc(landed[b], 16)
                    for b in range(2):
                        i = 2 * j + b
                        if used:
                            sp.wait_ge(e["scaled"], last_of(j - 1, b))
                            sp.wait_ge(e["turned_d"], last_of(j - 1, b))
                        sp.dma_start(groups(D[b][:, :], CT), one(by_chunk(k.d4), i)).then_inc(own_in[b], 16)
                        sp.dma_start(DR[b][:, :], row(k.dinv_row[bass.ds(i * CE, CE)], CE).to_broadcast([P, CE]))\
                            .then_inc(own_in[b], 16)
                    for b in range(2):
                        sp.wait_ge(got[b], 16 * CT * j + 16 * CT)
                        if used:
                            sp.wait_ge(e["turned_s"], last_of(j - 1, b))
                        sp.dma_start(W[b][:, :], landing[b][:, :]).then_inc(copied[b], 16)

                def store(j):
                    for b in range(2):
                        i = 2 * j + b
                        sp.wait_ge(e["z_s"], last_of(j, b))
                        sp.wait_ge(e["z_d"], last_of(j, b))
                        sp.dma_start(one(by_chunk(k.d5), i), groups(Z[b][:, 0:CT * C], CT)).then_inc(rows_out[b], 16)
                        sp.dma_start(one(by_chunk(k.s5), i), groups(Z[b][:, CT * C:], CT)).then_inc(rows_out[b], 16)

                load(0, used=False)
                with sp.Fori(0, ITERS - 1) as j:
                    load(j + 1)
                    store(j)
                store(ITERS - 1)
                for b in range(2):
                    sp.wait_ge(rows_out[b], 32 * ITERS)

            @block.tensor
            def _(pe):
                t = nc.tensor
                with pe.Fori(0, ITERS) as j:
                    for b in range(2):
                        pe.wait_ge(own_in[b], 32 * j + 32)
                        pe.wait_ge(e["flat_d"], 2 * j)
                        for n in range(CT):
                            i = t.transpose(pB[b][:, n * P:n * P + P], D[b][:, n * P:n * P + P], k.ident[:, :])
                        i.then_inc(e["turned_d"], 1)
                    for b in range(2):
                        pe.wait_ge(copied[b], 16 * j + 16)
                        pe.wait_ge(e["z_s"], 2 * j)
                        pe.wait_ge(e["z_d"], 2 * j)
                        for n in range(CT):
                            i = t.transpose(pA[b][:, n * P:n * P + P], W[b][:, n * P:n * P + P], k.ident[:, :])
                        i.then_inc(e["turned_s"], 1)
                    for b in range(2):
                        pe.wait_ge(e["flat_s"], last_of(j, b))
                        pe.wait_ge(e["relu_s"], 2 * j)
                        t.matmul(pS[b][:, :], k.w2[:, :], WF[b][:, :], start=True, stop=True)\
                            .then_inc(e["product_s"], 1)
                    for b in range(2):
                        pe.wait_ge(e["summed"], last_of(j, b))
                        pe.wait_ge(e["flat_d"], last_of(j, b))
                        pe.wait_ge(e["scaled"], 2 * j)
                        t.matmul(pD[b][:, :], k.w2[:, :], S[b][:, :], start=True, stop=False)
                        t.matmul(pD[b][:, :], k.w2[:, :], DF[b][:, :], start=False, stop=True)\
                            .then_inc(e["product_d"], 1)
                    for b in range(2):
                        pe.wait_ge(e["relu_s"], last_of(j, b))
                        pe.wait_ge(e["relu_d"], last_of(j, b))
                        for n in range(2 * CT):
                            h = HD[b] if n < CT else HS[b]
                            i = t.matmul(pA[b][:, n * C:n * C + C], h[:, n % CT * P:n % CT * P + P], k.w3[:, :],
                                         start=True, stop=True)
                        i.then_inc(e["third"], 1)

            @block.scalar
            def _(act):
                s = nc.scalar
                with act.Fori(0, ITERS) as j:
                    for b in range(2):
                        act.wait_ge(e["turned_d"], last_of(j, b))
                        act.wait_ge(e["product_d"], 2 * j)
                        s.activation(DF[b][:, :], pB[b][:, :], ACT.Copy).then_inc(e["flat_d"], 1)
                    for b in range(2):
                        act.wait_ge(e["turned_s"], last_of(j, b))
                        act.wait_ge(e["product_s"], 2 * j)
                        s.activation(WF[b][:, :], pA[b][:, :], ACT.Copy).then_inc(e["flat_s"], 1)
                    for b in range(2):
                        act.wait_ge(e["product_s"], last_of(j, b))
                        act.wait_ge(e["third"], 2 * j)
                        s.activation(HS[b][:, :], pS[b][:, :], ACT.Relu, bias=k.col[:, 5:6]).then_inc(e["relu_s"], 1)
                    for b in range(2):
                        act.wait_ge(e["scaled"], last_of(j, b))
                        s.activation(HD[b][:, :], HD[b][:, :], ACT.Relu, bias=k.col[:, 5:6]).then_inc(e["relu_d"], 1)
                    for b in range(2):
                        act.wait_ge(e["third"], last_of(j, b))
                        act.wait_ge(rows_out[b], 32 * j)
                        s.activation(Z[b][:, CT * C:], pA[b][:, CT * C:], ACT.Copy).then_inc(e["z_s"], 1)

            @block.vector
            def _(dve):
                v = nc.vector
                v.memset(S[1][:, :], 0.0).then_inc(e["starts"], 1)
                dve.wait_ge(e["starts"], 1)
                with dve.Fori(0, ITERS) as j:
                    for b in range(2):
                        at = bass.ds((2 * j + b) * CE, CE)
                        dve.wait_ge(e["flat_s"], last_of(j, b))
                        v.tensor_tensor_scan(S[b][:, :], k.same[:, at], pA[b][:, :], S[1 - b][:, CE - 1:CE],
                                             ALU.mult, ALU.add).then_inc(e["summed"], 1)
                        dve.wait_ge(e["summed"], last_of(j, b))
                    for b in range(2):
                        dve.wait_ge(e["product_d"], last_of(j, b))
                        v.tensor_tensor(HD[b][:, :], pD[b][:, :], DR[b][:, :], ALU.mult).then_inc(e["scaled"], 1)
                    for b in range(2):
                        dve.wait_ge(e["z_s"], last_of(j, b))
                        v.tensor_tensor(groups(Z[b][:, 0:CT * C], CT), groups(pA[b][:, 0:CT * C], CT),
                                        over(k.dinv[:, bass.ds((2 * j + b) * CT, CT)], C), ALU.mult)\
                            .then_inc(e["z_d"], 1)


def output_stage(nc, k, out):
    with Stage(nc, "ou") as g:
        pairs = lambda name, shape, dt=F32: [g.sb(f"{name}{b}", shape, dt) for b in range(2)]
        idx = pairs("idx", [P, CT], I32)
        put = pairs("put", [P, CT], I32)
        landing = pairs("landing", [P, CT * C])
        W = pairs("W", [P, CE])
        T = pairs("T", [P, CE])
        X3 = pairs("X3", [P, CT * C])
        O = pairs("O", [P, CT * C])
        Q = pairs("Q", [P, CT * C])
        F = pairs("F", [P, CT * C])
        st = pairs("st", [P, 4, CT])
        twice = g.sb("twice", [P, C])
        pA = [g.ps(f"pA{b}", [P, CE]) for b in range(2)]
        pO = [g.ps(f"pO{b}", [P, CT * C]) for b in range(2)]
        landed = g.pair("landed"); got = g.pair("got"); copied = g.pair("copied")
        own_in = g.pair("own_in"); scattered = g.pair("scattered")
        e = {n: g.sem(n) for n in ("staged", "passed", "starts", "turned", "flat", "summed", "totals", "scaled", "biased",
                                   "max", "less", "exp", "esum", "erec", "soft", "added", "sum", "cen", "sq", "sumsq",
                                   "ln", "dev", "norm", "put")}
        gp = nc.gpsimd
        with nc.Block() as block:

            @block.gpsimd
            def _(pool):
                in_tables, in_out = pool.to_reg(EP - 1), pool.to_reg(N - 1)

                def gather(j):
                    for b in range(2):
                        if not isinstance(j, int):
                            pool.wait_ge(copied[b], 16 * j)
                        gp.tensor_copy(idx[b][:, :], k.pos[:, bass.ds((2 * j + b) * CT, CT)])\
                            .then_inc(e["staged"], 1)
                    for b in range(2):
                        pool.wait_ge(e["staged"], last_of(j, b))
                        pool.wait_ge(landed[b], 16 * j + 16)
                        pool.sem_inc(e["passed"], 1)
                        for t in range(CT):
                            gp.indirect_dma_start(out=landing[b][:, t * C:(t + 1) * C], out_offset=None, in_=k.d5,
                                                  in_offset=bass.IndirectOffsetOnAxis(ap=idx[b][:, t:t + 1], axis=0),
                                                  bounds_check=in_tables, oob_is_err=False).then_inc(got[b], 16)

                def scatter(j):
                    for b in range(2):
                        pool.wait_ge(scattered[b], 16 * CT * j)
                        gp.tensor_copy(put[b][:, :], k.put[:, bass.ds((2 * j + b) * CT, CT)]).then_inc(e["put"], 1)
                    for b in range(2):
                        pool.wait_ge(e["put"], last_of(j, b))
                        pool.wait_ge(e["norm"], last_of(j, b))
                        pool.sem_inc(e["passed"], 1)
                        for t in range(CT):
                            gp.indirect_dma_start(out=out, out_offset=bass.IndirectOffsetOnAxis(
                                ap=put[b][:, t:t + 1], axis=0), in_=F[b][:, t * C:(t + 1) * C], in_offset=None,
                                bounds_check=in_out, oob_is_err=False).then_inc(scattered[b], 16)

                gather(0)
                with pool.Fori(0, ITERS - 1) as j:
                    gather(j + 1)
                    scatter(j)
                scatter(ITERS - 1)
                for b in range(2):
                    pool.wait_ge(scattered[b], 16 * CT * ITERS)

            @block.sync
            def _(sp):
                def load(j, used=True):
                    for b in range(2):
                        if used:
                            sp.wait_ge(copied[b], 16 * j)
                        sp.dma_start(groups(landing[b][:, :], CT), one(by_chunk(k.s5), 2 * j + b))\
                            .then_inc(landed[b], 16)
                    for b in range(2):
                        i = 2 * j + b
                        if used:
                            sp.wait_ge(e["turned"], last_of(j - 1, b))
                        sp.dma_start(ends(W[b])[:, :, 1, :], one(by_chunk(k.d5), i)).then_inc(own_in[b], 16)
                        if used:
                            sp.wait_ge(e["added"], last_of(j - 1, b))
                        sp.dma_start(groups(X3[b][:, :], CT), one(by_chunk(k.x3), i)).then_inc(own_in[b], 16)
                    for b in range(2):
                        sp.wait_ge(got[b], 16 * CT * j + 16 * CT)
                        sp.dma_start(ends(W[b])[:, :, 0, :], groups(landing[b][:, :], CT)).then_inc(copied[b], 16)

                load(0, used=False)
                with sp.Fori(1, ITERS) as j:
                    load(j)

            @block.tensor
            def _(pe):
                t = nc.tensor
                with pe.Fori(0, ITERS) as j:
                    for b in range(2):
                        pe.wait_ge(copied[b], 16 * j + 16)
                        pe.wait_ge(own_in[b], 32 * j + 32)
                        pe.wait_ge(e["summed"], 2 * j)
                        for n in range(CT):
                            i = t.transpose(pA[b][:, n * P:n * P + P], W[b][:, n * P:n * P + P], k.ident[:, :])
                        i.then_inc(e["turned"], 1)
                    for b in range(2):
                        pe.wait_ge(e["summed"], last_of(j, b))
                        pe.wait_ge(e["starts"], 3)
                        pe.wait_ge(e["scaled"], 2 * j)
                        for n in range(CT):
                            i = t.matmul(pO[b][:, n * C:n * C + C], T[b][:, n * P:n * P + P], twice[:, :],
                                         start=True, stop=True)
                        i.then_inc(e["totals"], 1)

            @block.scalar
            def _(act):
                s = nc.scalar
                s.preload_act_table_set(LN_EXP)
                with act.Fori(0, ITERS) as j:
                    for b in range(2):
                        act.wait_ge(e["turned"], last_of(j, b))
                        act.wait_ge(e["totals"], 2 * j)
                        s.activation(T[b][C:P, :], pA[b][C:P, :], ACT.Copy).then_inc(e["flat"], 1)
                    for b in range(2):
                        act.wait_ge(e["less"], last_of(j, b))
                        s.activation(O[b][:, :], O[b][:, :], ACT.Exp).then_inc(e["exp"], 1)
                    for b in range(2):
                        act.wait_ge(e["cen"], last_of(j, b))
                        act.wait_ge(e["sumsq"], 2 * j)
                        s.activation(Q[b][:, :], O[b][:, :], ACT.Square).then_inc(e["sq"], 1)
                    for b in range(2):
                        act.wait_ge(e["sumsq"], last_of(j, b))
                        s.activation(st[b][:, 2, :], st[b][:, 2, :], ACT.Ln, scale=1.0 / C, bias=k.eps[:, 0:1])\
                            .then_inc(e["ln"], 1)
                    for b in range(2):
                        act.wait_ge(e["ln"], last_of(j, b))
                        s.activation(st[b][:, 3, :], st[b][:, 2, :], ACT.Exp, scale=-0.5).then_inc(e["dev"], 1)

            @block.vector
            def _(dve):
                v = nc.vector
                O4 = lambda b: groups(O[b][:, :], CT)
                v.memset(T[1][0:C, :], 0.0).then_inc(e["starts"], 1)
                v.tensor_copy(twice[0:C, :], k.ident[0:C, 0:C]).then_inc(e["starts"], 1)
                v.tensor_copy(twice[C:P, :], k.ident[C:P, C:P]).then_inc(e["starts"], 1)
                dve.wait_ge(e["starts"], 3)
                with dve.Fori(0, ITERS) as j:
                    for b in range(2):
                        at = bass.ds((2 * j + b) * CE, CE)
                        dve.wait_ge(e["flat"], last_of(j, b))
                        v.tensor_tensor_scan(T[b][0:C, :], k.same[0:C, at], pA[b][0:C, :],
                                             T[1 - b][0:C, CE - 1:CE], ALU.mult, ALU.add).then_inc(e["summed"], 1)
                        dve.wait_ge(e["summed"], last_of(j, b))
                    for b in range(2):
                        dve.wait_ge(e["totals"], last_of(j, b))
                        v.tensor_tensor(O4(b), groups(pO[b][:, :], CT),
                                        over(k.dinv[:, bass.ds((2 * j + b) * CT, CT)], C), ALU.mult)\
                            .then_inc(e["scaled"], 1)
                    for b in range(2):
                        dve.wait_ge(e["scaled"], last_of(j, b))
                        v.tensor_tensor(O4(b), O4(b), k.b3[:, :].unsqueeze(1).to_broadcast([P, CT, C]), ALU.add)\
                            .then_inc(e["biased"], 1)
                    for b in range(2):
                        dve.wait_ge(e["biased"], last_of(j, b))
                        v.tensor_reduce(out=st[b][:, 0, :], in_=O4(b), op=ALU.max, axis=AX).then_inc(e["max"], 1)
                    for b in range(2):
                        dve.wait_ge(e["max"], last_of(j, b))
                        v.tensor_tensor(O4(b), O4(b), over(st[b][:, 0, :], C), ALU.subtract).then_inc(e["less"], 1)
                    for b in range(2):
                        dve.wait_ge(e["exp"], last_of(j, b))
                        v.tensor_reduce(out=st[b][:, 1, :], in_=O4(b), op=ALU.add, axis=AX).then_inc(e["esum"], 1)
                    for b in range(2):
                        dve.wait_ge(e["esum"], last_of(j, b))
                        v.reciprocal(st[b][:, 0, :], st[b][:, 1, :]).then_inc(e["erec"], 1)
                    for b in range(2):
                        dve.wait_ge(e["erec"], last_of(j, b))
                        v.tensor_tensor(O4(b), O4(b), over(st[b][:, 0, :], C), ALU.mult).then_inc(e["soft"], 1)
                    for b in range(2):
                        dve.wait_ge(e["soft"], last_of(j, b))
                        v.tensor_tensor(O4(b), O4(b), groups(X3[b][:, :], CT), ALU.add).then_inc(e["added"], 1)
                    for b in range(2):
                        dve.wait_ge(e["added"], last_of(j, b))
                        v.tensor_reduce(out=st[b][:, 1, :], in_=O4(b), op=ALU.add, axis=AX).then_inc(e["sum"], 1)
                    for b in range(2):
                        dve.wait_ge(e["sum"], last_of(j, b))
                        v.scalar_tensor_tensor(O4(b), over(st[b][:, 1, :], C), -1.0 / C, O4(b), ALU.mult, ALU.add)\
                            .then_inc(e["cen"], 1)
                    for b in range(2):
                        dve.wait_ge(e["sq"], last_of(j, b))
                        v.tensor_reduce(out=st[b][:, 2, :], in_=groups(Q[b][:, :], CT), op=ALU.add, axis=AX)\
                            .then_inc(e["sumsq"], 1)
                    for b in range(2):
                        dve.wait_ge(e["dev"], last_of(j, b))
                        dve.wait_ge(scattered[b], 16 * CT * j)
                        v.tensor_tensor(groups(F[b][:, :], CT), O4(b), over(st[b][:, 3, :], C), ALU.mult)\
                            .then_inc(e["norm"], 1)


def dense_stage(nc, k, out):
    with Stage(nc, "de") as g:
        pairs = lambda name, shape, dt=F32: [g.sb(f"{name}{b}", shape, dt) for b in range(2)]
        G, F = NODE_ROWS, NODE_ROWS * C
        X = [pairs(f"X{w}", [P, F]) for w in range(2)]
        XF = pairs("XF", [P, F])
        U = pairs("U", [P, F])
        Q = pairs("Q", [P, F])
        X3 = [pairs(f"X3{w}", [P, F]) for w in range(2)]
        UF = pairs("UF", [P, F])
        H1 = pairs("H1", [P, 2, F])
        H2 = pairs("H2", [P, 2, F])
        ZF = pairs("ZF", [P, F])
        O = [pairs(f"O{w}", [P, F]) for w in range(2)]
        R = pairs("R", [P, F])
        st = pairs("st", [P, 9, G])
        pX = [g.ps(f"pX{b}", [P, F]) for b in range(2)]
        pU = [g.ps(f"pU{b}", [P, F]) for b in range(2)]
        pH = [[g.ps(f"pH{b}{h}", [P, F]) for h in range(2)] for b in range(2)]
        x_in = [g.pair(f"x_in{w}_") for w in range(2)]; o_out = [g.pair(f"o_out{w}_") for w in range(2)]
        e = {n: g.sem(n) for n in (
            "turned", "flat", "product", "relu", "sq", "sumsq", "clamped", "ln", "inv", "scaled", "added", "sum", "cen",
            "sq2", "sumsq2", "ln2", "dev", "norm", "turned3", "flat3", "first0", "first1", "hid0", "hid1", "second0",
            "second1", "deep0", "deep1", "third", "zflat", "back", "max", "less", "exp", "esum", "erec", "soft", "mixed",
            "sq4", "sumsq4", "ln4", "dev4", "norm4")}
        last = D_FULL // 2
        assert D_FULL % 2 == 1 and last % 2 == 0

        def sizes(q):
            return (P, D_REST) if isinstance(q, int) and q == last else (P, P)

        def schedule(eng, step):
            step(0, None, None, 1)
            step(1, 0, None, 0)
            with eng.Fori(0, last // 2 - 1) as j:
                step(2 * j + 2, 2 * j + 1, 2 * j, 1)
                step(2 * j + 3, 2 * j + 2, 2 * j + 1, 0)
            step(last, last - 1, last - 2, 1)
            step(None, last, last - 1, 0)
            step(None, None, last, 1)

        with nc.Block() as block:

            @block.sync
            def _(sp):
                def load(q, w):
                    for b in range(2):
                        if not isinstance(q, int) or q >= 2:
                            sp.wait_ge(e["added"], 2 * q - 2)
                        p = sizes(q)[b]
                        sp.dma_start(X[w][b][0:p, :], node_rows(k.x1, 2 * q + b, p)).then_inc(x_in[w][b], 16)

                def store(q, w):
                    for b in range(2):
                        p = sizes(q)[b]
                        sp.wait_ge(e["norm4"], last_of(q, b))
                        sp.dma_start(node_rows(out, 2 * q + b, p), O[w][b][0:p, :]).then_inc(o_out[w][b], 16)

                load(0, 0)
                load(1, 1)
                load(2, 0)
                with sp.Fori(0, last // 2 - 2) as j:
                    load(2 * j + 3, 1)
                    store(2 * j, 0)
                    load(2 * j + 4, 0)
                    store(2 * j + 1, 1)
                load(last - 1, 1)
                store(last - 4, 0)
                load(last, 0)
                for q in range(last - 3, last + 1):
                    store(q, q % 2)
                for b in range(2):
                    sp.wait_ge(o_out[0][b], 16 * (last // 2 + 1))
                    sp.wait_ge(o_out[1][b], 16 * (last // 2))

            @block.tensor
            def _(pe):
                t = nc.tensor

                def step(q, r, s, w):
                    if q is not None:
                        for b, p in enumerate(sizes(q)):
                            pe.wait_ge(x_in[1 - w][b], 8 * q + (16 if w else 8))
                            reuse(pe, e["flat"], 2 * q)
                            for n in range(G // 2):
                                i = t.transpose(pX[b][:, n * P:n * P + p], X[1 - w][b][0:p, n * P:n * P + P],
                                                k.ident[0:p, 0:p])
                            i.then_inc(e["turned"], 1)
                    if q is not None:
                        for b, p in enumerate(sizes(q)):
                            pe.wait_ge(e["flat"], last_of(q, b))
                            reuse(pe, e["relu"], 2 * q)
                            t.matmul(pU[b][0:p, :], k.ones[0:1, 0:p], k.shift[:, :, :].rearrange("a n c -> a (n c)"),
                                     start=True, stop=False, skip_group_check=True)
                            for n in range(G // 2):
                                i = t.matmul(pU[b][0:p, n * P:n * P + P], XF[b][:, n * P:n * P + p], k.wbn_r[:, :],
                                             start=False, stop=n == G // 2 - 1, skip_group_check=True)
                            i.then_inc(e["product"], 1)
                    if r is not None:
                        for b, p in enumerate(sizes(r)):
                            pe.wait_ge(e["norm"], last_of(r, b))
                            reuse(pe, e["zflat"], 2 * r)
                            for n in range(G // 2):
                                i = t.transpose(pH[b][0][:, n * P:n * P + p], X3[w][b][0:p, n * P:n * P + P],
                                                k.ident[0:p, 0:p])
                            i.then_inc(e["turned3"], 1)
                        for b in range(2):
                            pe.wait_ge(e["flat3"], last_of(r, b))
                            reuse(pe, e["less"], 2 * r)
                            for h in range(2):
                                rows = slice(h * C, h * C + C)
                                t.matmul(pH[b][h][:, :], k.w1[rows, :], UF[b][rows, :], start=True, stop=True)\
                                    .then_inc(e[f"first{h}"], 1)
                        for b in range(2):
                            for h in range(2):
                                pe.wait_ge(e[f"hid{h}"], last_of(r, b))
                                t.matmul(pH[b][h][:, :], k.w2[:, :], H1[b][:, h, :], start=True, stop=True)\
                                    .then_inc(e[f"second{h}"], 1)
                        for b in range(2):
                            for h in range(2):
                                pe.wait_ge(e[f"deep{h}"], last_of(r, b))
                                i = t.matmul(pH[b][0][h * C:h * C + C, :], k.w3[:, :], H2[b][:, h, :],
                                             start=True, stop=True)
                            i.then_inc(e["third"], 1)
                        for b, p in enumerate(sizes(r)):
                            pe.wait_ge(e["zflat"], last_of(r, b))
                            for n in range(G // 2):
                                i = t.transpose(pH[b][1][0:p, n * P:n * P + P], ZF[b][:, n * P:n * P + p],
                                                k.ident[:, :])
                            i.then_inc(e["back"], 1)

                schedule(pe, step)

            @block.scalar
            def _(act):
                s = nc.scalar
                s.preload_act_table_set(LN_EXP)

                def hidden(r, h):
                    for b in range(2):
                        act.wait_ge(e[f"first{h}"], last_of(r, b))
                        reuse(act, e[f"second{h}"], 2 * r)
                        s.activation(H1[b][:, h, :], pH[b][h][:, :], ACT.Relu, bias=k.col[:, 4:5])\
                            .then_inc(e[f"hid{h}"], 1)

                def deeper(r, h):
                    for b in range(2):
                        act.wait_ge(e[f"second{h}"], last_of(r, b))
                        reuse(act, e["third"], 2 * r)
                        s.activation(H2[b][:, h, :], pH[b][h][:, :], ACT.Relu, bias=k.col[:, 5:6])\
                            .then_inc(e[f"deep{h}"], 1)

                def step(q, r, s_, w):
                    first, second, third = (
                        [] if n is None else [(b, slice(0, p)) for b, p in enumerate(sizes(n))] for n in (q, r, s_))
                    for b, p in first:
                        act.wait_ge(e["turned"], last_of(q, b))
                        reuse(act, e["product"], 2 * q)
                        s.activation(XF[b][:, :], pX[b][:, :], ACT.Copy).then_inc(e["flat"], 1)
                    for b, p in third:
                        act.wait_ge(e["less"], last_of(s_, b))
                        s.activation(O[1 - w][b][p, :], O[1 - w][b][p, :], ACT.Exp).then_inc(e["exp"], 1)
                    for b, p in first:
                        act.wait_ge(e["product"], last_of(q, b))
                        reuse(act, e["norm"], 2 * q)
                        s.activation(U[b][p, :], pU[b][p, :], ACT.Relu).then_inc(e["relu"], 1)
                    for b, p in first:
                        act.wait_ge(e["relu"], last_of(q, b))
                        reuse(act, e["sumsq2"], 2 * q)
                        s.activation(Q[b][p, :], U[b][p, :], ACT.Square).then_inc(e["sq"], 1)
                    for b, p in second:
                        act.wait_ge(e["turned3"], last_of(r, b))
                        reuse(act, e["first1"], 2 * r)
                        s.activation(UF[b][:, :], pH[b][0][:, :], ACT.Copy).then_inc(e["flat3"], 1)
                    if r is not None:
                        hidden(r, 0)
                        hidden(r, 1)
                    for b, p in first:
                        act.wait_ge(e["clamped"], last_of(q, b))
                        s.activation(st[b][p, 1, :], st[b][p, 0, :], ACT.Ln, scale=2.0 ** 20).then_inc(e["ln"], 1)
                    for b, p in first:
                        act.wait_ge(e["ln"], last_of(q, b))
                        s.activation(st[b][p, 1, :], st[b][p, 1, :], ACT.Exp, scale=-0.5, bias=k.eps[p, 2:3])\
                            .then_inc(e["inv"], 1)
                    if r is not None:
                        deeper(r, 0)
                    for b, p in third:
                        act.wait_ge(e["mixed"], last_of(s_, b))
                        s.activation(R[b][p, :], O[1 - w][b][p, :], ACT.Square).then_inc(e["sq4"], 1)
                    if r is not None:
                        deeper(r, 1)
                    for b, p in first:
                        act.wait_ge(e["cen"], last_of(q, b))
                        s.activation(Q[b][p, :], U[b][p, :], ACT.Square).then_inc(e["sq2"], 1)
                    for b, p in third:
                        act.wait_ge(e["sumsq4"], last_of(s_, b))
                        s.activation(st[b][p, 7, :], st[b][p, 7, :], ACT.Ln, scale=1.0 / C, bias=k.eps[p, 0:1])\
                            .then_inc(e["ln4"], 1)
                    for b, p in third:
                        act.wait_ge(e["ln4"], last_of(s_, b))
                        s.activation(st[b][p, 8, :], st[b][p, 7, :], ACT.Exp, scale=-0.5).then_inc(e["dev4"], 1)
                    for b, p in second:
                        act.wait_ge(e["third"], last_of(r, b))
                        reuse(act, e["back"], 2 * r)
                        s.activation(ZF[b][:, :], pH[b][0][:, :], ACT.Identity, bias=k.col[:, 6:7])\
                            .then_inc(e["zflat"], 1)
                    for b, p in first:
                        act.wait_ge(e["sumsq2"], last_of(q, b))
                        s.activation(st[b][p, 3, :], st[b][p, 3, :], ACT.Ln, scale=(1.0 + EPS) / C,
                                     bias=k.eps[p, 1:2]).then_inc(e["ln2"], 1)
                    for b, p in first:
                        act.wait_ge(e["ln2"], last_of(q, b))
                        s.activation(st[b][p, 4, :], st[b][p, 3, :], ACT.Exp, scale=-0.5).then_inc(e["dev"], 1)

                schedule(act, step)

            @block.gpsimd
            def _(pool):
                gp = nc.gpsimd

                def step(q, r, s, w):
                    if s is not None:
                        for b, p in enumerate(sizes(s)):
                            pool.wait_ge(e["erec"], last_of(s, b))
                            O8 = groups(O[1 - w][b][0:p, :], G)
                            gp.tensor_tensor(O8, O8, over(st[b][0:p, 5, :], C), ALU.mult).then_inc(e["soft"], 1)
                    if q is not None:
                        for b, p in enumerate(sizes(q)):
                            pool.wait_ge(e["scaled"], last_of(q, b))
                            gp.tensor_tensor(U[b][0:p, :], U[b][0:p, :], X[1 - w][b][0:p, :], ALU.add)\
                                .then_inc(e["added"], 1)

                schedule(pool, step)

            @block.vector
            def _(dve):
                v = nc.vector

                def step(q, r, s, w):
                    first, third = (
                        [] if n is None else [(b, slice(0, p)) for b, p in enumerate(sizes(n))] for n in (q, s))
                    g8 = lambda t, b, p: groups(t[b][p, :], G)
                    O_ = O[1 - w]
                    for b, p in third:
                        dve.wait_ge(e["back"], last_of(s, b))
                        v.tensor_reduce(out=st[b][p, 5, :], in_=groups(pH[b][1][p, :], G), op=ALU.max, axis=AX)\
                            .then_inc(e["max"], 1)
                    for b, p in third:
                        dve.wait_ge(e["max"], last_of(s, b))
                        reuse(dve, o_out[1 - w][b], 8 * s - (0 if w else 8))
                        v.tensor_tensor(g8(O_, b, p), groups(pH[b][1][p, :], G), over(st[b][p, 5, :], C),
                                        ALU.subtract).then_inc(e["less"], 1)
                    for b, p in first:
                        dve.wait_ge(e["sq"], last_of(q, b))
                        v.tensor_reduce(out=st[b][p, 0, :], in_=g8(Q, b, p), op=ALU.add, axis=AX).then_inc(e["sumsq"], 1)
                    for b, p in first:
                        dve.wait_ge(e["sumsq"], last_of(q, b))
                        v.tensor_scalar(st[b][p, 0, :], st[b][p, 0, :], 1e-24, None, ALU.max)\
                            .then_inc(e["clamped"], 1)
                    for b, p in third:
                        dve.wait_ge(e["exp"], last_of(s, b))
                        v.tensor_reduce(out=st[b][p, 6, :], in_=g8(O_, b, p), op=ALU.add, axis=AX).then_inc(e["esum"], 1)
                    for b, p in third:
                        dve.wait_ge(e["esum"], last_of(s, b))
                        v.reciprocal(st[b][p, 5, :], st[b][p, 6, :]).then_inc(e["erec"], 1)
                    for b, p in first:
                        dve.wait_ge(e["inv"], last_of(q, b))
                        v.tensor_tensor(g8(U, b, p), g8(U, b, p), over(st[b][p, 1, :], C), ALU.mult)\
                            .then_inc(e["scaled"], 1)
                    for b, p in third:
                        dve.wait_ge(e["soft"], last_of(s, b))
                        v.scalar_tensor_tensor(O_[b][p, :], O_[b][p, :], -1.0 / C, X3[1 - w][b][p, :], ALU.add, ALU.add)\
                            .then_inc(e["mixed"], 1)
                    for b, p in first:
                        dve.wait_ge(e["added"], last_of(q, b))
                        v.tensor_reduce(out=st[b][p, 2, :], in_=g8(U, b, p), op=ALU.add, axis=AX).then_inc(e["sum"], 1)
                    for b, p in first:
                        dve.wait_ge(e["sum"], last_of(q, b))
                        v.scalar_tensor_tensor(g8(U, b, p), over(st[b][p, 2, :], C), -1.0 / C, g8(U, b, p),
                                               ALU.mult, ALU.add).then_inc(e["cen"], 1)
                    for b, p in third:
                        dve.wait_ge(e["sq4"], last_of(s, b))
                        v.tensor_reduce(out=st[b][p, 7, :], in_=g8(R, b, p), op=ALU.add, axis=AX)\
                            .then_inc(e["sumsq4"], 1)
                    for b, p in first:
                        dve.wait_ge(e["sq2"], last_of(q, b))
                        v.tensor_reduce(out=st[b][p, 3, :], in_=g8(Q, b, p), op=ALU.add, axis=AX)\
                            .then_inc(e["sumsq2"], 1)
                    for b, p in third:
                        dve.wait_ge(e["dev4"], last_of(s, b))
                        v.tensor_tensor(g8(O_, b, p), g8(O_, b, p), over(st[b][p, 8, :], C), ALU.mult)\
                            .then_inc(e["norm4"], 1)
                    for b, p in first:
                        dve.wait_ge(e["dev"], last_of(q, b))
                        v.tensor_tensor(g8(X3[1 - w], b, p), g8(U, b, p), over(st[b][p, 4, :], C), ALU.mult)\
                            .then_inc(e["norm"], 1)

                schedule(dve, step)


_RAW = ["x", "edge_attr_3"] + ["L0_gnn_" + n for n in "Wd1 bd1 g1 b1 Wd2 bd2 g2 b2 W1 W2 W3".split()] + \
    ["L1_gnn_" + n for n in "W_l W_r b gamma beta".split()] + ["L2_gnn_W", "L2_gnn_b"] + \
    ["L3_gnn_b1", "L3_gnn_b2", "L3_gnn_b3"]


def kernel(**inputs):
    import numpy as np
    import concourse.bacc as bacc
    from concourse.bass_utils import run_bass_kernel_spmd

    given = {n: np.asarray(v) for n, v in inputs.items()}
    arrays = {n: given[n] for n in _RAW if n != "edge_attr_3"}
    pad = EP - E
    arrays["srcp"] = np.concatenate([given["src"], np.zeros(pad, np.int32)])
    arrays["dstp"] = np.concatenate([np.full(1, -1, np.int32), given["dst"], np.full(pad, N, np.int32),
                                     np.full(1, N, np.int32)])
    arrays["attrT"] = np.pad(given["edge_attr_3"].T, ((0, 0), (0, pad)))
    for n in (1, 2, 3):
        arrays[f"W{n}T"] = given[f"L3_gnn_W{n}"].T
    nc = bacc.Bacc("TRN2", target_bir_lowering=False, num_devices=1)
    aps = {}
    for n, v in arrays.items():
        arrays[n] = v = np.ascontiguousarray(v)
        aps[n] = nc.dram_tensor("in_" + n, v.shape, mybir.dt.from_np(v.dtype), kind="ExternalInput").ap()
    out = nc.dram_tensor("out", (N, C), F32, kind="ExternalOutput").ap()
    build(nc, aps, out)
    r = run_bass_kernel_spmd(nc, [{"in_" + n: v for n, v in arrays.items()}], core_ids=[0])
    return r.results[0]["out"]
```
